# Optimizing a Trainium2 kernel written in Bass

```python
import numpy as np
import jax
import jax.numpy as jnp

def _softmax(x, axis=-1):
    return jax.nn.softmax(x, axis=axis)

def _gelu(x):
    return jax.nn.gelu(x, approximate=True)

def _silu(x):
    return jax.nn.silu(x)

def _sigmoid(x):
    return jax.nn.sigmoid(x)

def _layernorm(x, axis=-1, eps=1e-05):
    m = jnp.mean(x, axis=axis, keepdims=True)
    v = jnp.var(x, axis=axis, keepdims=True)
    return (x - m) / jnp.sqrt(v + eps)

def _scatter_add(tgt, idx, src, axis=0):
    return tgt.at[idx].add(src)

def _segment_sum(src, seg, n):
    return jax.ops.segment_sum(src, seg, n)
kernel_name = 'mk_adaln_attn_ffn_d1_seqx_r8_8c6ebe'

def setup_inputs(seed: int=0):
    np.random.seed(seed)
    _w = jnp.asarray

    def _rec_inputs():
        import jax
        import jax.numpy as jnp
        _rk = jax.random.key(seed)
        x = -0.0002928 + 1 * jax.random.normal(jax.random.fold_in(_rk, 1), (32, 128, 128), jnp.float32)
        _lenS = 128 - jax.random.randint(jax.random.fold_in(_rk, 7), (32,), 0, max(1, 128 // 4) + 1, jnp.int32)
        _lenS2 = 128 - jax.random.randint(jax.random.fold_in(_rk, 8), (32,), 0, max(1, 128 // 4) + 1, jnp.int32)
        fside_BxS_0 = 0.0061147 + 1.02565 * jax.random.normal(jax.random.fold_in(_rk, 12), (32, 128), jnp.float32)
        itok_BxSxS_0_4 = jax.random.randint(jax.random.fold_in(_rk, 13), (32, 128, 128), 0, 5, jnp.int32)
        fside_BxSxS_0 = -3.24666e-05 + 0.0312493 * jax.random.normal(jax.random.fold_in(_rk, 14), (32, 128, 128), jnp.float32)
        cond_2048 = -4.62462e-05 + 0.0441849 * jax.random.normal(jax.random.fold_in(_rk, 16), (32, 256), jnp.float32)
        _validS = jnp.arange(128)[None, :] < _lenS[:, None]
        _validS2 = jnp.arange(128)[None, :] < _lenS2[:, None]
        _causal = jnp.tril(jnp.ones((128, 128), dtype=bool))
        mask_BxS_ff1 = jnp.where(jnp.ones((32, 128), dtype=bool), 1.0, 0.0).astype(jnp.float32)
        mask_BxS_ff0 = jnp.where(jnp.ones((32, 128), dtype=bool), 0.0, -1000000000.0).astype(jnp.float32)
        return (x, fside_BxS_0, itok_BxSxS_0_4, fside_BxSxS_0, cond_2048, mask_BxS_ff1, mask_BxS_ff0)
    x, fside_BxS_0, itok_BxSxS_0_4, fside_BxSxS_0, cond_2048, mask_BxS_ff1, mask_BxS_ff0 = _rec_inputs()

    def _L0_cond_setup():
        import jax, jax.numpy as jnp
        import numpy as np
        B, N, D = (4, 128, 128)
        T_ITER = 4
        E_TYPES = 4
        ALPHA = 0.2

        def _lin_w(key, out_f, in_f):
            bound = float(np.sqrt(3.0 / ((in_f + out_f) / 2.0)))
            return jax.random.uniform(key, (out_f, in_f), minval=-bound, maxval=bound, dtype=jnp.float32)

        def _lin(x, w, b):
            return x @ w.T + b

        def _qdgat_forward(ents, ent_mask, q_encoding, adj, types, init_mem, w_qin, b_qin, w_qt, b_qt, w_pl, b_pl, w_pc, b_pc, w_q, b_q, w_k, b_k, w_v, b_v, w_pk, b_pk, w_pv, b_pv, wes, w_mu, b_mu, w_cb, b_cb):
            d = ents.shape[-1]
            x_loc = ents
            x_ctx = jnp.broadcast_to(init_mem, ents.shape)
            var_drop = ent_mask[:, :, None]
            adj_pos = adj > 0
            q_base = jax.nn.elu(_lin(q_encoding, w_qin, b_qin))
            n_types = wes.shape[0] + 1
            for t in range(T_ITER):
                cmd = _lin(q_base, w_qt[t], b_qt[t])
                xc = x_ctx * var_drop
                pl = _lin(x_loc, w_pl, b_pl)
                pc = _lin(xc, w_pc, b_pc)
                x_joint = jnp.concatenate([x_loc, xc, pl * pc], axis=-1)
                q = _lin(x_joint, w_q, b_q)
                k = _lin(x_joint, w_k, b_k) * _lin(cmd, w_pk, b_pk)[:, None, :]
                v = _lin(x_joint, w_v, b_v) * _lin(cmd, w_pv, b_pv)[:, None, :]
                edge_score = jnp.zeros(adj.shape, jnp.float32)
                for i in range(n_types):
                    if types >> i & 1 == 1:
                        w1, w2 = (wes[i - 1, :d], wes[i - 1, d:])
                        s = (q @ w1)[:, :, None] + (k @ w2)[:, None, :]
                        edge_score = edge_score + jnp.where(adj == i, s, 0.0)
                e = jnp.where(edge_score > 0, edge_score, ALPHA * edge_score)
                logits = jnp.where(adj_pos, e, jnp.float32(-9000000000000000.0))
                prob = jax.nn.softmax(logits, axis=-1)
                message = jnp.einsum('bij,bjd->bid', prob, v)
                x_ctx = _lin(jnp.concatenate([xc, message], axis=-1), w_mu, b_mu)
            return _lin(jnp.concatenate([x_loc, x_ctx], axis=-1), w_cb, b_cb)
        key = jax.random.key(seed)
        ks = jax.random.split(key, 32)
        inp = {}
        inp['ents'] = jax.random.normal(ks[0], (B, N, D), jnp.float32)
        inp['ent_mask'] = jnp.ones((B, N), jnp.float32)
        inp['q_encoding'] = jax.random.normal(ks[1], (B, D), jnp.float32)
        inp['adj'] = jax.random.randint(ks[2], (B, N, N), 0, E_TYPES + 1, dtype=jnp.int32)
        inp['types'] = 30
        inp['init_mem'] = jax.random.normal(ks[3], (1, D), jnp.float32)
        inp['w_qin'] = _lin_w(ks[4], D, D)
        inp['b_qin'] = jnp.zeros((D,), jnp.float32)
        inp['w_qt'] = jnp.stack([_lin_w(ks[5 + t], D, D) for t in range(T_ITER)])
        inp['b_qt'] = jnp.zeros((T_ITER, D), jnp.float32)
        inp['w_pl'] = _lin_w(ks[9], D, D)
        inp['b_pl'] = jnp.zeros((D,), jnp.float32)
        inp['w_pc'] = _lin_w(ks[10], D, D)
        inp['b_pc'] = jnp.zeros((D,), jnp.float32)
        inp['w_q'] = _lin_w(ks[11], D, 3 * D)
        inp['b_q'] = jnp.zeros((D,), jnp.float32)
        inp['w_k'] = _lin_w(ks[12], D, 3 * D)
        inp['b_k'] = jnp.zeros((D,), jnp.float32)
        inp['w_v'] = _lin_w(ks[13], D, 3 * D)
        inp['b_v'] = jnp.zeros((D,), jnp.float32)
        inp['w_pk'] = _lin_w(ks[14], D, D)
        inp['b_pk'] = jnp.zeros((D,), jnp.float32)
        inp['w_pv'] = _lin_w(ks[15], D, D)
        inp['b_pv'] = jnp.zeros((D,), jnp.float32)
        wb = 1.414 * float(np.sqrt(6.0 / (2 * D + 1)))
        inp['wes'] = jax.random.uniform(ks[16], (E_TYPES, 2 * D), minval=-wb, maxval=wb, dtype=jnp.float32)
        inp['w_mu'] = _lin_w(ks[17], D, 2 * D)
        inp['b_mu'] = jnp.zeros((D,), jnp.float32)
        inp['w_cb'] = _lin_w(ks[18], D, 2 * D)
        inp['b_cb'] = jnp.zeros((D,), jnp.float32)
        return inp
    _L0_cond_all = _L0_cond_setup()
    _L0_cond_in = {k: v for k, v in _L0_cond_all.items() if k in ('init_mem', 'w_qin', 'b_qin', 'w_pl', 'b_pl', 'w_pc', 'b_pc', 'w_q', 'b_q', 'w_k', 'b_k', 'w_v', 'b_v', 'w_pk', 'b_pk', 'w_pv', 'b_pv', 'w_mu', 'b_mu', 'w_cb', 'b_cb')}
    del _L0_cond_all

    def _L0_attn_setup():
        import jax, jax.numpy as jnp
        import numpy as np
        EMB = 128
        HEADS = 16
        EPS = 1e-05

        def layer_norm(x):
            mu = jnp.mean(x, axis=-1, keepdims=True)
            var = jnp.var(x, axis=-1, keepdims=True)
            return (x - mu) / jnp.sqrt(var + EPS)

        def pattention(x, K, V):
            scale = EMB ** (-0.5)
            a = jax.nn.softmax(scale * jnp.einsum('btc,nc->btn', x, K), axis=-1)
            return jnp.einsum('btn,nc->btc', a, V)

        def causal_sdpa(q, k, v):
            T = q.shape[2]
            d = q.shape[-1]
            scores = jnp.einsum('bhqd,bhkd->bhqk', q, k) / jnp.sqrt(jnp.asarray(d, q.dtype))
            mask = jnp.tril(jnp.ones((T, T), dtype=bool))
            scores = jnp.where(mask, scores, jnp.asarray(-jnp.inf, q.dtype))
            attn = jax.nn.softmax(scores, axis=-1)
            return jnp.einsum('bhqk,bhkd->bhqd', attn, v)
        key = jax.random.key(seed)
        ks = jax.random.split(key, 11)
        B, T, C = (2, 256, EMB)
        N = 256 // 2
        inp = {'x': jax.random.normal(ks[0], (B, T, C), dtype=jnp.float32)}
        names = ['qK', 'qV', 'kK', 'kV', 'vK', 'vV', 'pK', 'pV']
        for i, nm in enumerate(names):
            inp[nm] = jax.random.normal(ks[1 + i], (N, C), dtype=jnp.float32)
        inp['fK'] = jax.random.normal(ks[9], (4 * N, C), dtype=jnp.float32)
        inp['fV'] = jax.random.normal(ks[10], (4 * N, C), dtype=jnp.float32)
        return inp
    _L0_attn_all = _L0_attn_setup()
    _L0_attn_in = {k: v for k, v in _L0_attn_all.items() if k in ('qK', 'qV', 'kK', 'kV', 'vK', 'vV', 'pK', 'pV', 'fK', 'fV')}
    del _L0_attn_all

    def _L0_cond2_setup():
        import jax, jax.numpy as jnp
        import numpy as np
        B, S, D_MODEL, D_INNER, D_STATE = (4, 512, 128, 256, 16)
        key = jax.random.key(seed)
        ks = jax.random.split(key, 12)
        inp = {'x': jax.random.normal(ks[0], (B, S, D_MODEL), jnp.float32), 't_emb': jax.random.normal(ks[1], (B, D_INNER), jnp.float32), 'W_in': jax.random.normal(ks[2], (2 * D_INNER, D_MODEL), jnp.float32) * 0.02, 'W_conv': jax.random.normal(ks[3], (D_INNER, 1, 4), jnp.float32) * 0.1, 'b_conv': jnp.zeros((D_INNER,), jnp.float32), 'ln_g': jnp.ones((D_INNER,), jnp.float32), 'ln_b': jnp.zeros((D_INNER,), jnp.float32), 'W_xproj': jax.random.normal(ks[4], (3 * D_STATE, D_INNER), jnp.float32) * 0.02, 'W_dt': jax.random.normal(ks[5], (D_STATE, D_STATE), jnp.float32) * 0.01, 'b_dt': jax.random.uniform(ks[6], (D_STATE,), jnp.float32) * 0.1, 'A_log': jax.random.normal(ks[7], (D_STATE,), jnp.float32) * 0.1, 'D': jnp.ones((D_INNER,), jnp.float32) * 0.1, 'W_out': jax.random.normal(ks[8], (D_MODEL, D_INNER), jnp.float32) * 0.02}
        return inp
    _L0_cond2_all = _L0_cond2_setup()
    _L0_cond2_in = {k: v for k, v in _L0_cond2_all.items() if k in ('W_in', 'W_conv', 'b_conv', 'ln_g', 'ln_b', 'W_xproj', 'W_dt', 'b_dt', 'A_log', 'D', 'W_out')}
    del _L0_cond2_all

    def _L0_ffn_setup():
        import jax, jax.numpy as jnp
        import numpy as np
        D_MODEL = 128
        HIDDEN = 256
        E_ROUTED = 14
        E_SHARED = 2
        TOP_K = 2
        EPS = 1e-09
        RMS_EPS = 1.1920929e-07

        def _ffn(xn, rw, W1, W2):
            ms = jnp.mean(xn * xn, axis=-1, keepdims=True)
            h = xn * jax.lax.rsqrt(ms + RMS_EPS) * rw
            return jax.nn.silu(h @ W1) @ W2
        key = jax.random.key(seed)
        ks = jax.random.split(key, 9)
        B, T = (2, 128)
        x = jax.random.normal(ks[0], (B, T, D_MODEL), dtype=jnp.float32)
        router_w = jax.random.normal(ks[1], (D_MODEL, E_ROUTED), dtype=jnp.float32) * 0.006
        rms_w = jnp.ones((E_ROUTED, D_MODEL), dtype=jnp.float32)
        w1 = jax.random.normal(ks[2], (E_ROUTED, D_MODEL, HIDDEN), dtype=jnp.float32) * 0.02
        w2 = jax.random.normal(ks[3], (E_ROUTED, HIDDEN, D_MODEL), dtype=jnp.float32) * 0.02
        rms_w_s = jnp.ones((E_SHARED, D_MODEL), dtype=jnp.float32)
        w1_s = jax.random.normal(ks[4], (E_SHARED, D_MODEL, HIDDEN), dtype=jnp.float32) * 0.02
        w2_s = jax.random.normal(ks[5], (E_SHARED, HIDDEN, D_MODEL), dtype=jnp.float32) * 0.02
        return {'x': x, 'router_w': router_w, 'rms_w': rms_w, 'w1': w1, 'w2': w2, 'rms_w_s': rms_w_s, 'w1_s': w1_s, 'w2_s': w2_s}
    _L0_ffn_all = _L0_ffn_setup()
    _L0_ffn_in = {k: v for k, v in _L0_ffn_all.items() if k in ('router_w', 'rms_w', 'w1', 'w2', 'rms_w_s', 'w1_s', 'w2_s')}
    del _L0_ffn_all
    return {'x': x, 'fside_BxS_0': fside_BxS_0, 'itok_BxSxS_0_4': itok_BxSxS_0_4, 'fside_BxSxS_0': fside_BxSxS_0, 'cond_2048': cond_2048, 'mask_BxS_ff1': mask_BxS_ff1, 'mask_BxS_ff0': mask_BxS_ff0, 'L0_cond_init_mem': _L0_cond_in['init_mem'], 'L0_cond_w_qin': _L0_cond_in['w_qin'], 'L0_cond_b_qin': _L0_cond_in['b_qin'], 'L0_cond_w_pl': _L0_cond_in['w_pl'], 'L0_cond_b_pl': _L0_cond_in['b_pl'], 'L0_cond_w_pc': _L0_cond_in['w_pc'], 'L0_cond_b_pc': _L0_cond_in['b_pc'], 'L0_cond_w_q': _L0_cond_in['w_q'], 'L0_cond_b_q': _L0_cond_in['b_q'], 'L0_cond_w_k': _L0_cond_in['w_k'], 'L0_cond_b_k': _L0_cond_in['b_k'], 'L0_cond_w_v': _L0_cond_in['w_v'], 'L0_cond_b_v': _L0_cond_in['b_v'], 'L0_cond_w_pk': _L0_cond_in['w_pk'], 'L0_cond_b_pk': _L0_cond_in['b_pk'], 'L0_cond_w_pv': _L0_cond_in['w_pv'], 'L0_cond_b_pv': _L0_cond_in['b_pv'], 'L0_cond_w_mu': _L0_cond_in['w_mu'], 'L0_cond_b_mu': _L0_cond_in['b_mu'], 'L0_cond_w_cb': _L0_cond_in['w_cb'], 'L0_cond_b_cb': _L0_cond_in['b_cb'], 'L0_attn_qK': _L0_attn_in['qK'], 'L0_attn_qV': _L0_attn_in['qV'], 'L0_attn_kK': _L0_attn_in['kK'], 'L0_attn_kV': _L0_attn_in['kV'], 'L0_attn_vK': _L0_attn_in['vK'], 'L0_attn_vV': _L0_attn_in['vV'], 'L0_attn_pK': _L0_attn_in['pK'], 'L0_attn_pV': _L0_attn_in['pV'], 'L0_attn_fK': _L0_attn_in['fK'], 'L0_attn_fV': _L0_attn_in['fV'], 'L0_cond2_W_in': _L0_cond2_in['W_in'], 'L0_cond2_W_conv': _L0_cond2_in['W_conv'], 'L0_cond2_b_conv': _L0_cond2_in['b_conv'], 'L0_cond2_ln_g': _L0_cond2_in['ln_g'], 'L0_cond2_ln_b': _L0_cond2_in['ln_b'], 'L0_cond2_W_xproj': _L0_cond2_in['W_xproj'], 'L0_cond2_W_dt': _L0_cond2_in['W_dt'], 'L0_cond2_b_dt': _L0_cond2_in['b_dt'], 'L0_cond2_A_log': _L0_cond2_in['A_log'], 'L0_cond2_D': _L0_cond2_in['D'], 'L0_cond2_W_out': _L0_cond2_in['W_out'], 'L0_ffn_router_w': _L0_ffn_in['router_w'], 'L0_ffn_rms_w': _L0_ffn_in['rms_w'], 'L0_ffn_w1': _L0_ffn_in['w1'], 'L0_ffn_w2': _L0_ffn_in['w2'], 'L0_ffn_rms_w_s': _L0_ffn_in['rms_w_s'], 'L0_ffn_w1_s': _L0_ffn_in['w1_s'], 'L0_ffn_w2_s': _L0_ffn_in['w2_s']}

def reference(x, fside_BxS_0, itok_BxSxS_0_4, fside_BxSxS_0, cond_2048, mask_BxS_ff1, mask_BxS_ff0, L0_cond_init_mem, L0_cond_w_qin, L0_cond_b_qin, L0_cond_w_pl, L0_cond_b_pl, L0_cond_w_pc, L0_cond_b_pc, L0_cond_w_q, L0_cond_b_q, L0_cond_w_k, L0_cond_b_k, L0_cond_w_v, L0_cond_b_v, L0_cond_w_pk, L0_cond_b_pk, L0_cond_w_pv, L0_cond_b_pv, L0_cond_w_mu, L0_cond_b_mu, L0_cond_w_cb, L0_cond_b_cb, L0_attn_qK, L0_attn_qV, L0_attn_kK, L0_attn_kV, L0_attn_vK, L0_attn_vV, L0_attn_pK, L0_attn_pV, L0_attn_fK, L0_attn_fV, L0_cond2_W_in, L0_cond2_W_conv, L0_cond2_b_conv, L0_cond2_ln_g, L0_cond2_ln_b, L0_cond2_W_xproj, L0_cond2_W_dt, L0_cond2_b_dt, L0_cond2_A_log, L0_cond2_D, L0_cond2_W_out, L0_ffn_router_w, L0_ffn_rms_w, L0_ffn_w1, L0_ffn_w2, L0_ffn_rms_w_s, L0_ffn_w1_s, L0_ffn_w2_s):
    import jax
    import jax.numpy as jnp

    def _L0_cond_ref(ents, ent_mask, q_encoding, adj, types, init_mem, w_qin, b_qin, w_qt, b_qt, w_pl, b_pl, w_pc, b_pc, w_q, b_q, w_k, b_k, w_v, b_v, w_pk, b_pk, w_pv, b_pv, wes, w_mu, b_mu, w_cb, b_cb):
        import jax, jax.numpy as jnp
        import numpy as np
        B, N, D = (4, 128, 128)
        T_ITER = 4
        E_TYPES = 4
        ALPHA = 0.2

        def _lin_w(key, out_f, in_f):
            bound = float(np.sqrt(3.0 / ((in_f + out_f) / 2.0)))
            return jax.random.uniform(key, (out_f, in_f), minval=-bound, maxval=bound, dtype=jnp.float32)

        def _lin(x, w, b):
            return x @ w.T + b

        def _qdgat_forward(ents, ent_mask, q_encoding, adj, types, init_mem, w_qin, b_qin, w_qt, b_qt, w_pl, b_pl, w_pc, b_pc, w_q, b_q, w_k, b_k, w_v, b_v, w_pk, b_pk, w_pv, b_pv, wes, w_mu, b_mu, w_cb, b_cb):
            d = ents.shape[-1]
            x_loc = ents
            x_ctx = jnp.broadcast_to(init_mem, ents.shape)
            var_drop = ent_mask[:, :, None]
            adj_pos = adj > 0
            q_base = jax.nn.elu(_lin(q_encoding, w_qin, b_qin))
            n_types = wes.shape[0] + 1
            for t in range(T_ITER):
                cmd = _lin(q_base, w_qt[t], b_qt[t])
                xc = x_ctx * var_drop
                pl = _lin(x_loc, w_pl, b_pl)
                pc = _lin(xc, w_pc, b_pc)
                x_joint = jnp.concatenate([x_loc, xc, pl * pc], axis=-1)
                q = _lin(x_joint, w_q, b_q)
                k = _lin(x_joint, w_k, b_k) * _lin(cmd, w_pk, b_pk)[:, None, :]
                v = _lin(x_joint, w_v, b_v) * _lin(cmd, w_pv, b_pv)[:, None, :]
                edge_score = jnp.zeros(adj.shape, jnp.float32)
                for i in range(n_types):
                    if types >> i & 1 == 1:
                        w1, w2 = (wes[i - 1, :d], wes[i - 1, d:])
                        s = (q @ w1)[:, :, None] + (k @ w2)[:, None, :]
                        edge_score = edge_score + jnp.where(adj == i, s, 0.0)
                e = jnp.where(edge_score > 0, edge_score, ALPHA * edge_score)
                logits = jnp.where(adj_pos, e, jnp.float32(-9000000000000000.0))
                prob = jax.nn.softmax(logits, axis=-1)
                message = jnp.einsum('bij,bjd->bid', prob, v)
                x_ctx = _lin(jnp.concatenate([xc, message], axis=-1), w_mu, b_mu)
            return _lin(jnp.concatenate([x_loc, x_ctx], axis=-1), w_cb, b_cb)
        return _qdgat_forward(ents, ent_mask, q_encoding, adj, types, init_mem, w_qin, b_qin, w_qt, b_qt, w_pl, b_pl, w_pc, b_pc, w_q, b_q, w_k, b_k, w_v, b_v, w_pk, b_pk, w_pv, b_pv, wes, w_mu, b_mu, w_cb, b_cb)

    def _L0_attn_ref(x, qK, qV, kK, kV, vK, vV, pK, pV, fK, fV):
        import jax, jax.numpy as jnp
        import numpy as np
        EMB = 128
        HEADS = 16
        EPS = 1e-05

        def layer_norm(x):
            mu = jnp.mean(x, axis=-1, keepdims=True)
            var = jnp.var(x, axis=-1, keepdims=True)
            return (x - mu) / jnp.sqrt(var + EPS)

        def pattention(x, K, V):
            scale = EMB ** (-0.5)
            a = jax.nn.softmax(scale * jnp.einsum('btc,nc->btn', x, K), axis=-1)
            return jnp.einsum('btn,nc->btc', a, V)

        def causal_sdpa(q, k, v):
            T = q.shape[2]
            d = q.shape[-1]
            scores = jnp.einsum('bhqd,bhkd->bhqk', q, k) / jnp.sqrt(jnp.asarray(d, q.dtype))
            mask = jnp.tril(jnp.ones((T, T), dtype=bool))
            scores = jnp.where(mask, scores, jnp.asarray(-jnp.inf, q.dtype))
            attn = jax.nn.softmax(scores, axis=-1)
            return jnp.einsum('bhqk,bhkd->bhqd', attn, v)
        B, T, C = x.shape
        H = HEADS
        D = C // H
        x_in = x
        h = layer_norm(x)
        k = pattention(h, kK, kV)
        q = pattention(h, qK, qV)
        v = pattention(h, vK, vV)
        to_heads = lambda t: t.reshape(B, T, H, D).transpose(0, 2, 1, 3)
        o = causal_sdpa(to_heads(q), to_heads(k), to_heads(v))
        o = o.transpose(0, 2, 1, 3).reshape(B, T, C)
        o = pattention(o, pK, pV)
        x = o + x_in
        x_inter = x
        x = pattention(layer_norm(x), fK, fV)
        return x + x_inter

    def _L0_cond2_ref(x, t_emb, W_in, W_conv, b_conv, ln_g, ln_b, W_xproj, W_dt, b_dt, A_log, D, W_out):
        import jax, jax.numpy as jnp
        import numpy as np
        B, S, D_MODEL, D_INNER, D_STATE = (4, 512, 128, 256, 16)
        d_inner = W_conv.shape[0]
        d_state = A_log.shape[0]
        xr, gate = jnp.split(x @ W_in.T, 2, axis=-1)
        xr = xr + t_emb[:, None, :]
        xc = jax.lax.conv_general_dilated(xr.transpose(0, 2, 1), W_conv, (1,), [(3, 0)], feature_group_count=d_inner, dimension_numbers=('NCH', 'OIH', 'NCH')) + b_conv[None, :, None]
        xc = jax.nn.silu(xc).transpose(0, 2, 1)
        mu = xc.mean(-1, keepdims=True)
        var = xc.var(-1, keepdims=True)
        xn = (xc - mu) / jnp.sqrt(var + 1e-05) * ln_g + ln_b
        Bm, Cm, dt = jnp.split(xn @ W_xproj.T, 3, axis=-1)
        dt = jnp.tanh(dt @ W_dt.T + b_dt) * 0.01
        A = -jnp.tanh(A_log)
        Ad = 1.0 + dt * A
        Bd = Bm * jnp.minimum(jnp.linalg.norm(xn, axis=-1, keepdims=True), 1.0)
        h0 = jnp.zeros((xn.shape[0], d_state, d_inner), xn.dtype)

        def step(h, inputs):
            ad, bd, xt, ct = inputs
            h = jnp.clip(h * ad[:, :, None] + bd[:, :, None] * xt[:, None, :], -10.0, 10.0)
            yt = jnp.einsum('bd,bdh->bh', ct, h)
            return (h, yt)
        _, ys = jax.lax.scan(step, h0, (Ad.transpose(1, 0, 2), Bd.transpose(1, 0, 2), xn.transpose(1, 0, 2), Cm.transpose(1, 0, 2)))
        y = ys.transpose(1, 0, 2) + D * xn
        return y * jax.nn.silu(gate) @ W_out.T

    def _L0_ffn_ref(x, router_w, rms_w, w1, w2, rms_w_s, w1_s, w2_s):
        import jax, jax.numpy as jnp
        import numpy as np
        D_MODEL = 128
        HIDDEN = 256
        E_ROUTED = 14
        E_SHARED = 2
        TOP_K = 2
        EPS = 1e-09
        RMS_EPS = 1.1920929e-07

        def _ffn(xn, rw, W1, W2):
            ms = jnp.mean(xn * xn, axis=-1, keepdims=True)
            h = xn * jax.lax.rsqrt(ms + RMS_EPS) * rw
            return jax.nn.silu(h @ W1) @ W2
        B, T, D = x.shape
        N = B * T
        xf = x.reshape(N, D)
        gates = jax.nn.softmax(xf @ router_w, axis=-1)
        top_v, top_i = jax.lax.top_k(gates, TOP_K)
        masked = jnp.zeros_like(gates).at[jnp.arange(N)[:, None], top_i].set(top_v)
        masked = masked / (masked.sum(axis=-1, keepdims=True) + EPS)
        routed = jax.vmap(lambda rw_, W1_, W2_: _ffn(xf, rw_, W1_, W2_))(rms_w, w1, w2)
        routed_out = jnp.einsum('end,ne->nd', routed, masked)
        shared = jax.vmap(lambda rw_, W1_, W2_: _ffn(xf, rw_, W1_, W2_))(rms_w_s, w1_s, w2_s).sum(0)
        return (routed_out + shared).reshape(B, T, D)
    x = x + _L0_attn_ref(_L0_cond_ref(x, mask_BxS_ff1, fside_BxS_0, itok_BxSxS_0_4, 30, L0_cond_init_mem, L0_cond_w_qin, L0_cond_b_qin, fside_BxSxS_0, mask_BxS_ff0, L0_cond_w_pl, L0_cond_b_pl, L0_cond_w_pc, L0_cond_b_pc, L0_cond_w_q, L0_cond_b_q, L0_cond_w_k, L0_cond_b_k, L0_cond_w_v, L0_cond_b_v, L0_cond_w_pk, L0_cond_b_pk, L0_cond_w_pv, L0_cond_b_pv, cond_2048, L0_cond_w_mu, L0_cond_b_mu, L0_cond_w_cb, L0_cond_b_cb), L0_attn_qK, L0_attn_qV, L0_attn_kK, L0_attn_kV, L0_attn_vK, L0_attn_vV, L0_attn_pK, L0_attn_pV, L0_attn_fK, L0_attn_fV)
    x = x + _L0_ffn_ref(_L0_cond2_ref(x, cond_2048, L0_cond2_W_in, L0_cond2_W_conv, L0_cond2_b_conv, L0_cond2_ln_g, L0_cond2_ln_b, L0_cond2_W_xproj, L0_cond2_W_dt, L0_cond2_b_dt, L0_cond2_A_log, L0_cond2_D, L0_cond2_W_out), L0_ffn_router_w, L0_ffn_rms_w, L0_ffn_w1, L0_ffn_w2, L0_ffn_rms_w_s, L0_ffn_w1_s, L0_ffn_w2_s)
    return x

_drawn_inputs = setup_inputs


def setup_inputs(seed=0):
    import zlib

    import numpy as np

    out = dict(_drawn_inputs(seed))
    spreads = {'L0_cond_b_qin': (0.0, 0.573),
     'L0_cond_b_pl': (0.0, 0.651),
     'L0_cond_b_pc': (0.0, 0.8),
     'L0_cond_b_q': (0.0, 0.8),
     'L0_cond_b_k': (0.0, 0.8),
     'L0_cond_b_v': (0.0, 0.342),
     'L0_cond_b_pk': (0.0, 0.8),
     'L0_cond_b_pv': (0.0, 0.1),
     'L0_cond_b_mu': (0.0, 0.1),
     'L0_cond_b_cb': (0.0, 0.8),
     'L0_cond2_b_conv': (0.0, 0.8),
     'L0_cond2_ln_g': (1.0, 0.6),
     'L0_cond2_ln_b': (0.0, 2.0),
     'L0_cond2_D': (0.10000000149011612, 0.6),
     'L0_ffn_rms_w': (1.0, 0.6),
     'L0_ffn_rms_w_s': (1.0, 0.6)}
    factors = {'cond_2048': 2.858,
     'L0_cond_w_pl': 4.348,
     'L0_cond_w_pc': 3.241,
     'L0_cond_w_q': 8.0,
     'L0_cond_w_k': 8.0,
     'L0_cond_w_pk': 8.0,
     'L0_attn_qK': 59.144,
     'L0_attn_qV': 58.991,
     'L0_attn_kK': 58.744,
     'L0_attn_kV': 58.913,
     'L0_attn_vK': 58.367,
     'L0_attn_vV': 58.581,
     'L0_attn_pK': 58.494,
     'L0_cond2_W_dt': 64.0,
     'L0_cond2_b_dt': 64.0,
     'L0_cond2_A_log': 64.0,
     'L0_ffn_router_w': 24.032,
     'L0_ffn_w1': 22.616,
     'L0_ffn_w2': 22.472,
     'L0_attn_pV': 7.193,
     'L0_attn_fK': 8.0,
     'L0_attn_fV': 8.0,
     'L0_cond2_W_in': 8.0,
     'L0_cond2_W_conv': 8.0,
     'L0_cond2_W_xproj': 8.0,
     'L0_cond2_W_out': 8.0,
     'L0_ffn_w1_s': 8.0,
     'L0_ffn_w2_s': 8.0}
    for name, (base, spread) in spreads.items():
        noise = np.random.default_rng([zlib.crc32(name.encode()), seed]).standard_normal(out[name].shape)
        drawn = base * np.exp(spread * noise) if base else spread * noise
        out[name] = jnp.asarray(drawn.astype(out[name].dtype))
    for name, factor in factors.items():
        out[name] = (out[name] * factor).astype(out[name].dtype)
    return out
```

```python
import math

B, S, D = 32, 128, 128
T_ITER, TYPES = 4, 4
ALPHA = 0.2
NO_EDGE = -9000000000000000.0
SERIES = 10
LN2_HIGH = 0.693359375
LN2_LOW = math.log(2.0) - LN2_HIGH
EXP_LOW = -60.0
LN_EPS = 1e-5
HEADS = 16
HD = D // HEADS
NF = 512
P_SCALE = float(D) ** -0.5
CAUSAL = -1e30
DI = 256
NH = DI // 128
N_STATE = 16
N_TAPS = 4
CLIP = 10.0
E_ROUTED, E_SHARED, HIDDEN = 14, 2, 256
NE = E_ROUTED + E_SHARED
RMS_EPS = 1.1920929e-07
GATE_EPS = 1e-9
GB = 4
GT = GB * S
NG = B // GB


class Signals:

    def __init__(self, nc, ctx, phase):
        self.nc, self.ctx, self.phase, self.taken = nc, ctx, phase, []

    def take(self, name, n=None):
        got = [self.ctx.enter_context(self.nc.semaphore(f"{self.phase}_{name}{i}")) for i in range(n or 1)]
        self.taken += got
        return got if n else got[0]

    def take_all(self, names, n=None):
        return [self.take(name, n) for name in names.split()]

    def clear(self):
        nums, runs = sorted(s.num for s in self.taken), []
        for k in nums:
            if runs and runs[-1][1] == k:
                runs[-1][1] = k + 1
            else:
                runs.append([k, k + 1])
        with self.nc.Block() as block:
            @block.sync
            def _(sp):
                for low, high in runs:
                    sp.sem_clear(range(low, high))


def edge_phase(nc, a, K):
    import concourse.bass as bass
    from concourse import mybir
    from contextlib import ExitStack
    f32, i32 = mybir.dt.float32, mybir.dt.int32
    ALU, ACT, AX = mybir.AluOpType, mybir.ActivationFunctionType, mybir.AxisListType
    ctx = ExitStack()
    NS = 2
    with ctx:
        def sb(name, shape, dt=f32):
            return ctx.enter_context(nc.sbuf_tensor(name, shape, dt))

        signals = Signals(nc, ctx, "edge")
        sem = signals.take

        PS = K["PS"]
        ident, ones_row = K["ident"], K["ones_row"]
        xT, adj, mask = sb("xT", [D, B * S]), sb("adj", [S, B, S], i32), sb("mask", [D, B * S])
        w_plT, w_pcT, w_qinT = sb("w_plT", [D, D]), sb("w_pcT", [D, D]), sb("w_qinT", [D, D])
        w_pkT, w_pvT = sb("w_pkT", [D, D]), sb("w_pvT", [D, D])
        w_q, w_k, w_vT = sb("w_q", [D, 3 * D]), sb("w_k", [D, 3 * D]), sb("w_vT", [D, 3, D])
        w_muT, w_cbT = sb("w_muT", [D, 2, D]), sb("w_cbT", [D, 2, D])
        w_qtT, qeT = sb("w_qtT", [D, T_ITER, D]), sb("qeT", [D, B])
        b_qtT, wesT = sb("b_qtT", [D, T_ITER]), sb("wesT", [D, 2, B])
        bias = sb("bias", [D, 9])
        rows = sb("rows", [1, 2, D])
        b_qin, b_pl, b_pc, b_q, b_k, b_pk, b_pv, b_mu, init = (bias[:, n:n + 1] for n in range(9))
        b_v, b_cb = rows[0:1, 0, :], rows[0:1, 1, :]
        q_lin, q_neg, q_exp, q_pos, q_base, q_round, q_rest = (
            sb(n, [D, B]) for n in ("q_lin", "q_neg", "q_exp", "q_pos", "q_base", "q_round", "q_rest"))
        q_int = sb("q_int", [D, B], i32)
        cmd, pk, pv = (sb(n, [D, T_ITER, B]) for n in ("cmd", "pk", "pv"))
        w2pk = sb("w2pk", [D, T_ITER * B, TYPES])
        edge_w = sb("edge_w", [D, 3, T_ITER * B, 2 * TYPES])
        edge_b = sb("edge_b", [1, T_ITER * B, 2 * TYPES])
        xg, plT, mT, xcT, xctxT, msgT = ([sb(f"{n}{s}", [D, GT]) for s in range(NS)]
                                         for n in ("xg", "plT", "mT", "xcT", "xctxT", "msgT"))
        is_type = [sb(f"is_type{s}", [S, GB, TYPES, S]) for s in range(NS)]
        scored = [sb(f"scored{s}", [S, GB, TYPES, S]) for s in range(NS)]
        no_edge = [sb(f"no_edge{s}", [S, GB, S]) for s in range(NS)]
        v_tok = [sb(f"v_tok{s}", [S, GB, D]) for s in range(NS)]
        ac = [sb(f"ac{s}", [S, GB, 2 * TYPES]) for s in range(NS)]
        half = [sb(f"half{s}", [S, GB, 2, S]) for s in range(NS)]
        edge = [sb(f"edge{s}", [S, GB, S]) for s in range(NS)]
        logit = [sb(f"logit{s}", [S, GB, S]) for s in range(NS)]
        prob = [sb(f"prob{s}", [S, GB, S]) for s in range(NS)]
        probT = [sb(f"probT{s}", [S, GB, S]) for s in range(NS)]
        neg_max, row_sum, inv_sum = ([sb(f"{n}{s}", [S, GB]) for s in range(NS)]
                                     for n in ("neg_max", "row_sum", "inv_sum"))
        cond_tok = K["cond_tok"]

        loads = [(w_qinT[:, :], a["w_qinT"]), (qeT[:, :], a["qeT"]), (bias[:, :], a["bias"]),
                 (w_qtT[:, :, :], a["w_qtT"].rearrange("t i o -> i t o")), (b_qtT[:, :], a["b_qtT"]),
                 (w_pkT[:, :], a["w_pkT"]), (w_pvT[:, :], a["w_pvT"]),
                 (wesT[:, :, :], a["condT"].rearrange("(h p) b -> p h b", p=D)),
                 (w_q[:, :], a["w_q"]), (w_k[:, :], a["w_k"]),
                 (rows[0:1, :, :], a["rows"].rearrange("(o r) d -> o r d", o=1))]
        loads2 = [(xT[:, :], a["xT"]), (adj[:, :, :], a["adj"].rearrange("b i j -> i b j")),
                  (mask[:, :], a["mask"].rearrange("(o b) s -> o (b s)", o=1).partition_broadcast(D)),
                  (w_plT[:, :], a["w_plT"]), (w_pcT[:, :], a["w_pcT"]),
                  (w_vT[:, :, :], a["w_vT"].rearrange("(c p) o -> p c o", p=D)),
                  (w_muT[:, :, :], a["w_muT"].rearrange("(c p) o -> p c o", p=D)),
                  (w_cbT[:, :, :], a["w_cbT"].rearrange("(c p) o -> p c o", p=D))]

        small_in, big_in = sem("small_in"), sem("big_in")
        q_lin_raw, q_lin_ok, q_step, q_ok = (sem(n) for n in ("q_lin_raw", "q_lin_ok", "q_step", "q_ok"))
        cmd_raw, cmd_ok, pkv_raw, pkv_ok, w2pk_ok, tab_raw, tab_ok = (
            sem(n) for n in ("cmd_raw", "cmd_ok", "pkv_raw", "pkv_ok", "w2pk_ok", "tab_raw", "tab_ok"))

        xc_ok = sem("xc_ok", NS)
        XC = T_ITER + 1

        with nc.Block() as block:
            @block.sync
            def _(sp):
                for dst, src in loads:
                    sp.dma_start(dst, src).then_inc(small_in, 16)
                for dst, src in loads2:
                    sp.dma_start(dst, src).then_inc(big_in, 16)
                sp.wait_ge(small_in, 16 * len(loads))
                sp.wait_ge(big_in, 16 * len(loads2))

            @block.tensor
            def _(pe):
                pe.wait_ge(small_in, 16 * len(loads))
                pe.matmul(PS[:, 0, 0:B], w_qinT[:, :], qeT[:, :], start=True, stop=True).then_inc(q_lin_raw, 1)
                pe.wait_ge(q_ok, 1)
                for t in range(T_ITER):
                    mm = pe.matmul(PS[:, 1, t * B:(t + 1) * B], w_qtT[:, t, :], q_base[:, :], start=True, stop=True)
                mm.then_inc(cmd_raw, 1)
                pe.wait_ge(cmd_ok, 1)
                pe.matmul(PS[:, 2, 0:T_ITER * B], w_pkT[:, :], cmd[:, :, :], start=True, stop=True)
                pe.matmul(PS[:, 3, 0:T_ITER * B], w_pvT[:, :], cmd[:, :, :], start=True, stop=True).then_inc(pkv_raw, 1)
                pe.wait_ge(w2pk_ok, 1)
                for c in range(3):
                    pe.matmul(PS[:, 4 + c, :], w_k[:, c * D:(c + 1) * D], w2pk[:, :, :], start=True, stop=True)
                    pe.matmul(PS[:, 0, c * TYPES:(c + 1) * TYPES], w_q[:, c * D:(c + 1) * D], wesT[:, 0, 0:TYPES],
                              start=True, stop=True)
                pe.matmul(PS[0:1, 7, :], b_k, w2pk[:, :, :], start=True, stop=True)
                pe.matmul(PS[0:1, 1, 0:TYPES], b_q, wesT[:, 0, 0:TYPES], start=True, stop=True).then_inc(tab_raw, 1)

            @block.vector
            def _(dve):
                dve.wait_ge(small_in, 16 * len(loads))
                dve.wait_ge(q_lin_raw, 1)
                dve.tensor_scalar(q_lin[:, :], PS[:, 0, 0:B], b_qin, None, ALU.add).then_inc(q_lin_ok, 1)
                dve.wait_ge(q_lin_ok, 1)
                done = 0

                def step(ins):
                    nonlocal done
                    done += 1
                    ins.then_inc(q_step, 1)
                    dve.wait_ge(q_step, done)

                step(dve.tensor_scalar(q_pos[:, :], q_lin[:, :], 0.0, None, ALU.max))
                step(dve.tensor_scalar(q_neg[:, :], q_lin[:, :], 0.0, EXP_LOW, ALU.min, ALU.max))
                step(dve.tensor_scalar(q_int[:, :], q_neg[:, :], 1.0 / math.log(2.0), None, ALU.mult))
                step(dve.tensor_copy(q_round[:, :], q_int[:, :]))
                step(dve.scalar_tensor_tensor(out=q_rest[:, :], in0=q_round[:, :], scalar=-LN2_HIGH, in1=q_neg[:, :],
                                              op0=ALU.mult, op1=ALU.add))
                step(dve.scalar_tensor_tensor(out=q_rest[:, :], in0=q_round[:, :], scalar=-LN2_LOW, in1=q_rest[:, :],
                                              op0=ALU.mult, op1=ALU.add))
                step(dve.tensor_scalar(q_exp[:, :], q_rest[:, :], 1.0 / math.factorial(SERIES), None, ALU.mult))
                for k in range(SERIES - 1, 0, -1):
                    step(dve.scalar_tensor_tensor(out=q_exp[:, :], in0=q_exp[:, :], scalar=1.0 / math.factorial(k),
                                                  in1=q_rest[:, :], op0=ALU.add, op1=ALU.mult))
                step(dve.tensor_scalar(q_int[:, :], q_round[:, :], 127.0, float(2 ** 23), ALU.add, ALU.mult))
                two_k = q_int[:, :].bitcast(f32)
                step(dve.tensor_tensor(q_exp[:, :], q_exp[:, :], two_k, ALU.mult))
                step(dve.scalar_tensor_tensor(out=q_pos[:, :], in0=two_k, scalar=-1.0, in1=q_pos[:, :], op0=ALU.add, op1=ALU.add))
                dve.tensor_tensor(q_base[:, :], q_exp[:, :], q_pos[:, :], ALU.add).then_inc(q_ok, 1)
                dve.wait_ge(cmd_raw, 1)
                dve.tensor_tensor(cmd[:, :, :], PS[:, 1, 0:T_ITER * B].rearrange("p (t b) -> p t b", t=T_ITER),
                                  b_qtT[:, :].unsqueeze(2).to_broadcast([D, T_ITER, B]), ALU.add).then_inc(cmd_ok, 1)
                dve.wait_ge(pkv_raw, 1)
                dve.tensor_scalar(pk[:, :, :], PS[:, 2, 0:T_ITER * B], b_pk, None, ALU.add).then_inc(pkv_ok, 1)
                dve.tensor_scalar(pv[:, :, :], PS[:, 3, 0:T_ITER * B], b_pv, None, ALU.add).then_inc(pkv_ok, 1)
                dve.wait_ge(pkv_ok, 2)
                dve.tensor_tensor(w2pk[:, :, :], pk[:, :, :].rearrange("p t b -> p (t b)").unsqueeze(2)
                                  .to_broadcast([D, T_ITER * B, TYPES]),
                                  wesT[:, 1:2, 0:TYPES].to_broadcast([D, T_ITER * B, TYPES]), ALU.mult).then_inc(w2pk_ok, 1)
                dve.wait_ge(tab_raw, 1)
                for c in range(3):
                    dve.tensor_copy(edge_w[:, c, :, TYPES:2 * TYPES],
                                    PS[:, 4 + c, :].rearrange("p (n m) -> p n m", m=TYPES)).then_inc(tab_ok, 1)
                    dve.tensor_copy(edge_w[:, c, :, 0:TYPES],
                                    PS[:, 0:1, c * TYPES:(c + 1) * TYPES].to_broadcast([D, T_ITER * B, TYPES])).then_inc(tab_ok, 1)
                dve.tensor_copy(edge_b[0:1, :, TYPES:2 * TYPES],
                                PS[0:1, 7, :].rearrange("p (n m) -> p n m", m=TYPES)).then_inc(tab_ok, 1)
                dve.tensor_copy(edge_b[0:1, :, 0:TYPES],
                                PS[0:1, 1:2, 0:TYPES].to_broadcast([1, T_ITER * B, TYPES])).then_inc(tab_ok, 1)
                dve.wait_ge(tab_ok, 8)
                for s in range(NS):
                    dve.sem_inc(xc_ok[s], 1)

        (x_ok, pl_raw, pl_ok, types_ok, combined_raw, group_done) = (
            sem(n, NS) for n in ("x_ok", "pl_raw", "pl_ok", "types_ok", "combined_raw", "group_done"))
        (pc_raw, m_ok, v_raw, v_ok, ac_ok, c_raw, masked_ok, half_ok, edge_ok, relu_ok, logit_ok, max_ok,
         exp_ok, inv_ok, prob_ok, probT_raw, probT_ok, msg_raw, msg_ok, mu_raw, xctx_ok) = (
            sem(n, NS) for n in ("pc_raw", "m_ok", "v_raw", "v_ok", "ac_ok", "c_raw", "masked_ok", "half_ok",
                                 "edge_ok", "relu_ok", "logit_ok", "max_ok", "exp_ok", "inv_ok", "prob_ok",
                                 "probT_raw", "probT_ok", "msg_raw", "msg_ok", "mu_raw", "xctx_ok"))
        PAIRS = NG // NS

        with nc.Block() as block:
            @block.tensor
            def _(pe):
                with pe.Fori(0, PAIRS) as i:
                    for s in range(NS):
                        pe.wait_ge(x_ok[s], i + 1)
                        pe.matmul(PS[:, 4 * s + 3, :], w_plT[:, :], xg[s][:, :], start=True, stop=True).then_inc(pl_raw[s], 1)
                    with pe.Fori(0, T_ITER) as t:
                        n = i * T_ITER + t + 1
                        for s in range(NS):
                            pe.wait_ge(xc_ok[s], i * XC + t + 2)
                            pe.matmul(PS[:, 4 * s, :], w_pcT[:, :], xcT[s][:, :], start=True, stop=True).then_inc(pc_raw[s], 1)
                        for s in range(NS):
                            pe.wait_ge(m_ok[s], n)
                            joint = [xg[s], xcT[s], mT[s]]
                            for b in range(GB):
                                at = t * B + i * (NS * GB) + (s * GB + b)
                                v_ps, ac_ps = PS[:, 4 * s + 1, b * D:(b + 1) * D], PS[:, 4 * s, b * 8:(b + 1) * 8]
                                pe.matmul(v_ps, ones_row[0:1, :], b_v, start=True, stop=False)
                                for c in range(3):
                                    pe.matmul(v_ps, joint[c][:, b * S:(b + 1) * S], w_vT[:, c, :], start=False, stop=(c == 2))
                                pe.matmul(ac_ps, ones_row[0:1, :], edge_b[0:1, bass.ds(at, 1), :], start=True, stop=False)
                                for c in range(3):
                                    mm = pe.matmul(ac_ps, joint[c][:, b * S:(b + 1) * S], edge_w[:, c, bass.ds(at, 1), :],
                                                   start=False, stop=(c == 2))
                            mm.then_inc(v_raw[s], 1)
                        for s in range(NS):
                            pe.wait_ge(ac_ok[s], n)
                            pe.wait_ge(v_ok[s], n)
                            for b in range(GB):
                                for m in range(TYPES):
                                    mm = pe.transpose(PS[:, 4 * s + b, m * S:(m + 1) * S],
                                                      ac[s][:, b, TYPES + m:TYPES + m + 1].to_broadcast([S, S]), ident[:, :])
                            mm.then_inc(c_raw[s], 1)
                        for s in range(NS):
                            pe.wait_ge(prob_ok[s], n)
                            for b in range(GB):
                                mm = pe.transpose(PS[:, 4 * s, b * S:(b + 1) * S], prob[s][:, b, :], ident[:, :])
                            mm.then_inc(probT_raw[s], 1)
                        for s in range(NS):
                            pe.wait_ge(probT_ok[s], n)
                            for b in range(GB):
                                mm = pe.matmul(PS[:, 4 * s + 1, b * S:(b + 1) * S], v_tok[s][:, b, :], probT[s][:, b, :],
                                               start=True, stop=True)
                            mm.then_inc(msg_raw[s], 1)
                        for s in range(NS):
                            pe.wait_ge(msg_ok[s], n)
                            pe.matmul(PS[:, 4 * s + 2, :], w_muT[:, 0, :], xcT[s][:, :], start=True, stop=False)
                            pe.matmul(PS[:, 4 * s + 2, :], w_muT[:, 1, :], msgT[s][:, :], start=False, stop=True).then_inc(mu_raw[s], 1)
                    for s in range(NS):
                        pe.wait_ge(xctx_ok[s], (i + 1) * T_ITER)
                        for b in range(GB):
                            out = PS[:, 4 * s + 3, b * D:(b + 1) * D]
                            pe.matmul(out, ones_row[0:1, :], b_cb, start=True, stop=False)
                            pe.matmul(out, xg[s][:, b * S:(b + 1) * S], w_cbT[:, 0, :], start=False, stop=False)
                            mm = pe.matmul(out, xctxT[s][:, b * S:(b + 1) * S], w_cbT[:, 1, :], start=False, stop=True)
                        mm.then_inc(combined_raw[s], 1)

            @block.scalar
            def _(act):
                with act.Fori(0, PAIRS) as i:
                    for s in range(NS):
                        act.activation(xg[s][:, :], xT[:, bass.ds((i * NS + s) * GT, GT)], ACT.Copy).then_inc(x_ok[s], 1)
                    with act.Fori(0, T_ITER) as t:
                        n = i * T_ITER + t + 1
                        for s in range(NS):
                            act.wait_ge(v_raw[s], n)
                            act.activation(v_tok[s][:, :, :], PS[:, 4 * s + 1, :], ACT.Copy).then_inc(v_ok[s], 1)
                        for s in range(NS):
                            act.wait_ge(max_ok[s], n)
                            for b in range(GB):
                                ins = act.activation(prob[s][:, b, :], logit[s][:, b, :], ACT.Exp,
                                                     bias=neg_max[s][:, b:b + 1], accum_out=row_sum[s][:, b:b + 1])
                            ins.then_inc(exp_ok[s], 1)
                        for s in range(NS):
                            act.wait_ge(probT_raw[s], n)
                            act.activation(probT[s][:, :, :], PS[:, 4 * s, :], ACT.Copy).then_inc(probT_ok[s], 1)
                        for s in range(NS):
                            act.wait_ge(mu_raw[s], n)
                            act.activation(xctxT[s][:, :], PS[:, 4 * s + 2, :], ACT.Identity, bias=b_mu).then_inc(xctx_ok[s], 1)
                    for s in range(NS):
                        act.wait_ge(combined_raw[s], i + 1)
                        act.activation(cond_tok[:, bass.ds((i * NS + s) * GB, GB), :],
                                       PS[:, 4 * s + 3, :].rearrange("p (b d) -> p b d", b=GB), ACT.Copy).then_inc(group_done[s], 1)
                for s in range(NS):
                    act.wait_ge(group_done[s], PAIRS)

            @block.vector
            def _(dve):
                with dve.Fori(0, PAIRS) as i:
                    for s in range(NS):
                        g = i * NS + s
                        for m in range(TYPES):
                            dve.tensor_scalar(is_type[s][:, :, m, :], adj[:, bass.ds(g * GB, GB), :], float(m + 1), None,
                                              ALU.is_equal).then_inc(types_ok[s], 1)
                        dve.tensor_scalar(no_edge[s][:, :, :], adj[:, bass.ds(g * GB, GB), :], 0.0, NO_EDGE,
                                          ALU.is_le, ALU.mult).then_inc(types_ok[s], 1)
                        dve.wait_ge(xc_ok[s], i * XC + 1)
                        dve.tensor_scalar(xcT[s][:, :], mask[:, bass.ds(g * GT, GT)], init, None, ALU.mult).then_inc(xc_ok[s], 1)
                    for s in range(NS):
                        dve.wait_ge(pl_raw[s], i + 1)
                        dve.tensor_scalar(plT[s][:, :], PS[:, 4 * s + 3, :], b_pl, None, ALU.add).then_inc(pl_ok[s], 1)
                    with dve.Fori(0, T_ITER) as t:
                        n = i * T_ITER + t + 1
                        for s in range(NS):
                            dve.wait_ge(pl_ok[s], i + 1)
                            dve.wait_ge(types_ok[s], (i + 1) * (TYPES + 1))
                            dve.wait_ge(pc_raw[s], n)
                            dve.scalar_tensor_tensor(out=mT[s][:, :], in0=PS[:, 4 * s, :], scalar=b_pc, in1=plT[s][:, :],
                                                     op0=ALU.add, op1=ALU.mult).then_inc(m_ok[s], 1)
                        for s in range(NS):
                            dve.wait_ge(v_raw[s], n)
                            dve.tensor_copy(ac[s][:, :, :], PS[:, 4 * s, 0:GB * 8].rearrange("p (b m) -> p b m", b=GB)).then_inc(ac_ok[s], 1)
                            dve.wait_ge(ac_ok[s], n)
                        for s in range(NS):
                            dve.wait_ge(c_raw[s], n)
                            for b in range(GB):
                                for m in range(TYPES):
                                    ins = dve.scalar_tensor_tensor(
                                        out=scored[s][:, b, m, :], in0=PS[:, 4 * s + b, m * S:(m + 1) * S],
                                        scalar=ac[s][:, b, m:m + 1], in1=is_type[s][:, b, m, :], op0=ALU.add, op1=ALU.mult)
                            ins.then_inc(masked_ok[s], 1)
                        for s in range(NS):
                            dve.wait_ge(masked_ok[s], n)
                            dve.tensor_tensor(half[s][:, :, :, :], scored[s][:, :, 0:2, :], scored[s][:, :, 2:4, :], ALU.add).then_inc(half_ok[s], 1)
                        for s in range(NS):
                            dve.wait_ge(half_ok[s], n)
                            dve.tensor_tensor(edge[s][:, :, :], half[s][:, :, 0, :], half[s][:, :, 1, :], ALU.add).then_inc(edge_ok[s], 1)
                        for s in range(NS):
                            dve.wait_ge(edge_ok[s], n)
                            dve.scalar_tensor_tensor(out=logit[s][:, :, :], in0=edge[s][:, :, :], scalar=ALPHA, in1=edge[s][:, :, :],
                                                     op0=ALU.mult, op1=ALU.max).then_inc(relu_ok[s], 1)
                        for s in range(NS):
                            dve.wait_ge(relu_ok[s], n)
                            dve.tensor_tensor(logit[s][:, :, :], logit[s][:, :, :], no_edge[s][:, :, :], ALU.add).then_inc(logit_ok[s], 1)
                        for s in range(NS):
                            dve.wait_ge(logit_ok[s], n)
                            dve.tensor_reduce(neg_max[s][:, :], logit[s][:, :, :], AX.X, ALU.max, negate=True).then_inc(max_ok[s], 1)
                        for s in range(NS):
                            dve.wait_ge(exp_ok[s], n)
                            dve.reciprocal(inv_sum[s][:, :], row_sum[s][:, :]).then_inc(inv_ok[s], 1)
                            dve.wait_ge(inv_ok[s], n)
                            dve.tensor_tensor(prob[s][:, :, :], prob[s][:, :, :],
                                              inv_sum[s][:, :].unsqueeze(2).to_broadcast([S, GB, S]), ALU.mult).then_inc(prob_ok[s], 1)
                        for s in range(NS):
                            dve.wait_ge(msg_raw[s], n)
                            dve.tensor_tensor(msgT[s][:, :].rearrange("p (b j) -> p b j", b=GB),
                                              PS[:, 4 * s + 1, :].rearrange("p (b j) -> p b j", b=GB),
                                              pv[:, bass.ds(t, 1), bass.ds(i * (NS * GB) + s * GB, GB)].rearrange("p o b -> p (o b)")
                                              .unsqueeze(2).to_broadcast([D, GB, S]), ALU.mult).then_inc(msg_ok[s], 1)
                        for s in range(NS):
                            dve.wait_ge(xctx_ok[s], n)
                            dve.tensor_tensor(xcT[s][:, :], xctxT[s][:, :], mask[:, bass.ds((i * NS + s) * GT, GT)], ALU.mult).then_inc(xc_ok[s], 1)
        signals.clear()



def attention_phase(nc, a, K):
    import concourse.bass as bass
    from concourse import mybir
    from contextlib import ExitStack
    f32 = mybir.dt.float32
    ALU, ACT, AX = mybir.AluOpType, mybir.ActivationFunctionType, mybir.AxisListType
    NS = 2
    PAIRS = B // NS
    with ExitStack() as ctx:
        def sb(name, shape, dt=f32):
            return ctx.enter_context(nc.sbuf_tensor(name, shape, dt))

        def per(name, shape):
            return [sb(f"{name}{s}", shape) for s in range(NS)]

        signals = Signals(nc, ctx, "attn")

        PS, ident, cond_tok, x3_tok, x3T = (K[n] for n in ("PS", "ident", "cond_tok", "x3_tok", "x3T"))
        x_tok = sb("x_tok", [S, B, D])
        qkv_KT, qkv_V = sb("qkv_KT", [D, 3 * D]), sb("qkv_V", [D, 3, D])
        p_KT, p_V = sb("p_KT", [D, D]), sb("p_V", [D, D])
        f_KT, f_V = sb("f_KT", [D, NF]), sb("f_V", [D, NF // 128, D])
        causal = sb("causal", [S, S])
        head16, head4 = sb("head16", [D, HEADS]), sb("head4", [D, 4])
        minus_half = sb("minus_half", [S, 1])
        stats, mv, veps, rstd = per("stats", [S, 6]), per("mv", [S, 2]), per("veps", [S, 1]), per("rstd", [S, 1])
        stats2, mv2, veps2, rstd2 = per("stats2", [S, 6]), per("mv2", [S, 2]), per("veps2", [S, 1]), per("rstd2", [S, 1])
        h, hT, h2, h2T = per("h", [S, D]), per("hT", [D, S]), per("h2", [S, D]), per("h2T", [D, S])
        qkv_nmax, qkv_bias, qkv_sum, qkv_inv = (per(n, [S, 3]) for n in ("qkv_nmax", "qkv_bias", "qkv_sum", "qkv_inv"))
        qkv_a, qkv_aT = per("qkv_a", [S, 3, D]), per("qkv_aT", [D, 3, S])
        qT, k_heads = per("qT", [D, S]), per("k_heads", [D, 4, S])
        v_aug = per("v_aug", [S, HEADS, HD + 1])
        score, head_max, expT = per("score", [S, HEADS, S]), per("head_max", [S, HEADS]), per("expT", [S, HEADS, S])
        head_inv, o, oT = per("head_inv", [S, HEADS]), per("o", [S, HEADS, HD]), per("oT", [D, S])
        p_nmax, p_bias, p_sum, p_inv = (per(n, [S, 1]) for n in ("p_nmax", "p_bias", "p_sum", "p_inv"))
        p_a, p_aT, x1 = per("p_a", [S, D]), per("p_aT", [D, S]), per("x1", [S, D])
        f_nmax, f_bias, f_sum, f_inv = (per(n, [S, 1]) for n in ("f_nmax", "f_bias", "f_sum", "f_inv"))
        f_a, f_aT, x2, x3 = per("f_a", [S, NF]), per("f_aT", [D, NF // 128, S]), per("x2", [S, D]), per("x3", [S, D])

        loads = [(x_tok[:, :, :], a["x"].rearrange("b s d -> s b d")), (qkv_KT[:, :], a["qkv_KT"]),
                 (qkv_V[:, :, :], a["qkv_V"].rearrange("j n c -> n j c")), (p_KT[:, :], a["p_KT"]),
                 (p_V[:, :], a["p_V"]), (f_KT[:, :], a["f_KT"]),
                 (f_V[:, :, :], a["f_V"].rearrange("(j n) c -> n j c", n=D))]
        loaded, filled, cut, made = signals.take_all("loaded filled cut made")

        with nc.Block() as block:
            @block.sync
            def _(sp):
                for dst, src in loads:
                    sp.dma_start(dst, src).then_inc(loaded, 16)
                sp.wait_ge(loaded, 16 * len(loads))

            @block.gpsimd
            def _(pool):
                pool.memset(causal[:, :], 0.0).then_inc(filled, 1)
                pool.memset(head16[:, :], float(HD) ** -0.5).then_inc(filled, 1)
                pool.memset(minus_half[:, :], -0.5).then_inc(filled, 1)
                for s in range(NS):
                    pool.memset(v_aug[s][:, :, :], 1.0).then_inc(filled, 1)
                pool.wait_ge(filled, 3 + NS)
                pool.affine_select(out=causal[:, :], in_=causal[:, :], compare_op=ALU.is_ge, fill=CAUSAL, base=0,
                                   pattern=[[-1, S]], channel_multiplier=1).then_inc(cut, 1)
                pool.affine_select(out=head16[:, :], in_=head16[:, :], compare_op=ALU.is_ge, fill=0.0, base=0,
                                   pattern=[[-HD, HEADS]], channel_multiplier=1).then_inc(cut, 1)
                pool.wait_ge(cut, 2)
                pool.affine_select(out=head16[:, :], in_=head16[:, :], compare_op=ALU.is_ge, fill=0.0, base=HD - 1,
                                   pattern=[[HD, HEADS]], channel_multiplier=-1).then_inc(cut, 1)

            @block.vector
            def _(dve):
                dve.wait_ge(cut, 3)
                dve.tensor_reduce(head4[:, :], head16[:, :].rearrange("p (r j) -> p j r", j=4), AX.X, ALU.add).then_inc(made, 1)
                dve.wait_ge(made, 1)

        (st_ok, st_seen, mv_ok, veps_ok, rstd_ok, h_ok, hT_raw, hT_ok, qkv_raw, qkv_nmax_ok, qkv_bias_ok, qkv_exp, qkv_inv_ok,
         qkv_a_ok, qkv_aT_raw, qkv_aT_ok, proj_raw, qv_ok, kh_ok, score_raw, score_ok, hmax_ok, shift_ok, hexp_ok,
         expT_raw, expT_ok, o_raw, hinv_ok, o_ok, oT_raw, oT_ok) = signals.take_all(
            "a_st_ok a_st_seen a_mv_ok a_veps_ok a_rstd_ok a_h_ok hT_raw hT_ok qkv_raw qkv_nmax_ok qkv_bias_ok qkv_exp qkv_inv_ok "
            "qkv_a_ok qkv_aT_raw qkv_aT_ok proj_raw qv_ok kh_ok score_raw score_ok hmax_ok shift_ok hexp_ok "
            "expT_raw expT_ok o_raw hinv_ok o_ok oT_raw oT_ok", NS)
        (p_raw, p_nmax_ok, p_bias_ok, p_exp, p_aT_raw, p_aT_ok, p_out_raw, p_inv_ok, x1_ok,
         f_st_ok, f_st_seen, f_mv_ok, f_veps_ok, f_rstd_ok, h2_ok, h2T_raw, h2T_ok, f_raw, f_nmax_ok, f_bias_ok, f_exp, f_aT_raw,
         f_aT_ok, f_out_raw, f_inv_ok, x2_ok, x3_ok, x3T_raw, stored) = signals.take_all(
            "p_raw p_nmax_ok p_bias_ok p_exp p_aT_raw p_aT_ok p_out_raw p_inv_ok x1_ok "
            "f_st_ok f_st_seen f_mv_ok f_veps_ok f_rstd_ok h2_ok h2T_raw h2T_ok f_raw f_nmax_ok f_bias_ok f_exp f_aT_raw "
            "f_aT_ok f_out_raw f_inv_ok x2_ok x3_ok x3T_raw x3_stored", NS)

        with nc.Block() as block:
            @block.gpsimd
            def _(pool):
                with pool.Fori(0, PAIRS) as i:
                    for s in range(NS):
                        pool.wait_ge(veps_ok[s], i + 1)
                        pool.tensor_tensor(rstd[s][:, :], veps[s][:, :], minus_half[:, :], ALU.pow).then_inc(rstd_ok[s], 1)
                    for s in range(NS):
                        pool.wait_ge(f_veps_ok[s], i + 1)
                        pool.tensor_tensor(rstd2[s][:, :], veps2[s][:, :], minus_half[:, :], ALU.pow).then_inc(f_rstd_ok[s], 1)

            @block.tensor
            def _(pe):
                with pe.Fori(0, PAIRS) as i:
                    n = i + 1
                    for s in range(NS):
                        pe.wait_ge(h_ok[s], n)
                        pe.transpose(PS[:, 4 * s, 0:S], h[s][:, :], ident[:, :]).then_inc(hT_raw[s], 1)
                    for s in range(NS):
                        pe.wait_ge(hT_ok[s], n)
                        pe.matmul(PS[:, 4 * s + 1, 0:3 * D], hT[s][:, :], qkv_KT[:, :], start=True, stop=True).then_inc(qkv_raw[s], 1)
                    for s in range(NS):
                        pe.wait_ge(qkv_a_ok[s], n)
                        for j in range(3):
                            mm = pe.transpose(PS[:, 4 * s + 2, j * S:(j + 1) * S], qkv_a[s][:, j, :], ident[:, :])
                        mm.then_inc(qkv_aT_raw[s], 1)
                    for s in range(NS):
                        pe.wait_ge(qkv_aT_ok[s], n)
                        pe.matmul(PS[:, 4 * s + 3, 0:S], qkv_V[:, 0, :], qkv_aT[s][:, 0, :], start=True, stop=True)
                        pe.matmul(PS[:, 4 * s, 0:S], qkv_V[:, 1, :], qkv_aT[s][:, 1, :], start=True, stop=True)
                        pe.matmul(PS[:, 4 * s + 3, 2 * S:3 * S], qkv_aT[s][:, 2, :], qkv_V[:, 2, :], start=True, stop=True)\
                          .then_inc(proj_raw[s], 1)
                    for s in range(NS):
                        pe.wait_ge(qv_ok[s], 2 * n)
                        pe.wait_ge(kh_ok[s], n)
                        for r in range(4):
                            mm = pe.matmul(PS[:, 4 * s + r, :], qT[s][32 * r:32 * r + 32, :], k_heads[s][32 * r:32 * r + 32, :, :],
                                           start=True, stop=True)
                        mm.then_inc(score_raw[s], 1)
                    for s in range(NS):
                        pe.wait_ge(hexp_ok[s], n)
                        for r in range(4):
                            for j in range(4):
                                mm = pe.transpose(PS[:, 4 * s + r, j * S:(j + 1) * S], score[s][:, 4 * r + j, :], ident[:, :])
                            mm.then_inc(expT_raw[s], 1)
                    for s in range(NS):
                        pe.wait_ge(expT_ok[s], 4 * n)
                        for j in range(HEADS):
                            mm = pe.matmul(PS[:, 4 * s, j * (HD + 1):(j + 1) * (HD + 1)], expT[s][:, j, :], v_aug[s][:, j, :],
                                           start=True, stop=True)
                        mm.then_inc(o_raw[s], 1)
                    for s in range(NS):
                        pe.wait_ge(o_ok[s], n)
                        pe.transpose(PS[:, 4 * s + 1, 0:S], o[s][:, :, :].rearrange("p h d -> p (h d)"), ident[:, :]).then_inc(oT_raw[s], 1)
                    for s in range(NS):
                        pe.wait_ge(oT_ok[s], n)
                        pe.matmul(PS[:, 4 * s + 1, 128:256], oT[s][:, :], p_KT[:, :], start=True, stop=True).then_inc(p_raw[s], 1)
                    for s in range(NS):
                        pe.wait_ge(p_exp[s], n)
                        pe.transpose(PS[:, 4 * s + 1, 256:384], p_a[s][:, :], ident[:, :]).then_inc(p_aT_raw[s], 1)
                    for s in range(NS):
                        pe.wait_ge(p_aT_ok[s], n)
                        pe.matmul(PS[:, 4 * s + 2, 0:D], p_aT[s][:, :], p_V[:, :], start=True, stop=True).then_inc(p_out_raw[s], 1)
                    for s in range(NS):
                        pe.wait_ge(h2_ok[s], n)
                        pe.transpose(PS[:, 4 * s + 2, 128:256], h2[s][:, :], ident[:, :]).then_inc(h2T_raw[s], 1)
                    for s in range(NS):
                        pe.wait_ge(h2T_ok[s], n)
                        pe.matmul(PS[:, 4 * s + 3, :], h2T[s][:, :], f_KT[:, :], start=True, stop=True).then_inc(f_raw[s], 1)
                    for s in range(NS):
                        pe.wait_ge(f_exp[s], n)
                        for j in range(NF // 128):
                            mm = pe.transpose(PS[:, 4 * s, j * S:(j + 1) * S], f_a[s][:, j * S:(j + 1) * S], ident[:, :])
                        mm.then_inc(f_aT_raw[s], 1)
                    for s in range(NS):
                        pe.wait_ge(f_aT_ok[s], n)
                        for j in range(NF // 128):
                            mm = pe.matmul(PS[:, 4 * s + 1, 384:512], f_aT[s][:, j, :], f_V[:, j, :], start=(j == 0), stop=(j == 3))
                        mm.then_inc(f_out_raw[s], 1)
                    for s in range(NS):
                        pe.wait_ge(x3_ok[s], n)
                        pe.transpose(PS[:, 4 * s + 2, 256:384], x3[s][:, :], ident[:, :]).then_inc(x3T_raw[s], 1)

            @block.scalar
            def _(act):
                with act.Fori(0, PAIRS) as i:
                    n = i + 1
                    for s in range(NS):
                        act.wait_ge(hT_raw[s], n)
                        act.activation(hT[s][:, :], PS[:, 4 * s, 0:S], ACT.Copy).then_inc(hT_ok[s], 1)
                    for s in range(NS):
                        act.wait_ge(qkv_bias_ok[s], n)
                        for j in range(3):
                            ins = act.activation(qkv_a[s][:, j, :], PS[:, 4 * s + 1, j * D:(j + 1) * D], ACT.Exp,
                                                 bias=qkv_bias[s][:, j:j + 1], scale=P_SCALE, accum_out=qkv_sum[s][:, j:j + 1])
                        ins.then_inc(qkv_exp[s], 1)
                    for s in range(NS):
                        act.wait_ge(qkv_aT_raw[s], n)
                        act.activation(qkv_aT[s][:, :, :], PS[:, 4 * s + 2, 0:3 * S], ACT.Copy).then_inc(qkv_aT_ok[s], 1)
                    for s in range(NS):
                        act.wait_ge(proj_raw[s], n)
                        act.activation(qT[s][:, :], PS[:, 4 * s + 3, 0:S], ACT.Copy).then_inc(qv_ok[s], 1)
                        act.activation(v_aug[s][:, :, 0:HD], PS[:, 4 * s + 3, 2 * S:3 * S].rearrange("p (h d) -> p h d", d=HD),
                                       ACT.Copy).then_inc(qv_ok[s], 1)
                    for s in range(NS):
                        act.wait_ge(shift_ok[s], n)
                        act.activation(score[s][:, :, :], score[s][:, :, :], ACT.Exp).then_inc(hexp_ok[s], 1)
                    for s in range(NS):
                        for r in range(4):
                            act.wait_ge(expT_raw[s], i * 4 + (r + 1))
                            act.activation(expT[s][:, 4 * r:4 * r + 4, :], PS[:, 4 * s + r, :], ACT.Copy).then_inc(expT_ok[s], 1)
                    for s in range(NS):
                        act.wait_ge(oT_raw[s], n)
                        act.activation(oT[s][:, :], PS[:, 4 * s + 1, 0:S], ACT.Copy).then_inc(oT_ok[s], 1)
                    for s in range(NS):
                        act.wait_ge(p_bias_ok[s], n)
                        act.activation(p_a[s][:, :], PS[:, 4 * s + 1, 128:256], ACT.Exp, bias=p_bias[s][:, 0:1], scale=P_SCALE,
                                       accum_out=p_sum[s][:, 0:1]).then_inc(p_exp[s], 1)
                    for s in range(NS):
                        act.wait_ge(p_aT_raw[s], n)
                        act.activation(p_aT[s][:, :], PS[:, 4 * s + 1, 256:384], ACT.Copy).then_inc(p_aT_ok[s], 1)
                    for s in range(NS):
                        act.wait_ge(h2T_raw[s], n)
                        act.activation(h2T[s][:, :], PS[:, 4 * s + 2, 128:256], ACT.Copy).then_inc(h2T_ok[s], 1)
                    for s in range(NS):
                        act.wait_ge(f_bias_ok[s], n)
                        act.activation(f_a[s][:, :], PS[:, 4 * s + 3, :], ACT.Exp, bias=f_bias[s][:, 0:1], scale=P_SCALE,
                                       accum_out=f_sum[s][:, 0:1]).then_inc(f_exp[s], 1)
                    for s in range(NS):
                        act.wait_ge(f_aT_raw[s], n)
                        act.activation(f_aT[s][:, :, :], PS[:, 4 * s, :], ACT.Copy).then_inc(f_aT_ok[s], 1)
                    for s in range(NS):
                        act.wait_ge(x3T_raw[s], n)
                        act.activation(x3T[:, bass.ds((i * NS + s) * S, S)], PS[:, 4 * s + 2, 256:384], ACT.Copy).then_inc(stored[s], 1)
                        act.activation(x3_tok[:, bass.ds(i * NS + s, 1), :], x3[s][:, :], ACT.Copy).then_inc(stored[s], 1)
                for s in range(NS):
                    act.wait_ge(stored[s], 2 * PAIRS)

            @block.vector
            def _(dve):
                with dve.Fori(0, PAIRS) as i:
                    n = i + 1
                    for s in range(NS):
                        dve.bn_stats(stats[s][:, :], cond_tok[:, bass.ds(i * NS + s, 1), :]).then_inc(st_ok[s], 1)
                    for s in range(NS):
                        dve.wait_ge(st_ok[s], n)
                        dve.sem_inc(st_seen[s], 1)
                        dve.bn_aggr(mv[s][:, :], stats[s][:, :]).then_inc(mv_ok[s], 1)
                    for s in range(NS):
                        dve.wait_ge(mv_ok[s], n)
                        dve.tensor_scalar(veps[s][:, :], mv[s][:, 1:2], LN_EPS, None, ALU.add).then_inc(veps_ok[s], 1)
                    for s in range(NS):
                        dve.wait_ge(rstd_ok[s], n)
                        dve.tensor_scalar(h[s][:, :], cond_tok[:, bass.ds(i * NS + s, 1), :].rearrange("p o d -> p (o d)"),
                                          mv[s][:, 0:1], rstd[s][:, 0:1], ALU.subtract, ALU.mult).then_inc(h_ok[s], 1)
                    for s in range(NS):
                        dve.wait_ge(qkv_raw[s], n)
                        dve.tensor_reduce(qkv_nmax[s][:, :], PS[:, 4 * s + 1, 0:3 * D].rearrange("p (j n) -> p j n", j=3),
                                          AX.X, ALU.max, negate=True).then_inc(qkv_nmax_ok[s], 1)
                        dve.wait_ge(qkv_nmax_ok[s], n)
                        dve.tensor_scalar(qkv_bias[s][:, :], qkv_nmax[s][:, :], P_SCALE, None, ALU.mult).then_inc(qkv_bias_ok[s], 1)
                    for s in range(NS):
                        dve.wait_ge(qkv_exp[s], n)
                        dve.reciprocal(qkv_inv[s][:, :], qkv_sum[s][:, :]).then_inc(qkv_inv_ok[s], 1)
                        dve.wait_ge(qkv_inv_ok[s], n)
                        dve.tensor_tensor(qkv_a[s][:, :, :], qkv_a[s][:, :, :],
                                          qkv_inv[s][:, :].unsqueeze(2).to_broadcast([S, 3, D]), ALU.mult).then_inc(qkv_a_ok[s], 1)
                    for s in range(NS):
                        dve.wait_ge(proj_raw[s], n)
                        dve.tensor_tensor(k_heads[s][:, :, :], PS[:, 4 * s:4 * s + 1, 0:S].to_broadcast([D, 4, S]),
                                          head4[:, :].unsqueeze(2).to_broadcast([D, 4, S]), ALU.mult).then_inc(kh_ok[s], 1)
                    for s in range(NS):
                        dve.wait_ge(score_raw[s], n)
                        dve.tensor_tensor(score[s][:, :, :], PS[:, 4 * s:4 * s + 4, :].rearrange("p r (j k) -> p (r j) k", k=S),
                                          causal[:, :].unsqueeze(1).to_broadcast([S, HEADS, S]), ALU.add).then_inc(score_ok[s], 1)
                        dve.wait_ge(score_ok[s], n)
                        dve.tensor_reduce(head_max[s][:, :], score[s][:, :, :], AX.X, ALU.max).then_inc(hmax_ok[s], 1)
                        dve.wait_ge(hmax_ok[s], n)
                        dve.tensor_tensor(score[s][:, :, :], score[s][:, :, :],
                                          head_max[s][:, :].unsqueeze(2).to_broadcast([S, HEADS, S]), ALU.subtract).then_inc(shift_ok[s], 1)
                    for s in range(NS):
                        dve.wait_ge(o_raw[s], n)
                        o_ps = PS[:, 4 * s, 0:HEADS * (HD + 1)].rearrange("p (h d) -> p h d", d=HD + 1)
                        dve.reciprocal(head_inv[s][:, :].unsqueeze(2), o_ps[:, :, HD:HD + 1]).then_inc(hinv_ok[s], 1)
                        dve.wait_ge(hinv_ok[s], n)
                        dve.tensor_tensor(o[s][:, :, :], o_ps[:, :, 0:HD],
                                          head_inv[s][:, :].unsqueeze(2).to_broadcast([S, HEADS, HD]), ALU.mult).then_inc(o_ok[s], 1)
                    for s in range(NS):
                        dve.wait_ge(p_raw[s], n)
                        dve.tensor_reduce(p_nmax[s][:, :], PS[:, 4 * s + 1, 128:256], AX.X, ALU.max, negate=True).then_inc(p_nmax_ok[s], 1)
                        dve.wait_ge(p_nmax_ok[s], n)
                        dve.tensor_scalar(p_bias[s][:, :], p_nmax[s][:, :], P_SCALE, None, ALU.mult).then_inc(p_bias_ok[s], 1)
                    for s in range(NS):
                        dve.wait_ge(p_exp[s], n)
                        dve.reciprocal(p_inv[s][:, :], p_sum[s][:, :]).then_inc(p_inv_ok[s], 1)
                        dve.wait_ge(p_inv_ok[s], n)
                        dve.wait_ge(p_out_raw[s], n)
                        dve.scalar_tensor_tensor(out=x1[s][:, :], in0=PS[:, 4 * s + 2, 0:D], scalar=p_inv[s][:, 0:1],
                                                 in1=cond_tok[:, bass.ds(i * NS + s, 1), :].rearrange("p o d -> p (o d)"),
                                                 op0=ALU.mult, op1=ALU.add).then_inc(x1_ok[s], 1)
                    for s in range(NS):
                        dve.wait_ge(x1_ok[s], n)
                        dve.bn_stats(stats2[s][:, :], x1[s][:, :]).then_inc(f_st_ok[s], 1)
                    for s in range(NS):
                        dve.wait_ge(f_st_ok[s], n)
                        dve.sem_inc(f_st_seen[s], 1)
                        dve.bn_aggr(mv2[s][:, :], stats2[s][:, :]).then_inc(f_mv_ok[s], 1)
                    for s in range(NS):
                        dve.wait_ge(f_mv_ok[s], n)
                        dve.tensor_scalar(veps2[s][:, :], mv2[s][:, 1:2], LN_EPS, None, ALU.add).then_inc(f_veps_ok[s], 1)
                    for s in range(NS):
                        dve.wait_ge(f_rstd_ok[s], n)
                        dve.tensor_scalar(h2[s][:, :], x1[s][:, :], mv2[s][:, 0:1], rstd2[s][:, 0:1],
                                          ALU.subtract, ALU.mult).then_inc(h2_ok[s], 1)
                    for s in range(NS):
                        dve.wait_ge(f_raw[s], n)
                        dve.tensor_reduce(f_nmax[s][:, :], PS[:, 4 * s + 3, :], AX.X, ALU.max, negate=True).then_inc(f_nmax_ok[s], 1)
                        dve.wait_ge(f_nmax_ok[s], n)
                        dve.tensor_scalar(f_bias[s][:, :], f_nmax[s][:, :], P_SCALE, None, ALU.mult).then_inc(f_bias_ok[s], 1)
                    for s in range(NS):
                        dve.wait_ge(f_exp[s], n)
                        dve.reciprocal(f_inv[s][:, :], f_sum[s][:, :]).then_inc(f_inv_ok[s], 1)
                        dve.wait_ge(f_inv_ok[s], n)
                        dve.wait_ge(f_out_raw[s], n)
                        dve.scalar_tensor_tensor(out=x2[s][:, :], in0=PS[:, 4 * s + 1, 384:512], scalar=f_inv[s][:, 0:1],
                                                 in1=x1[s][:, :], op0=ALU.mult, op1=ALU.add).then_inc(x2_ok[s], 1)
                        dve.wait_ge(x2_ok[s], n)
                        dve.tensor_tensor(x3[s][:, :], x2[s][:, :],
                                          x_tok[:, bass.ds(i * NS + s, 1), :].rearrange("p o d -> p (o d)"), ALU.add).then_inc(x3_ok[s], 1)
        signals.clear()



def scan_inputs_phase(nc, a, K):
    import concourse.bass as bass
    from concourse import mybir
    from contextlib import ExitStack
    f32 = mybir.dt.float32
    ALU, ACT = mybir.AluOpType, mybir.ActivationFunctionType
    NS = 2
    PAIRS = NG // NS
    PAD = N_TAPS - 1
    with ExitStack() as ctx:
        def sb(name, shape, dt=f32):
            return ctx.enter_context(nc.sbuf_tensor(name, shape, dt))

        def per(name, shape):
            return [sb(f"{name}{s}", shape) for s in range(NS)]

        signals = Signals(nc, ctx, "pre")
        PS, ident, x3T, gateT, xnT = (K[n] for n in ("PS", "ident", "x3T", "gateT", "xnT"))
        w_inT = sb("w_inT", [D, 2 * DI])
        tembT, taps, chan = sb("tembT", [128, NH, B]), sb("taps", [128, NH, N_TAPS]), sb("chan", [128, NH])
        ln_g, ln_b = sb("ln_g", [S, DI]), sb("ln_b", [S, DI])
        w_B, w_Cdt = sb("w_B", [128, NH, N_STATE]), sb("w_Cdt", [128, NH, 48])
        w_dtT = sb("w_dtT", [48, 48])
        state_cols = sb("state_cols", [N_STATE, 2])
        a_tanh, a_step = sb("a_tanh", [N_STATE, 1]), sb("a_step", [N_STATE, 1])
        ones_col, minus_half, plus_half = sb("ones_col", [128, 1]), sb("minus_half3", [S, GB]), sb("plus_half3", [S, GB])
        xr = per("xr", [128, NH, GB, PAD + S])
        conv = per("conv", [128, NH, GB, S])
        stats, mv, veps, rstd = per("st3", [S, GB, 6]), per("mv3", [S, GB, 2]), per("veps3", [S, GB]), per("rstd3", [S, GB])
        xn = per("xn", [S, GB, DI])
        xng, sq = per("xng", [128, NH, GT]), per("sq", [128, NH, GT])
        norm2, norm = per("norm2", [S, GB]), per("norm", [S, GB])
        bd = per("bd", [S, GB, N_STATE])
        cdt = per("cdt", [48, GT])
        ad = per("ad", [N_STATE, GT])

        loads = [(w_inT[:, :], a["w_inT"]), (tembT[:, :, :], a["condT"].rearrange("(h p) b -> p h b", p=128)),
                 (taps[:, :, :], a["taps"].rearrange("(h p) k -> p h k", p=128)),
                 (chan[:, :], a["b_conv"].rearrange("(h p) -> p h", p=128)),
                 (ln_g[:, :], a["ln_g"].rearrange("(o c) -> o c", o=1).partition_broadcast(S)),
                 (ln_b[:, :], a["ln_b"].rearrange("(o c) -> o c", o=1).partition_broadcast(S)),
                 (w_B[:, :, :], a["w_xpT"][:, 0:16].rearrange("(h p) s -> p h s", p=128)),
                 (w_Cdt[:, :, 0:16], a["w_xpT"][:, 16:32].rearrange("(h p) s -> p h s", p=128)),
                 (w_Cdt[:, :, 32:48], a["w_xpT"][:, 32:48].rearrange("(h p) s -> p h s", p=128)),
                 (w_dtT[32:48, 0:N_STATE], a["w_dtT"]), (state_cols[:, :], a["state_cols"])]
        cleared, loaded, filled, a_tanh_ok, a_step_ok = signals.take_all("cleared loaded filled a_tanh_ok a_step_ok")
        xn_sent, bd_sent, c_sent, ad_sent = signals.take_all("xn_sent bd_sent c_sent ad_sent", NS)
        with nc.Block() as block:
            @block.sync
            def _(sp):
                for s in range(NS):
                    for sent in (xn_sent, bd_sent, c_sent, ad_sent):
                        sp.sem_inc(sent[s], 16)
                sp.wait_ge(cleared, 2)
                for dst, src in loads:
                    sp.dma_start(dst, src, allow_slow_non_contiguous=True).then_inc(loaded, 16)
                sp.wait_ge(loaded, 16 * len(loads))

            @block.gpsimd
            def _(pool):
                pool.memset(w_Cdt[:, :, :], 0.0).then_inc(cleared, 1)
                pool.memset(w_dtT[:, :], 0.0).then_inc(cleared, 1)
                pool.memset(ones_col[:, :], 1.0).then_inc(filled, 1)
                pool.memset(minus_half[:, :], -0.5).then_inc(filled, 1)
                pool.memset(plus_half[:, :], 0.5).then_inc(filled, 1)
                for s in range(NS):
                    pool.memset(xr[s][:, :, :, :], 0.0).then_inc(filled, 1)
                pool.wait_ge(filled, 3 + NS)

            @block.scalar
            def _(act):
                act.wait_ge(loaded, 16 * len(loads))
                act.activation(a_tanh[:, :], state_cols[:, 1:2], ACT.Tanh).then_inc(a_tanh_ok, 1)

            @block.vector
            def _(dve):
                dve.wait_ge(a_tanh_ok, 1)
                dve.tensor_scalar(a_step[:, :], a_tanh[:, :], -0.01, None, ALU.mult).then_inc(a_step_ok, 1)
                dve.wait_ge(a_step_ok, 1)

        (in_raw, gate_ok, xr_ok, conv_ok, xc_ok, xc_tok_raw, st_ok, st_seen, mv_ok, veps_ok, rstd_ok, xhat_ok,
         scaled_ok, xn_ok, xnT_raw, xng_ok, xnT_ok, sq_ok, b_raw, cdt_raw, norm2_ok, norm_ok, bd_ok, cdt_ok, dt_raw,
         tanh_ok, ad_ok) = signals.take_all(
            "in_raw gate_ok xr_ok conv_ok xc_ok xc_tok_raw st_ok st_seen mv_ok veps_ok rstd_ok xhat_ok "
            "scaled_ok xn_ok xnT_raw xng_ok xnT_ok sq_ok b_raw cdt_raw norm2_ok norm_ok bd_ok cdt_ok dt_raw "
            "tanh_ok ad_ok", NS)

        with nc.Block() as block:
            @block.sync
            def _(sp):
                with sp.Fori(0, PAIRS) as i:
                    n = i + 1
                    for s in range(NS):
                        first = (i * NS + s) * GB
                        sp.wait_ge(xn_ok[s], n)
                        sp.dma_start(K["xn_d"][bass.ds(first, GB), :, :].rearrange("b t c -> t b c"), xn[s][:, :, :]).then_inc(xn_sent[s], 16)
                    for s in range(NS):
                        first = (i * NS + s) * GB
                        sp.wait_ge(bd_ok[s], n)
                        sp.dma_start(K["bd_d"][bass.ds(first, GB), :, :].rearrange("b t s -> t b s"), bd[s][:, :, :]).then_inc(bd_sent[s], 16)
                        sp.wait_ge(cdt_ok[s], n)
                        sp.dma_start(K["c_d"][bass.ds(first, GB), :, :].rearrange("b s t -> s b t"),
                                     cdt[s][0:N_STATE, :].rearrange("s (b t) -> s b t", b=GB)).then_inc(c_sent[s], 16)
                        sp.wait_ge(ad_ok[s], n)
                        sp.dma_start(K["ad_d"][bass.ds(first, GB), :, :].rearrange("b s t -> s b t"),
                                     ad[s][:, :].rearrange("s (b t) -> s b t", b=GB)).then_inc(ad_sent[s], 16)
                for s in range(NS):
                    for sent in (xn_sent, bd_sent, c_sent, ad_sent):
                        sp.wait_ge(sent[s], 16 * (PAIRS + 1))

            @block.gpsimd
            def _(pool):
                with pool.Fori(0, PAIRS) as i:
                    n = i + 1
                    for s in range(NS):
                        pool.wait_ge(veps_ok[s], n)
                        pool.tensor_tensor(rstd[s][:, :], veps[s][:, :], minus_half[:, :], ALU.pow).then_inc(rstd_ok[s], 1)
                    for s in range(NS):
                        pool.wait_ge(xhat_ok[s], n)
                        pool.tensor_tensor(xn[s][:, :, :], xn[s][:, :, :], ln_g[:, :].unsqueeze(1).to_broadcast([S, GB, DI]),
                                           ALU.mult).then_inc(scaled_ok[s], 1)
                        pool.wait_ge(scaled_ok[s], n)
                        pool.tensor_tensor(xn[s][:, :, :], xn[s][:, :, :], ln_b[:, :].unsqueeze(1).to_broadcast([S, GB, DI]),
                                           ALU.add).then_inc(xn_ok[s], 1)
                    for s in range(NS):
                        pool.wait_ge(norm2_ok[s], n)
                        pool.tensor_tensor(norm[s][:, :], norm2[s][:, :], plus_half[:, :], ALU.pow).then_inc(norm_ok[s], 1)

            @block.tensor
            def _(pe):
                with pe.Fori(0, PAIRS) as i:
                    n = i + 1
                    for s in range(NS):
                        for j in range(4):
                            mm = pe.matmul(PS[:, 4 * s + j, :], w_inT[:, j * 128:(j + 1) * 128],
                                           x3T[:, bass.ds((i * NS + s) * GT, GT)], start=True, stop=True)
                        mm.then_inc(in_raw[s], 1)
                    for s in range(NS):
                        pe.wait_ge(xc_ok[s], n)
                        for b in range(GB):
                            for h in range(NH):
                                at = (b % 2) * DI + h * 128
                                mm = pe.transpose(PS[:, 4 * s + b // 2, at:at + 128], conv[s][:, h, b, :], ident[:, :])
                        mm.then_inc(xc_tok_raw[s], 1)
                    for s in range(NS):
                        pe.wait_ge(xn_ok[s], n)
                        pe.wait_ge(gate_ok[s], n)
                        for h in range(NH):
                            for b in range(GB):
                                mm = pe.transpose(PS[:, 4 * s + 2 + h, b * S:(b + 1) * S], xn[s][:, b, h * 128:(h + 1) * 128], ident[:, :])
                        mm.then_inc(xnT_raw[s], 1)
                    for s in range(NS):
                        pe.wait_ge(sq_ok[s], n)
                        for h in range(NH):
                            mm = pe.matmul(PS[0:48, 4 * s + 1, :], w_Cdt[:, h, :], xng[s][:, h, :], start=(h == 0), stop=(h == 1))
                        mm.then_inc(cdt_raw[s], 1)
                        for b in range(GB):
                            for h in range(NH):
                                pe.matmul(PS[:, 4 * s, b * 16:(b + 1) * 16], xng[s][:, h, b * S:(b + 1) * S], w_B[:, h, :],
                                          start=(h == 0), stop=(h == 1))
                            for h in range(NH):
                                mm = pe.matmul(PS[:, 4 * s, 64 + b:65 + b], sq[s][:, h, b * S:(b + 1) * S], ones_col[:, :],
                                               start=(h == 0), stop=(h == 1))
                        mm.then_inc(b_raw[s], 1)
                    for s in range(NS):
                        pe.wait_ge(xnT_ok[s], n)
                        pe.wait_ge(cdt_ok[s], n)
                        pe.matmul(PS[0:48, 4 * s + 2, :], w_dtT[32:48, :], cdt[s][32:48, :], start=True, stop=True).then_inc(dt_raw[s], 1)
                    for s in range(NS):
                        pe.wait_ge(bd_ok[s], n)
                        pe.wait_ge(tanh_ok[s], n)

            @block.scalar
            def _(act):
                with act.Fori(0, PAIRS) as i:
                    n = i + 1
                    for s in range(NS):
                        act.wait_ge(in_raw[s], n)
                        for h in range(NH):
                            ins = act.activation(gateT[:, h, bass.ds((i * NS + s) * GT, GT)], PS[:, 4 * s + 2 + h, :], ACT.Silu)
                        ins.then_inc(gate_ok[s], 1)
                    for s in range(NS):
                        act.wait_ge(conv_ok[s], N_TAPS * NH * n)
                        act.activation(conv[s][:, :, :, :], conv[s][:, :, :, :], ACT.Silu).then_inc(xc_ok[s], 1)
                    for s in range(NS):
                        act.wait_ge(xnT_raw[s], n)
                        act.activation(xng[s][:, :, :], PS[:, 4 * s + 2:4 * s + 4, :], ACT.Copy).then_inc(xng_ok[s], 1)
                        act.activation(xnT[:, :, bass.ds((i * NS + s) * GT, GT)], PS[:, 4 * s + 2:4 * s + 4, :], ACT.Copy).then_inc(xnT_ok[s], 1)
                        act.wait_ge(xng_ok[s], n)
                        act.activation(sq[s][:, :, :], xng[s][:, :, :], ACT.Square).then_inc(sq_ok[s], 1)
                    for s in range(NS):
                        act.wait_ge(c_sent[s], 16 * n)
                        act.wait_ge(cdt_raw[s], n)
                        act.activation(cdt[s][:, :], PS[0:48, 4 * s + 1, :], ACT.Copy).then_inc(cdt_ok[s], 1)
                    for s in range(NS):
                        act.wait_ge(ad_sent[s], 16 * n)
                        act.wait_ge(dt_raw[s], n)
                        act.activation(ad[s][:, :], PS[0:N_STATE, 4 * s + 2, :], ACT.Tanh, bias=state_cols[:, 0:1]).then_inc(tanh_ok[s], 1)

            @block.vector
            def _(dve):
                with dve.Fori(0, PAIRS) as i:
                    n = i + 1
                    for s in range(NS):
                        dve.wait_ge(in_raw[s], n)
                        for h in range(NH):
                            dve.tensor_tensor(xr[s][:, h, :, PAD:PAD + S], PS[:, 4 * s + h, :].rearrange("p (b t) -> p b t", b=GB),
                                              tembT[:, h, bass.ds((i * NS + s) * GB, GB)].unsqueeze(2).to_broadcast([128, GB, S]),
                                              ALU.add).then_inc(xr_ok[s], 1)
                    for k in range(N_TAPS):
                        for s in range(NS):
                            for h in range(NH):
                                if k == 0:
                                    dve.wait_ge(xr_ok[s], NH * n)
                                    ins = dve.tensor_scalar(conv[s][:, h, :, :], xr[s][:, h, :, 0:S], taps[:, h, 0:1], chan[:, h:h + 1],
                                                            ALU.mult, ALU.add)
                                else:
                                    dve.wait_ge(conv_ok[s], i * (N_TAPS * NH) + ((k - 1) * NH + h + 1))
                                    ins = dve.scalar_tensor_tensor(out=conv[s][:, h, :, :], in0=xr[s][:, h, :, k:k + S],
                                                                   scalar=taps[:, h, k:k + 1], in1=conv[s][:, h, :, :],
                                                                   op0=ALU.mult, op1=ALU.add)
                                ins.then_inc(conv_ok[s], 1)
                    for s in range(NS):
                        dve.wait_ge(xc_tok_raw[s], n)
                        for b in range(GB):
                            ins = dve.bn_stats(stats[s][:, b, :], PS[:, 4 * s + b // 2, (b % 2) * DI:(b % 2 + 1) * DI])
                        ins.then_inc(st_ok[s], 1)
                        dve.wait_ge(st_ok[s], n)
                        dve.sem_inc(st_seen[s], 1)
                        for b in range(GB):
                            ins = dve.bn_aggr(mv[s][:, b, :], stats[s][:, b, :])
                        ins.then_inc(mv_ok[s], 1)
                        dve.wait_ge(mv_ok[s], n)
                        dve.tensor_scalar(veps[s][:, :].unsqueeze(2), mv[s][:, :, 1:2], LN_EPS, None, ALU.add).then_inc(veps_ok[s], 1)
                    for s in range(NS):
                        dve.wait_ge(xn_sent[s], 16 * n)
                        dve.wait_ge(rstd_ok[s], n)
                        for b in range(GB):
                            ins = dve.tensor_scalar(xn[s][:, b, :], PS[:, 4 * s + b // 2, (b % 2) * DI:(b % 2 + 1) * DI],
                                                    mv[s][:, b, 0:1], rstd[s][:, b:b + 1], ALU.subtract, ALU.mult)
                        ins.then_inc(xhat_ok[s], 1)
                    for s in range(NS):
                        dve.wait_ge(b_raw[s], n)
                        dve.tensor_scalar(norm2[s][:, :], PS[:, 4 * s, 64:64 + GB], 1.0, None, ALU.min).then_inc(norm2_ok[s], 1)
                    for s in range(NS):
                        dve.wait_ge(bd_sent[s], 16 * n)
                        dve.wait_ge(norm_ok[s], n)
                        dve.tensor_tensor(bd[s][:, :, :], PS[:, 4 * s, 0:GB * N_STATE].rearrange("p (b s) -> p b s", b=GB),
                                          norm[s][:, :].unsqueeze(2).to_broadcast([S, GB, N_STATE]), ALU.mult).then_inc(bd_ok[s], 1)
                    for s in range(NS):
                        dve.wait_ge(tanh_ok[s], n)
                        dve.tensor_scalar(ad[s][:, :], ad[s][:, :], a_step[:, 0:1], 1.0, ALU.mult, ALU.add).then_inc(ad_ok[s], 1)
        signals.clear()


def scan_phase(nc, a, K):
    import concourse.bass as bass
    from concourse import mybir
    from contextlib import ExitStack
    f32 = mybir.dt.float32
    ALU, ACT = mybir.AluOpType, mybir.ActivationFunctionType
    BG = 128 // N_STATE
    G = B // BG
    HALF = 8
    STEPS = 2 * HALF
    CHUNKS = S // STEPS
    RING = 4
    with ExitStack() as ctx:
        def sb(name, shape, dt=f32):
            return ctx.enter_context(nc.sbuf_tensor(name, shape, dt))

        signals = Signals(nc, ctx, "scan")
        PS, ident, xnT = (K[n] for n in ("PS", "ident", "xnT"))
        skip = sb("skip", [128, NH])
        decay, c_all = sb("decay", [128, G, S]), sb("c_all", [128, G, S])
        own = sb("own", [128, BG])
        PARTS = 4
        f32r = mybir.dt.float32r
        same_batch = sb("same_batch", [PARTS * B, B])
        x_in = [sb(f"x_in{k}", [PARTS * B, HALF, DI]) for k in range(2)]
        x_part = [sb(f"x_part{k}", [PARTS * B, HALF, DI], f32r) for k in range(2)]
        bd_in = [sb(f"bd_in{k}", [PARTS * B, HALF, N_STATE]) for k in range(2)]
        bd_high = [sb(f"bd_high{k}", [PARTS * B, HALF, N_STATE], f32r) for k in range(2)]
        bd_part = [sb(f"bd_part{k}", [PARTS * B, HALF, N_STATE]) for k in range(2)]
        bd_diag = [sb(f"bd_diag{k}", [PARTS * B, HALF, B, N_STATE], f32r) for k in range(2)]
        decay_now = [sb(f"decay_now{k}", [128, G, HALF]) for k in range(2)]
        WIDE = HALF * BG
        c_diag = [sb(f"c_diag{k}", [128, G * HALF * WIDE + WIDE]) for k in range(2)]
        y_tok = sb("y_tok", [WIDE, G, DI])
        y_new = sb("y_new", [128, NH, HALF * B])
        grown = sb("grown", [128, G, DI])
        state = [K["x3T"][:, k * G * DI:(k + 1) * G * DI].rearrange("p (g c) -> p g c", g=G) for k in range(RING)]

        resident_in, ones_ok, cut_ok, zero_ok, same_ok = signals.take_all("resident_in ones_ok cut_ok zero_ok same_ok")
        x_loaded, bd_loaded, diag_ok, c_ok, decay_ok = signals.take_all("x_loaded bd_loaded diag_ok c_ok decay_ok", 2)
        spread_go, load_go, add_go = signals.take_all("spread_go load_go add_go")
        x_high, x_parts, bd_high_ok, bd_part_ok, bd_low_ok = signals.take_all("x_high x_parts bd_high_ok bd_part_ok bd_low_ok", 2)
        bx_raw, grown_ok, state_ok, y_raw, y_stored = signals.take_all("bx_raw grown_ok state_ok y_raw y_stored")
        y_copied, yT_raw, y_added, wide_zero, skipped, turn_go = signals.take_all("y_copied yT_raw y_added wide_zero skipped turn_go")

        with nc.Block() as block:
            @block.sync
            def _(sp):
                sp.dma_start(decay[:, :, :], K["ad_d"].rearrange("(g b) s t -> (b s) g t", g=G)).then_inc(resident_in, 16)
                sp.dma_start(c_all[:, :, :], K["c_d"].rearrange("(g b) s t -> (b s) g t", g=G)).then_inc(resident_in, 16)
                sp.dma_start(skip[:, :], a["D"].rearrange("(h p) -> p h", p=128), allow_slow_non_contiguous=True).then_inc(resident_in, 16)
                sp.wait_ge(resident_in, 48)
                sp.sem_inc(state_ok, 1)
                sp.sem_inc(grown_ok, 2)
                sp.sem_inc(y_raw, RING)
                sp.sem_inc(y_stored, 2)
                sp.sem_inc(y_added, 1)
                sp.sem_inc(yT_raw, 1)

            @block.gpsimd
            def _(pool):
                pool.memset(own[:, :], 1.0).then_inc(ones_ok, 1)
                pool.memset(state[RING - 1][:, :, :], 0.0).then_inc(zero_ok, 1)
                for k in range(2):
                    pool.memset(c_diag[k][:, :], 0.0).then_inc(wide_zero, 1)
                pool.wait_ge(ones_ok, 1)
                pool.affine_select(out=own[:, :], in_=own[:, :], compare_op=ALU.is_ge, fill=0.0, base=0,
                                   pattern=[[-N_STATE, BG]], channel_multiplier=1).then_inc(cut_ok, 1)
                pool.wait_ge(cut_ok, 1)
                pool.affine_select(out=own[:, :], in_=own[:, :], compare_op=ALU.is_ge, fill=0.0, base=N_STATE - 1,
                                   pattern=[[N_STATE, BG]], channel_multiplier=-1).then_inc(cut_ok, 1)
                pool.wait_ge(cut_ok, 2)
                pool.wait_ge(zero_ok, 1)
                pool.wait_ge(wide_zero, 2)

            @block.vector
            def _(dve):
                dve.wait_ge(resident_in, 48)
                for h in range(NH):
                    dve.tensor_scalar(xnT[:, h, :], xnT[:, h, :], skip[:, h:h + 1], None, ALU.mult).then_inc(skipped, 1)
                dve.wait_ge(skipped, NH)
                dve.tensor_reduce(same_batch[:, :], ident[:, :].rearrange("p (q b) -> p b q", q=PARTS), mybir.AxisListType.X,
                                  ALU.add).then_inc(same_ok, 1)
                dve.wait_ge(same_ok, 1)

        with nc.Block() as block:
            @block.sync
            def _(sp):
                def load(k, at):
                    for q in range(PARTS):
                        sp.dma_start(x_in[k][q * B:(q + 1) * B, :, :], K["xn_d"][:, bass.ds(at, HALF), :]).then_inc(x_loaded[k], 16)
                        sp.dma_start(bd_in[k][q * B:(q + 1) * B, :, :], K["bd_d"][:, bass.ds(at, HALF), :]).then_inc(bd_loaded[k], 16)

                for k in range(2):
                    load(k, k * HALF)
                with sp.Fori(1, CHUNKS) as c:
                    for k in range(2):
                        sp.wait_ge(bd_low_ok[k], 2 * c)
                        sp.wait_ge(x_parts[k], c)
                        sp.sem_inc(load_go, 1)
                        load(k, c * STEPS + k * HALF)

            @block.gpsimd
            def _(pool):
                def spread_bd(k, n):
                    pool.tensor_tensor(bd_diag[k][:, :, :, :],
                                       bd_part[k][:, :, :].unsqueeze(2).to_broadcast([PARTS * B, HALF, B, N_STATE]),
                                       same_batch[:, :].unsqueeze(1).unsqueeze(3).to_broadcast([PARTS * B, HALF, B, N_STATE]),
                                       ALU.mult).then_inc(diag_ok[k], 1)

                def spread_c(k, at, n):
                    for g in range(G):
                        own_columns = c_diag[k][:, g * HALF * WIDE:(g + 1) * HALF * WIDE + WIDE].rearrange(
                            "p (t w) -> p t w", w=WIDE + BG)[:, :, 0:BG]
                        pool.tensor_tensor(own_columns, c_all[:, g, bass.ds(at, HALF)].unsqueeze(2).to_broadcast([128, HALF, BG]),
                                           own[:, :].unsqueeze(1).to_broadcast([128, HALF, BG]), ALU.mult).then_inc(c_ok[k], 1)
                    pool.tensor_copy(decay_now[k][:, :, :], decay[:, :, bass.ds(at, HALF)]).then_inc(decay_ok[k], 1)
                    pool.wait_ge(diag_ok[k], n)
                    pool.wait_ge(c_ok[k], G * n)
                    pool.wait_ge(decay_ok[k], n)

                def x_low(k):
                    low = x_part[k][2 * B:4 * B, :, :]
                    pool.tensor_tensor(low, x_in[k][2 * B:4 * B, :, :], low.bitcast(f32), ALU.subtract).then_inc(x_parts[k], 1)

                def bd_low(k, n):
                    pool.wait_ge(bd_high_ok[k], n)
                    pool.wait_ge(x_parts[k], n)
                    for q in (1, 3):
                        part = (slice(q * B, (q + 1) * B),) + (slice(None),) * 2
                        ins = pool.tensor_tensor(bd_part[k][part], bd_in[k][part], bd_high[k][part].bitcast(f32), ALU.subtract)
                        ins.then_inc(bd_low_ok[k], 1)
                        pool.wait_ge(bd_low_ok[k], 2 * n - (q == 1))
                    pool.wait_ge(bd_part_ok[k], n)

                def add(k, at, n):
                    for h in range(NH):
                        into = xnT[:, h, :].rearrange("p (b t) -> p b t", b=B)[:, :, bass.ds(at, HALF)]
                        ins = pool.tensor_tensor(into, into, y_new[:, h, :].rearrange("p (g t b) -> p g b t", g=G, t=HALF), ALU.add)
                    ins.then_inc(y_added, 1)
                    pool.wait_ge(y_added, n + 1)

                for k in range(2):
                    pool.wait_ge(x_high[k], 1)
                    x_low(k)
                    bd_low(k, 1)
                    spread_bd(k, 1)
                    spread_c(k, k * HALF, 1)
                with pool.Fori(1, CHUNKS) as c:
                    for k in range(2):
                        pool.wait_ge(x_high[k], c + 1)
                        x_low(k)
                        bd_low(k, c + 1)
                        spread_bd(k, c + 1)
                        pool.wait_ge(y_stored, c * 2 + (k + 1))
                        pool.sem_inc(add_go, 1)
                        add(k, (c - 1) * STEPS + k * HALF, c * 2 + (k - 1))
                        spread_c(k, c * STEPS + k * HALF, c + 1)
                for k in range(2):
                    pool.wait_ge(y_stored, CHUNKS * 2 + (k + 1))
                    add(k, (CHUNKS - 1) * STEPS + k * HALF, CHUNKS * 2 + (k - 1))

            @block.tensor
            def _(pe):
                def inputs(c, j):
                    k, tt = j // HALF, j % HALF
                    if tt == 0:
                        pe.wait_ge(x_parts[k], c + 1)
                        pe.wait_ge(diag_ok[k], c + 1)
                    pe.wait_ge(grown_ok, c * STEPS + (j + 1))
                    for g in range(G):
                        mm = pe.matmul(PS[:, 2 * (j % 2) + g // 2, (g % 2) * DI:(g % 2 + 1) * DI],
                                       bd_diag[k][:, tt, g * BG:(g + 1) * BG, :].rearrange("p b s -> p (b s)"), x_part[k][:, tt, :],
                                       start=True, stop=True)
                    mm.then_inc(bx_raw, 1)

                def outputs(c, j):
                    k, tt = j // HALF, j % HALF
                    if tt == 0:
                        pe.wait_ge(c_ok[k], G * (c + 1))
                        pe.wait_ge(y_stored, c * 2 + (k + 1))
                    pe.wait_ge(state_ok, c * STEPS + (j + 2))
                    for g in range(G):
                        at = (g * HALF + tt) * WIDE
                        mm = pe.matmul(PS[0:WIDE, 4 + 2 * k + g // 2, (g % 2) * DI:(g % 2 + 1) * DI], c_diag[k][:, at:at + WIDE],
                                       state[j % RING][:, g, :], start=(tt == 0 and g % 2 == 0),
                                       stop=(tt == HALF - 1 and g % 2 == 1))
                    mm.then_inc(y_raw, 1)
                    if tt == HALF - 1:
                        pe.wait_ge(y_copied, c * 2 + (k + 1))
                        pe.sem_inc(turn_go, 1)
                        for h in range(NH):
                            for g in range(G):
                                at = (h * G + g) * WIDE
                                mm = pe.transpose(PS[:, 4 + 2 * k, at:at + WIDE], y_tok[:, g, h * 128:(h + 1) * 128],
                                                  ident[0:WIDE, 0:WIDE])
                        mm.then_inc(yT_raw, 1)

                inputs(0, 0)
                inputs(0, 1)
                with pe.Fori(0, CHUNKS - 1) as c:
                    for j in range(STEPS):
                        inputs(c + (j + 2) // STEPS, (j + 2) % STEPS)
                        outputs(c, j)
                for j in range(STEPS):
                    if j + 2 < STEPS:
                        inputs(CHUNKS - 1, j + 2)
                    outputs(CHUNKS - 1, j)

            @block.scalar
            def _(act):
                def split_x(k, n):
                    act.wait_ge(x_loaded[k], 16 * PARTS * n)
                    act.activation(x_part[k][:, :, :], x_in[k][:, :, :], ACT.Copy).then_inc(x_high[k], 1)

                def split_bd(k, n):
                    act.wait_ge(bd_loaded[k], 16 * PARTS * n)
                    act.activation(bd_high[k][:, :, :], bd_in[k][:, :, :], ACT.Copy).then_inc(bd_high_ok[k], 1)
                    act.wait_ge(bd_high_ok[k], n)
                    for q in (0, 2):
                        ins = act.activation(bd_part[k][q * B:(q + 1) * B, :, :], bd_high[k][q * B:(q + 1) * B, :, :].bitcast(f32), ACT.Copy)
                    ins.then_inc(bd_part_ok[k], 1)

                def copy_y(c, k):
                    act.wait_ge(yT_raw, c * 2 + (k + 1))
                    act.wait_ge(y_raw, c * STEPS + (RING + (k + 1) * HALF))
                    act.activation(y_tok[:, :, :], PS[0:WIDE, 4 + 2 * k:4 + 2 * k + 2, :], ACT.Copy).then_inc(y_copied, 1)

                def store_y(c, k):
                    act.wait_ge(y_added, c * 2 + (k + 1))
                    act.wait_ge(yT_raw, c * 2 + (k + 2))
                    act.activation(y_new[:, :, :], PS[:, 4 + 2 * k, :], ACT.Copy).then_inc(y_stored, 1)

                for k in range(2):
                    split_x(k, 1)
                    split_bd(k, 1)
                with act.Fori(0, CHUNKS - 1) as c:
                    for k in range(2):
                        act.wait_ge(bx_raw, c * STEPS + (k + 1) * HALF)
                        split_x(k, c + 2)
                        split_bd(k, c + 2)
                        copy_y(c, k)
                        store_y(c, k)
                for k in range(2):
                    copy_y(CHUNKS - 1, k)
                    store_y(CHUNKS - 1, k)

            @block.vector
            def _(dve):
                with dve.Fori(0, CHUNKS) as c:
                    for j in range(STEPS):
                        k, tt = j // HALF, j % HALF
                        if tt == 0:
                            dve.wait_ge(decay_ok[k], c + 1)
                        dve.wait_ge(bx_raw, c * STEPS + (j + 1))
                        dve.wait_ge(state_ok, c * STEPS + (j + 1))
                        for g in range(G):
                            ins = dve.scalar_tensor_tensor(out=grown[:, g, :], in0=state[(j - 1) % RING][:, g, :],
                                                           scalar=decay_now[k][:, g, tt:tt + 1],
                                                           in1=PS[:, 2 * (j % 2) + g // 2, (g % 2) * DI:(g % 2 + 1) * DI],
                                                           op0=ALU.mult, op1=ALU.add)
                        ins.then_inc(grown_ok, 1)
                        dve.wait_ge(grown_ok, c * STEPS + (j + 3))
                        dve.wait_ge(y_raw, c * STEPS + (j + 1))
                        dve.tensor_scalar(state[j % RING][:, :, :], grown[:, :, :], CLIP, -CLIP, ALU.min, ALU.max).then_inc(state_ok, 1)
        signals.clear()


def expert_inputs_phase(nc, a, K):
    import concourse.bass as bass
    from concourse import mybir
    from contextlib import ExitStack
    f32 = mybir.dt.float32
    ALU, ACT, AX = mybir.AluOpType, mybir.ActivationFunctionType, mybir.AxisListType
    NS = 2
    PAIRS = NG // NS
    with ExitStack() as ctx:
        def sb(name, shape, dt=f32):
            return ctx.enter_context(nc.sbuf_tensor(name, shape, dt))

        def per(name, shape):
            return [sb(f"{name}{s}", shape) for s in range(NS)]

        signals = Signals(nc, ctx, "gates")
        PS, ident, yT, gateT, hT, gate = (K[n] for n in ("PS", "ident", "xnT", "gateT", "hT", "gate"))
        w_outT, router = sb("w_outT", [128, NH, D]), sb("router", [D, E_ROUTED])
        minus_half, rank = sb("minus_half5", [S, GB]), sb("rank", [S, E_ROUTED])
        z = per("z", [128, NH, GT])
        x4, x4n, x4T, junk = per("x4", [S, GB, D]), per("x4n", [S, GB, D]), per("x4T", [D, GT]), per("junk", [S, D])
        ms, meps, rrms = per("ms", [S, GB]), per("meps", [S, GB]), per("rrms", [S, GB])
        small = {n: per(n, [S, GB]) for n in ("lmax", "gsum", "ginv", "top", "pick", "msum", "msum_eps", "minv")}
        wide = {n: per(n, [S, GB, E_ROUTED]) for n in ("shifted", "gexp", "g", "same", "ranked", "first", "rest", "second", "both", "kept")}
        loads = [(w_outT[:, :, :], a["w_outT"].rearrange("(h p) d -> p h d", p=128)), (router[:, :], a["router"])]
        loaded, filled = signals.take_all("loaded filled")
        with nc.Block() as block:
            @block.sync
            def _(sp):
                for dst, src in loads:
                    sp.dma_start(dst, src, allow_slow_non_contiguous=True).then_inc(loaded, 16)
                sp.wait_ge(loaded, 16 * len(loads))

            @block.gpsimd
            def _(pool):
                pool.memset(minus_half[:, :], -0.5).then_inc(filled, 1)
                for e in range(E_ROUTED):
                    pool.memset(rank[:, e:e + 1], float(E_ROUTED - e)).then_inc(filled, 1)
                pool.wait_ge(filled, 1 + E_ROUTED)

        (z_ok, x4_raw, ms_ok, x4_ok, meps_ok, rrms_ok, x4n_ok, hT_raw, x4T_raw, hT_ok, x4T_ok, router_raw, link,
         shifted_ok, gexp_ok, inv_ok, gate_ok) = signals.take_all(
            "z_ok x4_raw ms_ok x4_ok meps_ok rrms_ok x4n_ok hT_raw x4T_raw hT_ok x4T_ok router_raw link "
            "shifted_ok gexp_ok inv_ok gate_ok", NS)
        with nc.Block() as block:
            @block.gpsimd
            def _(pool):
                with pool.Fori(0, PAIRS) as i:
                    for s in range(NS):
                        pool.wait_ge(meps_ok[s], i + 1)
                        pool.tensor_tensor(rrms[s][:, :], meps[s][:, :], minus_half[:, :], ALU.pow).then_inc(rrms_ok[s], 1)

            @block.tensor
            def _(pe):
                with pe.Fori(0, PAIRS) as i:
                    n = i + 1
                    for s in range(NS):
                        pe.wait_ge(z_ok[s], NH * n)
                        for b in range(GB):
                            for h in range(NH):
                                mm = pe.matmul(PS[:, 4 * s, b * D:(b + 1) * D], z[s][:, h, b * S:(b + 1) * S], w_outT[:, h, :],
                                               start=(h == 0), stop=(h == 1))
                        mm.then_inc(x4_raw[s], 1)
                    for s in range(NS):
                        pe.wait_ge(x4_ok[s], n)
                        for b in range(GB):
                            mm = pe.transpose(PS[:, 4 * s + 2, b * S:(b + 1) * S], x4[s][:, b, :], ident[:, :])
                        mm.then_inc(x4T_raw[s], 1)
                    for s in range(NS):
                        pe.wait_ge(x4n_ok[s], n)
                        for b in range(GB):
                            mm = pe.transpose(PS[:, 4 * s + 1, b * S:(b + 1) * S], x4n[s][:, b, :], ident[:, :])
                        mm.then_inc(hT_raw[s], 1)
                    for s in range(NS):
                        pe.wait_ge(x4T_ok[s], n)
                        for b in range(GB):
                            mm = pe.matmul(PS[:, 4 * s + 3, b * 16:b * 16 + E_ROUTED], x4T[s][:, b * S:(b + 1) * S], router[:, :],
                                           start=True, stop=True)
                        mm.then_inc(router_raw[s], 1)

            @block.scalar
            def _(act):
                with act.Fori(0, PAIRS) as i:
                    n = i + 1
                    for s in range(NS):
                        act.wait_ge(x4_raw[s], n)
                        for b in range(GB):
                            ins = act.activation(junk[s][:, :], PS[:, 4 * s, b * D:(b + 1) * D], ACT.Square, accum_out=ms[s][:, b:b + 1])
                            ins.then_inc(ms_ok[s], 1)
                            act.wait_ge(ms_ok[s], i * GB + (b + 1))
                        act.activation(x4[s][:, :, :], PS[:, 4 * s, :], ACT.Copy).then_inc(x4_ok[s], 1)
                    for s in range(NS):
                        act.wait_ge(x4T_raw[s], n)
                        act.activation(x4T[s][:, :], PS[:, 4 * s + 2, :], ACT.Copy).then_inc(x4T_ok[s], 1)
                    for s in range(NS):
                        act.wait_ge(hT_raw[s], n)
                        act.activation(hT[:, bass.ds((i * NS + s) * GT, GT)], PS[:, 4 * s + 1, :], ACT.Copy).then_inc(hT_ok[s], 1)
                    for s in range(NS):
                        act.wait_ge(shifted_ok[s], n)
                        act.activation(wide["gexp"][s][:, :, :], wide["shifted"][s][:, :, :], ACT.Exp).then_inc(gexp_ok[s], 1)
                for s in range(NS):
                    act.wait_ge(hT_ok[s], PAIRS)

            @block.vector
            def _(dve):
                LINKS = 4 + 11 + 4

                def spread(v):
                    return v[:, :].unsqueeze(2).to_broadcast([S, GB, E_ROUTED])

                with dve.Fori(0, PAIRS) as i:
                    n = i + 1
                    for s in range(NS):
                        at = (i * NS + s) * GT
                        for h in range(NH):
                            dve.tensor_tensor(z[s][:, h, :], yT[:, h, bass.ds(at, GT)], gateT[:, h, bass.ds(at, GT)], ALU.mult).then_inc(z_ok[s], 1)
                    for s in range(NS):
                        dve.wait_ge(ms_ok[s], GB * n)
                        dve.tensor_scalar(meps[s][:, :], ms[s][:, :], 1.0 / D, RMS_EPS, ALU.mult, ALU.add).then_inc(meps_ok[s], 1)
                    for s in range(NS):
                        dve.wait_ge(x4_ok[s], n)
                        dve.wait_ge(rrms_ok[s], n)
                        dve.tensor_tensor(x4n[s][:, :, :], x4[s][:, :, :], rrms[s][:, :].unsqueeze(2).to_broadcast([S, GB, D]),
                                          ALU.mult).then_inc(x4n_ok[s], 1)
                    for s in range(NS):
                        count = [0]

                        def step(ins):
                            count[0] += 1
                            ins.then_inc(link[s], 1)
                            dve.wait_ge(link[s], i * LINKS + count[0])

                        w = {k: v[s] for k, v in wide.items()}
                        m = {k: v[s] for k, v in small.items()}
                        dve.wait_ge(router_raw[s], n)
                        logits = PS[:, 4 * s + 3, 0:GB * 16].rearrange("p (b e) -> p b e", e=16)[:, :, 0:E_ROUTED]
                        step(dve.tensor_reduce(m["lmax"][:, :], logits, AX.X, ALU.max))
                        dve.tensor_tensor(w["shifted"][:, :, :], logits, spread(m["lmax"]), ALU.subtract).then_inc(shifted_ok[s], 1)
                        dve.wait_ge(gexp_ok[s], n)
                        step(dve.tensor_reduce(m["gsum"][:, :], w["gexp"][:, :, :], AX.X, ALU.add))
                        step(dve.reciprocal(m["ginv"][:, :], m["gsum"][:, :]))
                        step(dve.tensor_tensor(w["g"][:, :, :], w["gexp"][:, :, :], spread(m["ginv"]), ALU.mult))
                        rank_all = rank[:, :].unsqueeze(1).to_broadcast([S, GB, E_ROUTED])
                        for source, found in (("g", "first"), ("rest", "second")):
                            step(dve.tensor_reduce(m["top"][:, :], w[source][:, :, :], AX.X, ALU.max))
                            step(dve.tensor_tensor(w["same"][:, :, :], w[source][:, :, :], spread(m["top"]), ALU.is_equal))
                            step(dve.tensor_tensor(w["ranked"][:, :, :], w["same"][:, :, :], rank_all, ALU.mult))
                            step(dve.tensor_reduce(m["pick"][:, :], w["ranked"][:, :, :], AX.X, ALU.max))
                            step(dve.tensor_tensor(w[found][:, :, :], w["ranked"][:, :, :], spread(m["pick"]), ALU.is_equal))
                            if found == "first":
                                step(dve.scalar_tensor_tensor(out=w["rest"][:, :, :], in0=w["first"][:, :, :], scalar=-2.0,
                                                              in1=w["g"][:, :, :], op0=ALU.mult, op1=ALU.add))
                        step(dve.tensor_tensor(w["both"][:, :, :], w["first"][:, :, :], w["second"][:, :, :], ALU.add))
                        step(dve.tensor_tensor(w["kept"][:, :, :], w["both"][:, :, :], w["g"][:, :, :], ALU.mult))
                        step(dve.tensor_reduce(m["msum"][:, :], w["kept"][:, :, :], AX.X, ALU.add))
                        dve.tensor_scalar(m["msum_eps"][:, :], m["msum"][:, :], GATE_EPS, None, ALU.add).then_inc(link[s], 1)
                        count[0] += 1
                        dve.wait_ge(link[s], i * LINKS + count[0])
                        dve.reciprocal(m["minv"][:, :], m["msum_eps"][:, :]).then_inc(inv_ok[s], 1)
                        dve.wait_ge(inv_ok[s], n)
                        dve.tensor_tensor(gate[:, bass.ds((i * NS + s) * GB, GB), :], w["kept"][:, :, :], spread(m["minv"]),
                                          ALU.mult).then_inc(gate_ok[s], 1)
                        assert count[0] == LINKS, count[0]
                for s in range(NS):
                    dve.wait_ge(gate_ok[s], PAIRS)
        signals.clear()


def experts_phase(nc, a, K, out):
    import concourse.bass as bass
    from concourse import mybir
    from contextlib import ExitStack
    f32 = mybir.dt.float32
    ALU, ACT = mybir.AluOpType, mybir.ActivationFunctionType
    NHID = HIDDEN // 128
    with ExitStack() as ctx:
        def sb(name, shape, dt=f32):
            return ctx.enter_context(nc.sbuf_tensor(name, shape, dt))

        signals = Signals(nc, ctx, "moe")
        PS, hT, gate, x3_tok = (K[n] for n in ("PS", "hT", "gate", "x3_tok"))
        w1, w2 = sb("w1", [D, NE, HIDDEN]), sb("w2", [128, NE, NHID, D])
        rms_wT = sb("rms_wT", [D, NE])
        act_out = [sb(f"act_out{k}", [128, NHID, GT]) for k in range(2)]
        gate_now = sb("gate_now", [S, GB, E_ROUTED])
        total = [sb(f"total{k}", [S, GB, D]) for k in range(2)]
        loads = [(w1[:, :, :], a["w1"].rearrange("e d f -> d e f")), (rms_wT[:, :], a["rms_wT"]),
                 (w2[:, :, :, :], a["w2"].rearrange("e (h p) d -> p e h d", p=128))]
        loaded, scaled = signals.take_all("loaded scaled")
        up_raw, silu_ok, down_raw, sum_ok, stored = signals.take_all("up_raw silu_ok down_raw sum_ok stored")
        gates_here = signals.take("gates_here")
        with nc.Block() as block:
            @block.sync
            def _(sp):
                for dst, src in loads:
                    sp.dma_start(dst, src).then_inc(loaded, 16)
                sp.wait_ge(loaded, 16 * len(loads))
                for s in (silu_ok, down_raw, sum_ok):
                    sp.sem_inc(s, 2)

            @block.vector
            def _(dve):
                dve.wait_ge(loaded, 16 * len(loads))
                for e in range(NE):
                    dve.tensor_scalar(w1[:, e, :], w1[:, e, :], rms_wT[:, e:e + 1], None, ALU.mult).then_inc(scaled, 1)
                dve.wait_ge(scaled, NE)

        with nc.Block() as block:
            @block.tensor
            def _(pe):
                def up(g, e):
                    pe.wait_ge(silu_ok, g * NE + (e + 1))
                    for h in range(NHID):
                        mm = pe.matmul(PS[:, 2 * (e % 2) + h, :], w1[:, e, h * 128:(h + 1) * 128], hT[:, bass.ds(g * GT, GT)],
                                       start=True, stop=True)
                    mm.then_inc(up_raw, 1)

                def down(g, e):
                    pe.wait_ge(silu_ok, g * NE + (e + 3))
                    pe.wait_ge(sum_ok, g * NE + (e + 1))
                    for b in range(GB):
                        for h in range(NHID):
                            mm = pe.matmul(PS[:, 4 + e % 2, b * D:(b + 1) * D], act_out[e % 2][:, h, b * S:(b + 1) * S], w2[:, e, h, :],
                                           start=(h == 0), stop=(h == NHID - 1))
                    mm.then_inc(down_raw, 1)

                with pe.Fori(0, NG) as g:
                    up(g, 0)
                    for e in range(1, NE):
                        up(g, e)
                        down(g, e - 1)
                    down(g, NE - 1)

            @block.scalar
            def _(act):
                with act.Fori(0, NG) as g:
                    for e in range(NE):
                        act.wait_ge(up_raw, g * NE + (e + 1))
                        act.wait_ge(down_raw, g * NE + (e + 1))
                        act.activation(act_out[e % 2][:, :, :], PS[:, 2 * (e % 2):2 * (e % 2) + 2, :], ACT.Silu).then_inc(silu_ok, 1)

            @block.vector
            def _(dve):
                with dve.Fori(0, NG) as g:
                    dve.wait_ge(sum_ok, g * NE + 2)
                    dve.tensor_scalar(gate_now[:, :, :], gate[:, bass.ds(g * GB, GB), :], 1.0, None, ALU.mult).then_inc(gates_here, 1)
                    dve.wait_ge(gates_here, g + 1)
                    for e in range(NE):
                        dve.wait_ge(sum_ok, g * NE + (e + 2))
                        dve.wait_ge(down_raw, g * NE + (e + 3))
                        if e < E_ROUTED:
                            for b in range(GB):
                                prior = x3_tok[:, bass.ds(g * GB + b, 1), :].rearrange("p o d -> p (o d)") if e == 0 else total[(e - 1) % 2][:, b, :]
                                ins = dve.scalar_tensor_tensor(out=total[e % 2][:, b, :], in0=PS[:, 4 + e % 2, b * D:(b + 1) * D],
                                                               scalar=gate_now[:, b, e:e + 1], in1=prior, op0=ALU.mult, op1=ALU.add)
                        else:
                            into = x3_tok[:, bass.ds(g * GB, GB), :] if e == NE - 1 else total[e % 2][:, :, :]
                            ins = dve.tensor_tensor(into, PS[:, 4 + e % 2, :].rearrange("p (b d) -> p b d", b=GB),
                                                    total[(e - 1) % 2][:, :, :], ALU.add)
                        ins.then_inc(sum_ok, 1)

            @block.sync
            def _(sp):
                with sp.Fori(0, NG) as g:
                    sp.wait_ge(sum_ok, g * NE + (NE + 2))
                    sp.dma_start(out[bass.ds(g * GB, GB), :, :].rearrange("b s d -> s b d"), x3_tok[:, bass.ds(g * GB, GB), :]).then_inc(stored, 16)
                sp.wait_ge(stored, 16 * NG)
        signals.clear()


def constants_phase(nc, K):
    from concourse import mybir
    from contextlib import ExitStack
    ALU = mybir.AluOpType
    with ExitStack() as ctx:
        signals = Signals(nc, ctx, "constants")
        zeroed, made = signals.take_all("zeroed made")
        with nc.Block() as block:
          @block.gpsimd
          def _(pool):
            pool.memset(K["ident"][:, :], 0.0).then_inc(zeroed, 1)
            pool.memset(K["ones_row"][:, :], 1.0).then_inc(made, 1)
            pool.wait_ge(zeroed, 1)
            pool.affine_select(out=K["ident"][:, :], in_=K["ident"][:, :], compare_op=ALU.not_equal, fill=1.0, base=0,
                               pattern=[[-1, 128]], channel_multiplier=1).then_inc(made, 1)
            pool.wait_ge(made, 2)
        signals.clear()


def build(nc, a, out, stop="all"):
    from concourse import mybir
    from contextlib import ExitStack
    f32 = mybir.dt.float32
    with ExitStack() as ctx:
        def sb(name, shape, dt=f32):
            return ctx.enter_context(nc.sbuf_tensor(name, shape, dt))
        K = {n: a[n] for n in ("xn_d", "bd_d", "c_d", "ad_d")}
        K |= {"PS": ctx.enter_context(nc.psum_tensor("PS", [128, 8, 512], f32)),
             "ident": sb("ident", [128, 128]), "ones_row": sb("ones_row", [1, 128]),
             "cond_tok": sb("cond_tok", [S, B, D])}
        constants_phase(nc, K)
        edge_phase(nc, a, K)
        if stop != "edge":
            K["x3_tok"], K["x3T"] = K["cond_tok"], sb("x3T", [D, B * S])
            attention_phase(nc, a, K)
            if stop != "attention":
                K["gateT"], K["xnT"] = sb("gateT", [128, NH, B * S]), sb("xnT", [128, NH, B * S])
                scan_inputs_phase(nc, a, K)
                scan_phase(nc, a, K)
                K["hT"], K["gate"] = K["x3T"], sb("gate", [S, B, E_ROUTED])
                expert_inputs_phase(nc, a, K)
                experts_phase(nc, a, K, out)
        if stop in ("edge", "attention"):
            with nc.semaphore("dumped") as dumped, nc.Block() as block:
                @block.sync
                def _(sp):
                    sp.dma_start(out.rearrange("b s d -> s b d"), K["cond_tok" if stop == "edge" else "x3_tok"][:, :, :]).then_inc(dumped, 16)
                    sp.wait_ge(dumped, 16)


def kernel(**inputs):
    import numpy as np
    import concourse.bacc as bacc
    from concourse import mybir
    from concourse.bass_utils import run_bass_kernel_spmd

    L = {k.replace("L0_", ""): np.asarray(v) for k, v in inputs.items()}
    x = L["x"].reshape(B * S, D)
    arrays = {
        "xT": x.T, "adj": L["itok_BxSxS_0_4"], "mask": L["mask_BxS_ff1"], "qeT": L["fside_BxS_0"].T,
        "b_qtT": L["mask_BxS_ff0"][:T_ITER].T, "w_qtT": L["fside_BxSxS_0"][:T_ITER].transpose(0, 2, 1),
        "condT": L["cond_2048"].T,
        "w_qinT": L["cond_w_qin"].T, "w_plT": L["cond_w_pl"].T, "w_pcT": L["cond_w_pc"].T, "w_pkT": L["cond_w_pk"].T,
        "w_pvT": L["cond_w_pv"].T, "w_q": L["cond_w_q"], "w_k": L["cond_w_k"], "w_vT": L["cond_w_v"].T,
        "w_muT": L["cond_w_mu"].T, "w_cbT": L["cond_w_cb"].T,
        "bias": np.stack([L["cond_" + n] for n in ("b_qin", "b_pl", "b_pc", "b_q", "b_k", "b_pk", "b_pv", "b_mu")]
                         + [L["cond_init_mem"][0]], axis=1),
        "x": L["x"],
        "w_inT": L["cond2_W_in"].T, "taps": L["cond2_W_conv"][:, 0, :], "b_conv": L["cond2_b_conv"],
        "ln_g": L["cond2_ln_g"], "ln_b": L["cond2_ln_b"], "w_xpT": L["cond2_W_xproj"].T, "w_dtT": L["cond2_W_dt"].T,
        "state_cols": np.stack([L["cond2_b_dt"], L["cond2_A_log"]], axis=1), "D": L["cond2_D"],
        "w_outT": L["cond2_W_out"].T, "router": L["ffn_router_w"],
        "w1": np.concatenate([L["ffn_w1"], L["ffn_w1_s"]]), "w2": np.concatenate([L["ffn_w2"], L["ffn_w2_s"]]),
        "rms_wT": np.concatenate([L["ffn_rms_w"], L["ffn_rms_w_s"]]).T,
        "qkv_KT": np.concatenate([L[f"attn_{n}K"].T for n in "qkv"], axis=1),
        "qkv_V": np.stack([L[f"attn_{n}V"] for n in "qkv"]),
        "p_KT": L["attn_pK"].T, "p_V": L["attn_pV"], "f_KT": L["attn_fK"].T, "f_V": L["attn_fV"],
        "rows": np.stack([L["cond_b_v"], L["cond_b_cb"]]),
    }
    nc = bacc.Bacc("TRN2", target_bir_lowering=False, num_devices=1)
    given, aps = {}, {}
    for name, v in arrays.items():
        v = np.ascontiguousarray(v)
        given[f"in_{name}"] = v
        aps[name] = nc.dram_tensor(f"in_{name}", v.shape, mybir.dt.from_np(v.dtype), kind="ExternalInput").ap()
    out = nc.dram_tensor("out_0", (B, S, D), mybir.dt.float32, kind="ExternalOutput").ap()
    for name, shape in (("xn_d", (B, S, DI)), ("bd_d", (B, S, N_STATE)), ("c_d", (B, N_STATE, S)), ("ad_d", (B, N_STATE, S))):
        aps[name] = nc.dram_tensor(name, shape, mybir.dt.float32, kind="Internal").ap()
    build(nc, aps, out, STOP)
    r = run_bass_kernel_spmd(nc, [given], core_ids=[0])
    return r.results[0]["out_0"]


STOP = "all"
```

```python
import math

B, S, D = 32, 128, 128
T_ITER, TYPES = 4, 4
ALPHA = 0.2
NO_EDGE = -9000000000000000.0
SERIES = 10
LN2_HIGH = 0.693359375
LN2_LOW = math.log(2.0) - LN2_HIGH
EXP_LOW = -60.0
LN_EPS = 1e-5
HEADS = 16
HD = D // HEADS
NF = 512
P_SCALE = float(D) ** -0.5
CAUSAL = -1e30
DI = 256
NH = DI // 128
N_STATE = 16
N_TAPS = 4
CLIP = 10.0
E_ROUTED, E_SHARED, HIDDEN = 14, 2, 256
NE = E_ROUTED + E_SHARED
RMS_EPS = 1.1920929e-07
GATE_EPS = 1e-9
GB = 4
GT = GB * S
NG = B // GB


class Signals:

    def __init__(self, nc, ctx, phase):
        self.nc, self.ctx, self.phase, self.taken = nc, ctx, phase, []

    def take(self, name, n=None):
        got = [self.ctx.enter_context(self.nc.semaphore(f"{self.phase}_{name}{i}")) for i in range(n or 1)]
        self.taken += got
        return got if n else got[0]

    def take_all(self, names, n=None):
        return [self.take(name, n) for name in names.split()]

    def clear(self):
        nums, runs = sorted(s.num for s in self.taken), []
        for k in nums:
            if runs and runs[-1][1] == k:
                runs[-1][1] = k + 1
            else:
                runs.append([k, k + 1])
        with self.nc.Block() as block:
            @block.sync
            def _(sp):
                for low, high in runs:
                    sp.sem_clear(range(low, high))


def edge_phase(nc, a, K):
    import concourse.bass as bass
    from concourse import mybir
    from contextlib import ExitStack
    f32, i32 = mybir.dt.float32, mybir.dt.int32
    ALU, ACT, AX = mybir.AluOpType, mybir.ActivationFunctionType, mybir.AxisListType
    ctx = ExitStack()
    NS = 4
    EB = 2
    ET = EB * S
    TURNS = B // (NS * EB)
    X = [2 * s for s in range(NS)]
    Y = [2 * s + 1 for s in range(NS)]
    with ctx:
        def sb(name, shape, dt=f32):
            return ctx.enter_context(nc.sbuf_tensor(name, shape, dt))

        signals = Signals(nc, ctx, "edge")
        sem = signals.take

        PS = K["PS"]
        ident, ones_row = K["ident"], K["ones_row"]
        xT, adj, mask = sb("xT", [D, B * S]), sb("adj", [S, B, S], i32), sb("mask", [D, B * S])
        w_plT, w_pcT, w_qinT = sb("w_plT", [D, D]), sb("w_pcT", [D, D]), sb("w_qinT", [D, D])
        w_pkT, w_pvT = sb("w_pkT", [D, D]), sb("w_pvT", [D, D])
        w_q, w_k, w_vT = sb("w_q", [D, 3 * D]), sb("w_k", [D, 3 * D]), sb("w_vT", [D, 3, D])
        w_muT, w_cbT = sb("w_muT", [D, 2, D]), sb("w_cbT", [D, 2, D])
        w_qtT, qeT = sb("w_qtT", [D, T_ITER, D]), sb("qeT", [D, B])
        b_qtT, wesT = sb("b_qtT", [D, T_ITER]), sb("wesT", [D, 2, B])
        bias = sb("bias", [D, 10])
        rows = sb("rows", [1, D])
        b_qin, b_pl, b_pc, b_q, b_k, b_pk, b_pv, b_mu, init, b_v = (bias[:, n:n + 1] for n in range(10))
        b_cb = rows[0:1, :]
        q_lin, q_neg, q_exp, q_pos, q_base, q_round, q_rest = (
            sb(n, [D, B]) for n in ("q_lin", "q_neg", "q_exp", "q_pos", "q_base", "q_round", "q_rest"))
        q_int = sb("q_int", [D, B], i32)
        cmd, pk, pv = (sb(n, [D, T_ITER, B]) for n in ("cmd", "pk", "pv"))
        w2pk = sb("w2pk", [D, T_ITER * B, TYPES])
        edge_w = sb("edge_w", [D, 3, T_ITER * B, 2 * TYPES])
        edge_b = sb("edge_b", [S, T_ITER * B, 2 * TYPES])
        def per(name, shape):
            return [sb(f"{name}{s}", shape) for s in range(NS)]

        xg, plT, mT, xcT, xctxT, msgT = (per(n, [D, ET]) for n in ("xg", "plT", "mT", "xcT", "xctxT", "msgT"))
        is_type, scored = per("is_type", [S, EB, TYPES, S]), per("scored", [S, EB, TYPES, S])
        lifted, half = per("lifted", [S, EB, 2, S]), per("half", [S, EB, 2, S])
        no_edge, edge, logit, prob, probT = (per(n, [S, EB, S]) for n in ("no_edge", "edge", "logit", "prob", "probT"))
        v_tok, ac = per("v_tok", [S, EB, D]), per("ac", [S, EB, 2 * TYPES])
        neg_max, row_sum, inv_sum = (per(n, [S, EB]) for n in ("neg_max", "row_sum", "inv_sum"))
        cond_tok = K["cond_tok"]

        loads = [(w_qinT[:, :], a["w_qinT"]), (qeT[:, :], a["qeT"]), (bias[:, :], a["bias"]),
                 (w_qtT[:, :, :], a["w_qtT"].rearrange("t i o -> i t o")), (b_qtT[:, :], a["b_qtT"]),
                 (w_pkT[:, :], a["w_pkT"]), (w_pvT[:, :], a["w_pvT"]),
                 (wesT[:, :, :], a["condT"].rearrange("(h p) b -> p h b", p=D)),
                 (w_q[:, :], a["w_q"]), (w_k[:, :], a["w_k"]),
                 (rows[0:1, :], a["b_cb"].rearrange("(o d) -> o d", o=1))]
        loads2 = [(xT[:, :], a["xT"]), (adj[:, :, :], a["adj"].rearrange("b i j -> i b j")),
                  (mask[:, :], a["mask"].rearrange("(o b) s -> o (b s)", o=1).partition_broadcast(D)),
                  (w_plT[:, :], a["w_plT"]), (w_pcT[:, :], a["w_pcT"]),
                  (w_vT[:, :, :], a["w_vT"].rearrange("(c p) o -> p c o", p=D)),
                  (w_muT[:, :, :], a["w_muT"].rearrange("(c p) o -> p c o", p=D)),
                  (w_cbT[:, :, :], a["w_cbT"].rearrange("(c p) o -> p c o", p=D))]

        small_in, big_in = sem("small_in"), sem("big_in")
        q_lin_raw, q_lin_ok, q_step, q_ok = (sem(n) for n in ("q_lin_raw", "q_lin_ok", "q_step", "q_ok"))
        cmd_raw, cmd_ok, pkv_raw, pkv_ok, w2pk_ok, tab_raw, tab_ok = (
            sem(n) for n in ("cmd_raw", "cmd_ok", "pkv_raw", "pkv_ok", "w2pk_ok", "tab_raw", "tab_ok"))

        xc_ok = sem("xc_ok")

        with nc.Block() as block:
            @block.sync
            def _(sp):
                for dst, src in loads:
                    sp.dma_start(dst, src).then_inc(small_in, 16)
                for dst, src in loads2:
                    sp.dma_start(dst, src).then_inc(big_in, 16)
                sp.wait_ge(small_in, 16 * len(loads))
                sp.wait_ge(big_in, 16 * len(loads2))

            @block.tensor
            def _(pe):
                pe.wait_ge(small_in, 16 * len(loads))
                pe.matmul(PS[:, 0, 0:B], w_qinT[:, :], qeT[:, :], start=True, stop=True).then_inc(q_lin_raw, 1)
                pe.wait_ge(q_ok, 1)
                for t in range(T_ITER):
                    mm = pe.matmul(PS[:, 1, t * B:(t + 1) * B], w_qtT[:, t, :], q_base[:, :], start=True, stop=True)
                mm.then_inc(cmd_raw, 1)
                pe.wait_ge(cmd_ok, 1)
                pe.matmul(PS[:, 2, 0:T_ITER * B], w_pkT[:, :], cmd[:, :, :], start=True, stop=True)
                pe.matmul(PS[:, 3, 0:T_ITER * B], w_pvT[:, :], cmd[:, :, :], start=True, stop=True).then_inc(pkv_raw, 1)
                pe.wait_ge(w2pk_ok, 1)
                for c in range(3):
                    pe.matmul(PS[:, 4 + c, :], w_k[:, c * D:(c + 1) * D], w2pk[:, :, :], start=True, stop=True)
                    pe.matmul(PS[:, 0, c * TYPES:(c + 1) * TYPES], w_q[:, c * D:(c + 1) * D], wesT[:, 0, 0:TYPES],
                              start=True, stop=True)
                pe.matmul(PS[:, 7, :], b_k.to_broadcast([D, S]), w2pk[:, :, :], start=True, stop=True)
                pe.matmul(PS[:, 1, 0:TYPES], b_q.to_broadcast([D, S]), wesT[:, 0, 0:TYPES], start=True, stop=True).then_inc(tab_raw, 1)

            @block.vector
            def _(dve):
                dve.wait_ge(small_in, 16 * len(loads))
                dve.wait_ge(q_lin_raw, 1)
                dve.tensor_scalar(q_lin[:, :], PS[:, 0, 0:B], b_qin, None, ALU.add).then_inc(q_lin_ok, 1)
                dve.wait_ge(q_lin_ok, 1)
                done = 0

                def step(ins):
                    nonlocal done
                    done += 1
                    ins.then_inc(q_step, 1)
                    dve.wait_ge(q_step, done)

                step(dve.tensor_scalar(q_pos[:, :], q_lin[:, :], 0.0, None, ALU.max))
                step(dve.tensor_scalar(q_neg[:, :], q_lin[:, :], 0.0, EXP_LOW, ALU.min, ALU.max))
                step(dve.tensor_scalar(q_int[:, :], q_neg[:, :], 1.0 / math.log(2.0), None, ALU.mult))
                step(dve.tensor_copy(q_round[:, :], q_int[:, :]))
                step(dve.scalar_tensor_tensor(out=q_rest[:, :], in0=q_round[:, :], scalar=-LN2_HIGH, in1=q_neg[:, :],
                                              op0=ALU.mult, op1=ALU.add))
                step(dve.scalar_tensor_tensor(out=q_rest[:, :], in0=q_round[:, :], scalar=-LN2_LOW, in1=q_rest[:, :],
                                              op0=ALU.mult, op1=ALU.add))
                step(dve.tensor_scalar(q_exp[:, :], q_rest[:, :], 1.0 / math.factorial(SERIES), None, ALU.mult))
                for k in range(SERIES - 1, 0, -1):
                    step(dve.scalar_tensor_tensor(out=q_exp[:, :], in0=q_exp[:, :], scalar=1.0 / math.factorial(k),
                                                  in1=q_rest[:, :], op0=ALU.add, op1=ALU.mult))
                step(dve.tensor_scalar(q_int[:, :], q_round[:, :], 127.0, float(2 ** 23), ALU.add, ALU.mult))
                two_k = q_int[:, :].bitcast(f32)
                step(dve.tensor_tensor(q_exp[:, :], q_exp[:, :], two_k, ALU.mult))
                step(dve.scalar_tensor_tensor(out=q_pos[:, :], in0=two_k, scalar=-1.0, in1=q_pos[:, :], op0=ALU.add, op1=ALU.add))
                dve.tensor_tensor(q_base[:, :], q_exp[:, :], q_pos[:, :], ALU.add).then_inc(q_ok, 1)
                dve.wait_ge(cmd_raw, 1)
                dve.tensor_tensor(cmd[:, :, :], PS[:, 1, 0:T_ITER * B].rearrange("p (t b) -> p t b", t=T_ITER),
                                  b_qtT[:, :].unsqueeze(2).to_broadcast([D, T_ITER, B]), ALU.add).then_inc(cmd_ok, 1)
                dve.wait_ge(pkv_raw, 1)
                dve.tensor_scalar(pk[:, :, :], PS[:, 2, 0:T_ITER * B], b_pk, None, ALU.add).then_inc(pkv_ok, 1)
                dve.tensor_scalar(pv[:, :, :], PS[:, 3, 0:T_ITER * B], b_pv, None, ALU.add).then_inc(pkv_ok, 1)
                dve.wait_ge(pkv_ok, 2)
                dve.tensor_tensor(w2pk[:, :, :], pk[:, :, :].rearrange("p t b -> p (t b)").unsqueeze(2)
                                  .to_broadcast([D, T_ITER * B, TYPES]),
                                  wesT[:, 1:2, 0:TYPES].to_broadcast([D, T_ITER * B, TYPES]), ALU.mult).then_inc(w2pk_ok, 1)
                dve.wait_ge(tab_raw, 1)
                for c in range(3):
                    dve.tensor_copy(edge_w[:, c, :, TYPES:2 * TYPES],
                                    PS[:, 4 + c, :].rearrange("p (n m) -> p n m", m=TYPES)).then_inc(tab_ok, 1)
                    dve.tensor_copy(edge_w[:, c, :, 0:TYPES],
                                    PS[:, 0:1, c * TYPES:(c + 1) * TYPES].to_broadcast([D, T_ITER * B, TYPES])).then_inc(tab_ok, 1)
                dve.tensor_copy(edge_b[:, :, TYPES:2 * TYPES],
                                PS[:, 7, :].rearrange("p (n m) -> p n m", m=TYPES)).then_inc(tab_ok, 1)
                dve.tensor_copy(edge_b[:, :, 0:TYPES],
                                PS[:, 1:2, 0:TYPES].to_broadcast([S, T_ITER * B, TYPES])).then_inc(tab_ok, 1)
                dve.wait_ge(tab_ok, 8)
                dve.sem_inc(xc_ok, NS)

        (x_ok, pl_raw, pl_ok, types_ok, combined_raw, group_done, pc_raw, m_ok, v_raw, v_ok, ac_ok, c_raw, lifted_ok,
         late_ok, early_ok, half_ok, edge_ok, open_ok, relu_ok, max_ok, exp_ok, inv_ok, prob_ok, probT_raw, probT_ok,
         msg_raw, msg_ok, mu_raw, xctx_ok) = signals.take_all(
            "x_ok pl_raw pl_ok types_ok combined_raw group_done pc_raw m_ok v_raw v_ok ac_ok c_raw lifted_ok "
            "late_ok early_ok half_ok edge_ok open_ok relu_ok max_ok exp_ok inv_ok prob_ok probT_raw probT_ok "
            "msg_raw msg_ok mu_raw xctx_ok")

        def turn(i, s):
            return i * NS + (s + 1)

        def xc_count(i, s, t):
            return i * ((T_ITER + 1) * NS) + t * NS + (NS + s + 1)

        def round_(i, t, s):
            return i * (T_ITER * NS) + t * NS + (s + 1)

        EARLY, LATE = (0, 1), (2, 3)

        with nc.Block() as block:
            @block.tensor
            def _(pe):
                def head(i, t, pair):
                    for s in pair:
                        pe.wait_ge(xc_ok, xc_count(i, s, t))
                        pe.matmul(PS[:, Y[s], ET:2 * ET], w_pcT[:, :], xcT[s][:, :], start=True, stop=True).then_inc(pc_raw, 1)
                    for s in pair:
                        pe.wait_ge(m_ok, round_(i, t, s))
                        joint = [xg[s], xcT[s], mT[s]]
                        for b in range(EB):
                            at = t * B + i * (NS * EB) + (s * EB + b)
                            v_ps, ac_ps = PS[:, X[s], b * D:(b + 1) * D], PS[:, Y[s], b * 2 * TYPES:(b + 1) * 2 * TYPES]
                            for c in range(3):
                                pe.matmul(v_ps, joint[c][:, b * S:(b + 1) * S], w_vT[:, c, :], start=(c == 0), stop=(c == 2))
                            for c in range(3):
                                mm = pe.matmul(ac_ps, joint[c][:, b * S:(b + 1) * S], edge_w[:, c, bass.ds(at, 1), :],
                                               start=(c == 0), stop=(c == 2))
                        mm.then_inc(v_raw, 1)
                    for s in pair:
                        pe.wait_ge(ac_ok, round_(i, t, s))
                        pe.wait_ge(v_ok, round_(i, t, s))
                        for b in range(EB):
                            for m in range(TYPES):
                                mm = pe.transpose(PS[:, (X, Y)[m // 2][s], (b * 2 + m % 2) * S:(b * 2 + m % 2 + 1) * S],
                                                  ac[s][:, b, TYPES + m:TYPES + m + 1].to_broadcast([S, S]), ident[:, :])
                        mm.then_inc(c_raw, 1)

                def tail(i, t, pair):
                    for s in pair:
                        pe.wait_ge(prob_ok, round_(i, t, s))
                        for b in range(EB):
                            mm = pe.transpose(PS[:, X[s], b * S:(b + 1) * S], prob[s][:, b, :], ident[:, :])
                        mm.then_inc(probT_raw, 1)
                    for s in pair:
                        pe.wait_ge(probT_ok, round_(i, t, s))
                        for b in range(EB):
                            mm = pe.matmul(PS[:, Y[s], b * S:(b + 1) * S], v_tok[s][:, b, :], probT[s][:, b, :],
                                           start=True, stop=True)
                        mm.then_inc(msg_raw, 1)
                        pe.matmul(PS[:, X[s], ET:2 * ET], w_muT[:, 0, :], xcT[s][:, :], start=True, stop=False)
                    for s in pair:
                        pe.wait_ge(msg_ok, round_(i, t, s))
                        pe.matmul(PS[:, X[s], ET:2 * ET], w_muT[:, 1, :], msgT[s][:, :], start=False, stop=True).then_inc(mu_raw, 1)

                with pe.Fori(0, TURNS) as i:
                    for s in range(NS):
                        pe.wait_ge(x_ok, turn(i, s))
                        pe.matmul(PS[:, X[s], 0:ET], w_plT[:, :], xg[s][:, :], start=True, stop=True).then_inc(pl_raw, 1)
                    head(i, 0, EARLY)
                    head(i, 0, LATE)
                    with pe.Fori(1, T_ITER) as t:
                        for pair in (EARLY, LATE):
                            tail(i, t - 1, pair)
                            head(i, t, pair)
                    for pair in (EARLY, LATE):
                        tail(i, T_ITER - 1, pair)
                    for s in range(NS):
                        pe.wait_ge(xctx_ok, turn(i, s))
                        for b in range(EB):
                            out = PS[:, Y[s], b * D:(b + 1) * D]
                            pe.matmul(out, ones_row[0:1, :], b_cb, start=True, stop=False)
                            pe.matmul(out, xg[s][:, b * S:(b + 1) * S], w_cbT[:, 0, :], start=False, stop=False)
                            mm = pe.matmul(out, xctxT[s][:, b * S:(b + 1) * S], w_cbT[:, 1, :], start=False, stop=True)
                        mm.then_inc(combined_raw, 1)

            @block.scalar
            def _(act):
                def keep_v(i, t, s):
                    act.wait_ge(v_raw, round_(i, t, s))
                    act.activation(v_tok[s][:, :, :], PS[:, X[s], 0:ET], ACT.Copy).then_inc(v_ok, 1)

                def lift(i, t, s):
                    act.wait_ge(c_raw, round_(i, t, s))
                    for b in range(EB):
                        for m in range(2):
                            ins = act.activation(lifted[s][:, b, m, :], PS[:, X[s], (b * 2 + m) * S:(b * 2 + m + 1) * S],
                                                 ACT.Identity, bias=ac[s][:, b, m:m + 1])
                    ins.then_inc(lifted_ok, 1)

                def exp(i, t, s):
                    act.wait_ge(max_ok, round_(i, t, s))
                    for b in range(EB):
                        ins = act.activation(prob[s][:, b, :], logit[s][:, b, :], ACT.Exp,
                                             bias=neg_max[s][:, b:b + 1], accum_out=row_sum[s][:, b:b + 1])
                    ins.then_inc(exp_ok, 1)

                def keep_probT(i, t, s):
                    act.wait_ge(probT_raw, round_(i, t, s))
                    act.activation(probT[s][:, :, :], PS[:, X[s], 0:ET], ACT.Copy).then_inc(probT_ok, 1)

                def beside(i, t_scores, scores, t, other):
                    for s in scores[:1]:
                        lift(i, t_scores, s)
                    for s in other:
                        keep_probT(i, t - 1, s)
                    for s in scores[1:]:
                        lift(i, t_scores, s)
                    for s, o in zip(scores, other):
                        exp(i, t_scores, s)
                        keep_v(i, t, o)

                with act.Fori(0, TURNS) as i:
                    for s in range(NS):
                        act.activation(xg[s][:, :], xT[:, bass.ds((i * NS + s) * ET, ET)], ACT.Copy).then_inc(x_ok, 1)
                    for s in EARLY:
                        keep_v(i, 0, s)
                    for s in EARLY:
                        lift(i, 0, s)
                    for s, o in zip(EARLY, LATE):
                        exp(i, 0, s)
                        keep_v(i, 0, o)
                    with act.Fori(1, T_ITER) as t:
                        beside(i, t - 1, LATE, t, EARLY)
                        beside(i, t, EARLY, t, LATE)
                    for s in LATE:
                        lift(i, T_ITER - 1, s)
                    for s in EARLY:
                        keep_probT(i, T_ITER - 1, s)
                    for s in LATE:
                        exp(i, T_ITER - 1, s)
                    for s in LATE:
                        keep_probT(i, T_ITER - 1, s)
                    for s in range(NS):
                        act.wait_ge(xc_ok, xc_count(i, s, T_ITER))
                        act.activation(xctxT[s][:, :], PS[:, X[s], ET:2 * ET], ACT.Identity, bias=b_mu).then_inc(xctx_ok, 1)
                    for s in range(NS):
                        act.wait_ge(combined_raw, turn(i, s))
                        act.activation(cond_tok[:, bass.ds((i * NS + s) * EB, EB), :],
                                       PS[:, Y[s], 0:ET].rearrange("p (b d) -> p b d", b=EB), ACT.Copy).then_inc(group_done, 1)
                act.wait_ge(group_done, TURNS * NS)

            @block.gpsimd
            def _(pool):
                def add_up(i, t, pair):
                    for s in pair:
                        pool.wait_ge(types_ok, (i + 1) * (NS * (TYPES + 1)))
                        pool.wait_ge(lifted_ok, round_(i, t, s))
                        pool.tensor_tensor(scored[s][:, :, 0:2, :], lifted[s][:, :, :, :], is_type[s][:, :, 0:2, :], ALU.mult)\
                            .then_inc(early_ok, 1)
                        pool.wait_ge(early_ok, round_(i, t, s))
                        pool.wait_ge(late_ok, round_(i, t, s))
                        pool.tensor_tensor(half[s][:, :, :, :], scored[s][:, :, 0:2, :], scored[s][:, :, 2:4, :], ALU.add).then_inc(half_ok, 1)
                        pool.wait_ge(half_ok, round_(i, t, s))
                        pool.tensor_tensor(edge[s][:, :, :], half[s][:, :, 0, :], half[s][:, :, 1, :], ALU.add).then_inc(edge_ok, 1)

                with pool.Fori(0, TURNS) as i:
                    add_up(i, 0, EARLY)
                    with pool.Fori(1, T_ITER) as t:
                        add_up(i, t - 1, LATE)
                        add_up(i, t, EARLY)
                    add_up(i, T_ITER - 1, LATE)

            @block.vector
            def _(dve):
                def multiply(i, t, s):
                    dve.wait_ge(pl_ok, turn(i, s))
                    dve.wait_ge(types_ok, (i + 1) * (NS * (TYPES + 1)))
                    dve.wait_ge(pc_raw, round_(i, t, s))
                    dve.scalar_tensor_tensor(out=mT[s][:, :], in0=PS[:, Y[s], ET:2 * ET], scalar=b_pc, in1=plT[s][:, :],
                                             op0=ALU.add, op1=ALU.mult).then_inc(m_ok, 1)

                def keep_ac(i, t, s):
                    dve.wait_ge(v_raw, round_(i, t, s))
                    dve.tensor_tensor(ac[s][:, :, :], PS[:, Y[s], 0:EB * 2 * TYPES].rearrange("p (b m) -> p b m", b=EB),
                                      edge_b[:, bass.ds(t * B + i * (NS * EB) + s * EB, EB), :], ALU.add).then_inc(ac_ok, 1)

                def late_types(i, t, s):
                    dve.wait_ge(ac_ok, round_(i, t, s))
                    dve.wait_ge(c_raw, round_(i, t, s))
                    for b in range(EB):
                        for m in (2, 3):
                            ins = dve.scalar_tensor_tensor(
                                out=scored[s][:, b, m, :], in0=PS[:, Y[s], (b * 2 + m - 2) * S:(b * 2 + m - 1) * S],
                                scalar=ac[s][:, b, m:m + 1], in1=is_type[s][:, b, m, :], op0=ALU.add, op1=ALU.mult)
                    ins.then_inc(late_ok, 1)

                def to_max(i, t, s):
                    dve.wait_ge(edge_ok, round_(i, t, s))
                    dve.scalar_tensor_tensor(out=logit[s][:, :, :], in0=edge[s][:, :, :], scalar=ALPHA, in1=edge[s][:, :, :],
                                             op0=ALU.mult, op1=ALU.max).then_inc(relu_ok, 1)
                    dve.wait_ge(relu_ok, round_(i, t, s))
                    dve.tensor_tensor(logit[s][:, :, :], logit[s][:, :, :], no_edge[s][:, :, :], ALU.add).then_inc(open_ok, 1)
                    dve.wait_ge(open_ok, round_(i, t, s))
                    dve.tensor_reduce(neg_max[s][:, :], logit[s][:, :, :], AX.X, ALU.max, negate=True).then_inc(max_ok, 1)

                def to_prob(i, t, s):
                    dve.wait_ge(exp_ok, round_(i, t, s))
                    dve.reciprocal(inv_sum[s][:, :], row_sum[s][:, :]).then_inc(inv_ok, 1)
                    dve.wait_ge(inv_ok, round_(i, t, s))
                    dve.tensor_tensor(prob[s][:, :, :], prob[s][:, :, :],
                                      inv_sum[s][:, :].unsqueeze(2).to_broadcast([S, EB, S]), ALU.mult).then_inc(prob_ok, 1)

                def update(i, t, pair):
                    for s in pair:
                        dve.wait_ge(msg_raw, round_(i, t, s))
                        dve.scalar_tensor_tensor(out=msgT[s][:, :].rearrange("p (b j) -> p b j", b=EB),
                                                 in0=PS[:, Y[s], 0:ET].rearrange("p (b j) -> p b j", b=EB), scalar=b_v,
                                                 in1=pv[:, bass.ds(t, 1), bass.ds(i * (NS * EB) + s * EB, EB)]
                                                 .rearrange("p o b -> p (o b)").unsqueeze(2).to_broadcast([D, EB, S]),
                                                 op0=ALU.add, op1=ALU.mult).then_inc(msg_ok, 1)
                    for s in pair:
                        dve.wait_ge(mu_raw, round_(i, t, s))
                        dve.scalar_tensor_tensor(out=xcT[s][:, :], in0=PS[:, X[s], ET:2 * ET], scalar=b_mu,
                                                 in1=mask[:, bass.ds((i * NS + s) * ET, ET)], op0=ALU.add, op1=ALU.mult).then_inc(xc_ok, 1)

                def beside(i, t_scores, scores, t, other, first=False):
                    for s in scores:
                        late_types(i, t_scores, s)
                    if not first:
                        update(i, t - 1, other)
                    for s in other:
                        multiply(i, t, s)
                    for s in scores:
                        to_max(i, t_scores, s)
                    for s, o in zip(scores, other):
                        keep_ac(i, t, o)
                        to_prob(i, t_scores, s)

                with dve.Fori(0, TURNS) as i:
                    for s in range(NS):
                        g = i * NS + s
                        for m in range(TYPES):
                            dve.tensor_scalar(is_type[s][:, :, m, :], adj[:, bass.ds(g * EB, EB), :], float(m + 1), None,
                                              ALU.is_equal).then_inc(types_ok, 1)
                        dve.tensor_scalar(no_edge[s][:, :, :], adj[:, bass.ds(g * EB, EB), :], 0.0, NO_EDGE,
                                          ALU.is_le, ALU.mult).then_inc(types_ok, 1)
                        dve.wait_ge(xc_ok, xc_count(i, s, 0) - NS)
                        dve.tensor_scalar(xcT[s][:, :], mask[:, bass.ds(g * ET, ET)], init, None, ALU.mult).then_inc(xc_ok, 1)
                    for s in range(NS):
                        dve.wait_ge(pl_raw, turn(i, s))
                        dve.tensor_scalar(plT[s][:, :], PS[:, X[s], 0:ET], b_pl, None, ALU.add).then_inc(pl_ok, 1)
                    for s in EARLY:
                        multiply(i, 0, s)
                    for s in EARLY:
                        keep_ac(i, 0, s)
                    beside(i, 0, EARLY, 0, LATE, first=True)
                    with dve.Fori(1, T_ITER) as t:
                        beside(i, t - 1, LATE, t, EARLY)
                        beside(i, t, EARLY, t, LATE)
                    for s in LATE:
                        late_types(i, T_ITER - 1, s)
                    update(i, T_ITER - 1, EARLY)
                    for s in LATE:
                        to_max(i, T_ITER - 1, s)
                    for s in LATE:
                        to_prob(i, T_ITER - 1, s)
                    update(i, T_ITER - 1, LATE)
        signals.clear()



def attention_phase(nc, a, K):
    import concourse.bass as bass
    from concourse import mybir
    from contextlib import ExitStack
    f32, bf16 = mybir.dt.float32, mybir.dt.bfloat16
    ALU, ACT, AX = mybir.AluOpType, mybir.ActivationFunctionType, mybir.AxisListType
    NS = 4
    TURNS = B // NS
    QUADS = HEADS // 4
    WIDE = HEADS * HD
    X = [2 * s for s in range(NS)]
    Y = [2 * s + 1 for s in range(NS)]
    with ExitStack() as ctx:
        def sb(name, shape, dt=f32):
            return ctx.enter_context(nc.sbuf_tensor(name, shape, dt))

        def per(name, shape):
            return [sb(f"{name}{s}", shape) for s in range(NS)]

        signals = Signals(nc, ctx, "attn")

        PS, ident, cond_tok, x3_tok, x3T = (K[n] for n in ("PS", "ident", "cond_tok", "x3_tok", "x3T"))
        x_tok = sb("x_tok", [S, B, D])
        qkv_KT, qkv_V = sb("qkv_KT", [D, 3 * D]), sb("qkv_V", [D, 3, D])
        p_KT, p_V = sb("p_KT", [D, D]), sb("p_V", [D, D])
        f_KT, f_V = sb("f_KT", [D, NF]), sb("f_V", [D, NF // 128, D])
        causal = sb("causal", [S, S])
        causal_bf, ident_bf = sb("causal_bf", [S, S], bf16), sb("ident_bf", [S, S], bf16)
        head16, head4, quad_rows = sb("head16", [D, HEADS]), sb("head4", [D, 4]), sb("quad_rows", [D, QUADS])
        minus_half = sb("minus_half", [S, NS])
        stats, mv = sb("stats", [S, NS, 6]), sb("mv", [S, NS, 2])
        veps, rstd = sb("veps", [S, NS]), sb("rstd", [S, NS])
        stats2, mv2, veps2, rstd2 = per("stats2", [S, 6]), per("mv2", [S, 2]), per("veps2", [S, 1]), per("rstd2", [S, 1])
        h, hT, h2, h2T = per("h", [S, D]), per("hT", [D, S]), per("h2", [S, D]), per("h2T", [D, S])
        qkv_nmax, qkv_sum, qkv_inv = (per(n, [S, 3]) for n in ("qkv_nmax", "qkv_sum", "qkv_inv"))
        q_rows, k_heads = per("q_rows", [D, QUADS, S]), per("k_heads", [D, 4, S])
        v_wide = per("v_wide", [S, HEADS * WIDE + WIDE])
        weight, head_nmax, weightT = per("weight", [S, HEADS, S]), per("head_nmax", [S, HEADS]), per("weightT", [S, HEADS, S])
        head_sum, head_inv, inv_rows, oT = per("head_sum", [S, HEADS]), per("head_inv", [S, HEADS, HD]), per("inv_rows", [D, S]), per("oT", [D, S])
        p_nmax, p_sum, p_inv = (per(n, [S, 1]) for n in ("p_nmax", "p_sum", "p_inv"))
        p_a, p_aT, x1 = per("p_a", [S, D]), per("p_aT", [D, S]), per("x1", [S, D])
        f_nmax, f_sum, f_inv = (per(n, [S, 1]) for n in ("f_nmax", "f_sum", "f_inv"))
        x2, x3 = per("x2", [S, D]), per("x3", [S, D])
        qkv_a, qkv_aT = [w[:, 0:3, :] for w in weight], [w[:, 0:3, :] for w in weightT]
        f_a, f_aT = [w[:, 4:8, :].rearrange("p j n -> p (j n)") for w in weight], [w[:, 4:8, :] for w in weightT]

        loads = [(x_tok[:, :, :], a["x"].rearrange("b s d -> s b d")), (qkv_KT[:, :], a["qkv_KT"]),
                 (qkv_V[:, :, :], a["qkv_V"].rearrange("j n c -> n j c")), (p_KT[:, :], a["p_KT"]),
                 (p_V[:, :], a["p_V"]), (f_KT[:, :], a["f_KT"]),
                 (f_V[:, :, :], a["f_V"].rearrange("(j n) c -> n j c", n=D))]
        loaded, filled, cut, made = signals.take_all("loaded filled cut made")

        with nc.Block() as block:
            @block.sync
            def _(sp):
                for dst, src in loads:
                    sp.dma_start(dst, src).then_inc(loaded, 16)
                sp.wait_ge(loaded, 16 * len(loads))

            @block.gpsimd
            def _(pool):
                pool.memset(causal[:, :], 0.0).then_inc(filled, 1)
                pool.memset(head16[:, :], float(HD) ** -0.5).then_inc(filled, 1)
                pool.memset(quad_rows[:, :], 1.0).then_inc(filled, 1)
                pool.memset(minus_half[:, :], -0.5).then_inc(filled, 1)
                for s in range(NS):
                    pool.memset(v_wide[s][:, :], 0.0).then_inc(filled, 1)
                pool.wait_ge(filled, 4 + NS)
                pool.affine_select(out=causal[:, :], in_=causal[:, :], compare_op=ALU.is_ge, fill=CAUSAL, base=0,
                                   pattern=[[-1, S]], channel_multiplier=1).then_inc(cut, 1)
                for t, width, n in ((head16, HD, HEADS), (quad_rows, 4 * HD, QUADS)):
                    pool.affine_select(out=t[:, :], in_=t[:, :], compare_op=ALU.is_ge, fill=0.0, base=0,
                                       pattern=[[-width, n]], channel_multiplier=1).then_inc(cut, 1)
                pool.wait_ge(cut, 3)
                for t, width, n in ((head16, HD, HEADS), (quad_rows, 4 * HD, QUADS)):
                    pool.affine_select(out=t[:, :], in_=t[:, :], compare_op=ALU.is_ge, fill=0.0, base=width - 1,
                                       pattern=[[width, n]], channel_multiplier=-1).then_inc(cut, 1)

            @block.vector
            def _(dve):
                dve.wait_ge(cut, 5)
                dve.tensor_reduce(head4[:, :], head16[:, :].rearrange("p (r j) -> p j r", j=4), AX.X, ALU.add).then_inc(made, 1)
                dve.tensor_copy(causal_bf[:, :], causal[:, :]).then_inc(made, 1)
                dve.tensor_copy(ident_bf[:, :], ident[:, :]).then_inc(made, 1)
                dve.wait_ge(loaded, 16 * len(loads))
                for t in (qkv_KT, p_KT, f_KT):
                    dve.tensor_scalar(t[:, :], t[:, :], P_SCALE, None, ALU.mult).then_inc(made, 1)
                dve.wait_ge(made, 6)

        (st_ok, st_seen, mv_ok, veps_ok, rstd_ok, h_ok, hT_raw, hT_ok, qkv_raw, qkv_nmax_ok, qkv_exp, qkv_inv_ok,
         qkv_a_ok, qkv_aT_raw, qkv_aT_ok, proj_raw, v_ok, qk_ok, score_raw, hmax_ok, hexp_ok, hinv_ok,
         wT_raw, wT_even, wT_odd, inv_raw, inv_ok, o_raw, oT_ok) = signals.take_all(
            "a_st_ok a_st_seen a_mv_ok a_veps_ok a_rstd_ok a_h_ok hT_raw hT_ok qkv_raw qkv_nmax_ok qkv_exp qkv_inv_ok "
            "qkv_a_ok qkv_aT_raw qkv_aT_ok proj_raw v_ok qk_ok score_raw hmax_ok hexp_ok hinv_ok "
            "wT_raw wT_even wT_odd inv_raw inv_ok o_raw oT_ok")
        (p_raw, p_nmax_ok, p_exp, p_aT_raw, p_aT_ok, p_out_raw, p_inv_ok, x1_ok,
         f_st_ok, f_st_seen, f_mv_ok, f_veps_ok, f_rstd_ok, h2_ok, h2T_raw, h2T_ok, f_raw, f_nmax_ok, f_exp, f_aT_raw,
         f_aT_ok, f_out_raw, f_inv_ok, x2_ok, x3_ok, x3T_raw, stored) = signals.take_all(
            "p_raw p_nmax_ok p_exp p_aT_raw p_aT_ok p_out_raw p_inv_ok x1_ok "
            "f_st_ok f_st_seen f_mv_ok f_veps_ok f_rstd_ok h2_ok h2T_raw h2T_ok f_raw f_nmax_ok f_exp f_aT_raw "
            "f_aT_ok f_out_raw f_inv_ok x2_ok x3_ok x3T_raw x3_stored")

        def count(i, s, part=0, parts=1):
            return i * (parts * NS) + (part * NS + s + 1)

        with nc.Block() as block:
            @block.gpsimd
            def _(pool):
                with pool.Fori(0, TURNS) as i:
                    pool.wait_ge(veps_ok, i + 1)
                    pool.tensor_tensor(rstd[:, :], veps[:, :], minus_half[:, :], ALU.pow).then_inc(rstd_ok, 1)
                    for s in range(NS):
                        pool.wait_ge(f_veps_ok, count(i, s))
                        pool.tensor_tensor(rstd2[s][:, :], veps2[s][:, :], minus_half[:, 0:1], ALU.pow).then_inc(f_rstd_ok, 1)

            @block.tensor
            def _(pe):
                with pe.Fori(0, TURNS) as i:
                    for s in range(NS):
                        pe.wait_ge(h_ok, count(i, s))
                        pe.transpose(PS[:, X[s], 0:S], h[s][:, :], ident[:, :]).then_inc(hT_raw, 1)
                    for s in range(NS):
                        pe.wait_ge(hT_ok, count(i, s))
                        pe.matmul(PS[:, Y[s], 0:3 * D], hT[s][:, :], qkv_KT[:, :], start=True, stop=True).then_inc(qkv_raw, 1)
                    for s in range(NS):
                        pe.wait_ge(qkv_a_ok, count(i, s))
                        for j in range(3):
                            mm = pe.transpose(PS[:, X[s], j * S:(j + 1) * S], qkv_a[s][:, j, :], ident[:, :])
                        mm.then_inc(qkv_aT_raw, 1)
                    for s in range(NS):
                        pe.wait_ge(qkv_aT_ok, count(i, s))
                        pe.matmul(PS[:, Y[s], 0:S], qkv_V[:, 0, :], qkv_aT[s][:, 0, :], start=True, stop=True)
                        pe.matmul(PS[:, Y[s], S:2 * S], qkv_V[:, 1, :], qkv_aT[s][:, 1, :], start=True, stop=True)
                        pe.matmul(PS[:, X[s], 0:S], qkv_aT[s][:, 2, :], qkv_V[:, 2, :], start=True, stop=True).then_inc(proj_raw, 1)
                    for r in range(QUADS):
                        for s in range(NS):
                            if r == 0:
                                pe.wait_ge(qk_ok, count(i, s, 1, 2))
                                pe.wait_ge(v_ok, count(i, s))
                            if r >= 2:
                                pe.wait_ge(hexp_ok, count(i, s, r - 2, QUADS))
                            bank = PS[:, (X, Y)[r % 2][s], :]
                            pe.matmul(bank, q_rows[s][:, r, :], k_heads[s][:, :, :], start=True, stop=False)
                            pe.matmul(bank, ident_bf[:, :], causal_bf[:, :].unsqueeze(1).to_broadcast([S, 4, S]), start=False,
                                      stop=True).then_inc(score_raw, 1)
                    for r in range(QUADS):
                        for s in range(NS):
                            if r < 2:
                                pe.wait_ge(hexp_ok, count(i, s, r + 2, QUADS))
                            else:
                                pe.wait_ge((wT_even, wT_odd)[r % 2], count(i, s, 0, 2))
                            for j in range(4):
                                mm = pe.transpose(PS[:, (X, Y)[r % 2][s], j * S:(j + 1) * S], weight[s][:, 4 * r + j, :], ident[:, :])
                            mm.then_inc(wT_raw, 1)
                    for s in range(NS):
                        pe.wait_ge(wT_odd, count(i, s, 1, 2))
                        pe.wait_ge(hinv_ok, count(i, s))
                        pe.transpose(PS[:, Y[s], 0:S], head_inv[s][:, :, :].rearrange("p h d -> p (h d)"), ident[:, :])\
                          .then_inc(inv_raw, 1)
                        pe.wait_ge(wT_even, count(i, s, 1, 2))
                        for j in range(HEADS):
                            mm = pe.matmul(PS[:, X[s], 0:S], v_wide[s][:, j * WIDE:(j + 1) * WIDE], weightT[s][:, j, :],
                                           start=(j == 0), stop=(j == HEADS - 1))
                        mm.then_inc(o_raw, 1)
                    for s in range(NS):
                        pe.wait_ge(oT_ok, count(i, s))
                        pe.matmul(PS[:, Y[s], 128:256], oT[s][:, :], p_KT[:, :], start=True, stop=True).then_inc(p_raw, 1)
                    for s in range(NS):
                        pe.wait_ge(p_exp, count(i, s))
                        pe.transpose(PS[:, X[s], 128:256], p_a[s][:, :], ident[:, :]).then_inc(p_aT_raw, 1)
                    for s in range(NS):
                        pe.wait_ge(p_aT_ok, count(i, s))
                        pe.matmul(PS[:, Y[s], 256:384], p_aT[s][:, :], p_V[:, :], start=True, stop=True).then_inc(p_out_raw, 1)
                    for s in range(NS):
                        pe.wait_ge(h2_ok, count(i, s))
                        pe.transpose(PS[:, X[s], 256:384], h2[s][:, :], ident[:, :]).then_inc(h2T_raw, 1)
                    for s in range(NS):
                        pe.wait_ge(h2T_ok, count(i, s))
                        pe.matmul(PS[:, Y[s], :], h2T[s][:, :], f_KT[:, :], start=True, stop=True).then_inc(f_raw, 1)
                    for s in range(NS):
                        pe.wait_ge(f_exp, count(i, s))
                        for j in range(NF // 128):
                            mm = pe.transpose(PS[:, X[s], j * S:(j + 1) * S], f_a[s][:, j * S:(j + 1) * S], ident[:, :])
                        mm.then_inc(f_aT_raw, 1)
                    for s in range(NS):
                        pe.wait_ge(f_aT_ok, count(i, s))
                        for j in range(NF // 128):
                            mm = pe.matmul(PS[:, Y[s], 0:D], f_aT[s][:, j, :], f_V[:, j, :], start=(j == 0), stop=(j == 3))
                        mm.then_inc(f_out_raw, 1)
                    for s in range(NS):
                        pe.wait_ge(x3_ok, count(i, s))
                        pe.transpose(PS[:, Y[s], 256:384], x3[s][:, :], ident[:, :]).then_inc(x3T_raw, 1)

            @block.scalar
            def _(act):
                with act.Fori(0, TURNS) as i:
                    for s in range(NS):
                        act.wait_ge(hT_raw, count(i, s))
                        act.activation(hT[s][:, :], PS[:, X[s], 0:S], ACT.Copy).then_inc(hT_ok, 1)
                    for s in range(NS):
                        act.wait_ge(qkv_nmax_ok, count(i, s))
                        for j in range(3):
                            ins = act.activation(qkv_a[s][:, j, :], PS[:, Y[s], j * D:(j + 1) * D], ACT.Exp,
                                                 bias=qkv_nmax[s][:, j:j + 1], accum_out=qkv_sum[s][:, j:j + 1])
                        ins.then_inc(qkv_exp, 1)
                    for s in range(NS):
                        act.wait_ge(qkv_aT_raw, count(i, s))
                        act.activation(qkv_aT[s][:, :, :], PS[:, X[s], 0:3 * S], ACT.Copy).then_inc(qkv_aT_ok, 1)
                    for s in range(NS):
                        act.wait_ge(proj_raw, count(i, s))
                        columns = v_wide[s][:, :].rearrange("p (h w) -> p h w", w=WIDE + HD)[:, :, 0:HD]
                        act.activation(columns, PS[:, X[s], 0:S].rearrange("p (h d) -> p h d", d=HD), ACT.Copy).then_inc(v_ok, 1)
                    for r in range(QUADS):
                        for s in range(NS):
                            act.wait_ge(hmax_ok, count(i, s, r, QUADS))
                            for j in range(4):
                                k = 4 * r + j
                                ins = act.activation(weight[s][:, k, :], PS[:, (X, Y)[r % 2][s], j * S:(j + 1) * S], ACT.Exp,
                                                     bias=head_nmax[s][:, k:k + 1], accum_out=head_sum[s][:, k:k + 1])
                            ins.then_inc(hexp_ok, 1)
                    for r in (0, 2):
                        for s in range(NS):
                            act.wait_ge(wT_raw, count(i, s, r, QUADS))
                            act.activation(weightT[s][:, 4 * r:4 * r + 4, :], PS[:, X[s], :], ACT.Copy).then_inc(wT_even, 1)
                    for s in range(NS):
                        act.wait_ge(inv_raw, count(i, s))
                        act.activation(inv_rows[s][:, :], PS[:, Y[s], 0:S], ACT.Copy).then_inc(inv_ok, 1)
                    for s in range(NS):
                        act.wait_ge(p_nmax_ok, count(i, s))
                        act.activation(p_a[s][:, :], PS[:, Y[s], 128:256], ACT.Exp, bias=p_nmax[s][:, 0:1],
                                       accum_out=p_sum[s][:, 0:1]).then_inc(p_exp, 1)
                    for s in range(NS):
                        act.wait_ge(p_aT_raw, count(i, s))
                        act.activation(p_aT[s][:, :], PS[:, X[s], 128:256], ACT.Copy).then_inc(p_aT_ok, 1)
                    for s in range(NS):
                        act.wait_ge(h2T_raw, count(i, s))
                        act.activation(h2T[s][:, :], PS[:, X[s], 256:384], ACT.Copy).then_inc(h2T_ok, 1)
                    for s in range(NS):
                        act.wait_ge(f_nmax_ok, count(i, s))
                        act.activation(f_a[s][:, :], PS[:, Y[s], :], ACT.Exp, bias=f_nmax[s][:, 0:1],
                                       accum_out=f_sum[s][:, 0:1]).then_inc(f_exp, 1)
                    for s in range(NS):
                        act.wait_ge(f_aT_raw, count(i, s))
                        act.activation(f_aT[s][:, :, :], PS[:, X[s], :], ACT.Copy).then_inc(f_aT_ok, 1)
                    for s in range(NS):
                        act.wait_ge(x3T_raw, count(i, s))
                        act.activation(x3T[:, bass.ds((i * NS + s) * S, S)], PS[:, Y[s], 256:384], ACT.Copy).then_inc(stored, 1)
                        act.activation(x3_tok[:, bass.ds(i * NS + s, 1), :], x3[s][:, :], ACT.Copy).then_inc(stored, 1)
                act.wait_ge(stored, 2 * B)

            @block.vector
            def _(dve):
                with dve.Fori(0, TURNS) as i:
                    for s in range(NS):
                        dve.bn_stats(stats[:, s, :], cond_tok[:, bass.ds(i * NS + s, 1), :]).then_inc(st_ok, 1)
                    for s in range(NS):
                        dve.wait_ge(st_ok, count(i, s))
                        dve.sem_inc(st_seen, 1)
                        dve.bn_aggr(mv[:, s, :], stats[:, s, :]).then_inc(mv_ok, 1)
                    dve.wait_ge(mv_ok, count(i, NS - 1))
                    dve.tensor_scalar(veps[:, :], mv[:, :, 1:2].rearrange("p s o -> p (s o)"), LN_EPS, None, ALU.add).then_inc(veps_ok, 1)
                    for s in range(NS):
                        dve.wait_ge(rstd_ok, i + 1)
                        dve.tensor_scalar(h[s][:, :], cond_tok[:, bass.ds(i * NS + s, 1), :].rearrange("p o d -> p (o d)"),
                                          mv[:, s, 0:1], rstd[:, s:s + 1], ALU.subtract, ALU.mult).then_inc(h_ok, 1)
                    for s in range(NS):
                        dve.wait_ge(qkv_raw, count(i, s))
                        dve.tensor_reduce(qkv_nmax[s][:, :], PS[:, Y[s], 0:3 * D].rearrange("p (j n) -> p j n", j=3),
                                          AX.X, ALU.max, negate=True).then_inc(qkv_nmax_ok, 1)
                    for s in range(NS):
                        dve.wait_ge(qkv_exp, count(i, s))
                        dve.reciprocal(qkv_inv[s][:, :], qkv_sum[s][:, :]).then_inc(qkv_inv_ok, 1)
                        dve.wait_ge(qkv_inv_ok, count(i, s))
                        dve.tensor_tensor(qkv_a[s][:, :, :], qkv_a[s][:, :, :],
                                          qkv_inv[s][:, :].unsqueeze(2).to_broadcast([S, 3, D]), ALU.mult).then_inc(qkv_a_ok, 1)
                    for s in range(NS):
                        dve.wait_ge(proj_raw, count(i, s))
                        dve.tensor_tensor(q_rows[s][:, :, :], PS[:, Y[s]:Y[s] + 1, 0:S].to_broadcast([D, QUADS, S]),
                                          quad_rows[:, :].unsqueeze(2).to_broadcast([D, QUADS, S]), ALU.mult).then_inc(qk_ok, 1)
                        dve.tensor_tensor(k_heads[s][:, :, :], PS[:, Y[s]:Y[s] + 1, S:2 * S].to_broadcast([D, 4, S]),
                                          head4[:, :].unsqueeze(2).to_broadcast([D, 4, S]), ALU.mult).then_inc(qk_ok, 1)
                    for r in range(QUADS):
                        for s in range(NS):
                            dve.wait_ge(score_raw, count(i, s, r, QUADS))
                            dve.tensor_reduce(head_nmax[s][:, 4 * r:4 * r + 4],
                                              PS[:, (X, Y)[r % 2][s], :].rearrange("p (j k) -> p j k", j=4),
                                              AX.X, ALU.max, negate=True).then_inc(hmax_ok, 1)
                    for s in range(NS):
                        dve.wait_ge(hexp_ok, count(i, s, QUADS - 1, QUADS))
                        dve.reciprocal(head_inv[s][:, :, :], head_sum[s][:, :].unsqueeze(2).to_broadcast([S, HEADS, HD])).then_inc(hinv_ok, 1)
                    for r in (1, 3):
                        for s in range(NS):
                            dve.wait_ge(wT_raw, count(i, s, r, QUADS))
                            dve.tensor_copy(weightT[s][:, 4 * r:4 * r + 4, :], PS[:, Y[s], :].rearrange("p (j k) -> p j k", j=4)).then_inc(wT_odd, 1)
                    for s in range(NS):
                        dve.wait_ge(o_raw, count(i, s))
                        dve.wait_ge(inv_ok, count(i, s))
                        dve.tensor_tensor(oT[s][:, :], PS[:, X[s], 0:S], inv_rows[s][:, :], ALU.mult).then_inc(oT_ok, 1)
                    for s in range(NS):
                        dve.wait_ge(p_raw, count(i, s))
                        dve.tensor_reduce(p_nmax[s][:, :], PS[:, Y[s], 128:256], AX.X, ALU.max, negate=True).then_inc(p_nmax_ok, 1)
                    for s in range(NS):
                        dve.wait_ge(p_exp, count(i, s))
                        dve.reciprocal(p_inv[s][:, :], p_sum[s][:, :]).then_inc(p_inv_ok, 1)
                    for s in range(NS):
                        dve.wait_ge(p_inv_ok, count(i, s))
                        dve.wait_ge(p_out_raw, count(i, s))
                        dve.scalar_tensor_tensor(out=x1[s][:, :], in0=PS[:, Y[s], 256:384], scalar=p_inv[s][:, 0:1],
                                                 in1=cond_tok[:, bass.ds(i * NS + s, 1), :].rearrange("p o d -> p (o d)"),
                                                 op0=ALU.mult, op1=ALU.add).then_inc(x1_ok, 1)
                    for s in range(NS):
                        dve.wait_ge(x1_ok, count(i, s))
                        dve.bn_stats(stats2[s][:, :], x1[s][:, :]).then_inc(f_st_ok, 1)
                    for s in range(NS):
                        dve.wait_ge(f_st_ok, count(i, s))
                        dve.sem_inc(f_st_seen, 1)
                        dve.bn_aggr(mv2[s][:, :], stats2[s][:, :]).then_inc(f_mv_ok, 1)
                    for s in range(NS):
                        dve.wait_ge(f_mv_ok, count(i, s))
                        dve.tensor_scalar(veps2[s][:, :], mv2[s][:, 1:2], LN_EPS, None, ALU.add).then_inc(f_veps_ok, 1)
                    for s in range(NS):
                        dve.wait_ge(f_rstd_ok, count(i, s))
                        dve.tensor_scalar(h2[s][:, :], x1[s][:, :], mv2[s][:, 0:1], rstd2[s][:, 0:1],
                                          ALU.subtract, ALU.mult).then_inc(h2_ok, 1)
                    for s in range(NS):
                        dve.wait_ge(f_raw, count(i, s))
                        dve.tensor_reduce(f_nmax[s][:, :], PS[:, Y[s], :], AX.X, ALU.max, negate=True).then_inc(f_nmax_ok, 1)
                    for s in range(NS):
                        dve.wait_ge(f_exp, count(i, s))
                        dve.reciprocal(f_inv[s][:, :], f_sum[s][:, :]).then_inc(f_inv_ok, 1)
                    for s in range(NS):
                        dve.wait_ge(f_inv_ok, count(i, s))
                        dve.wait_ge(f_out_raw, count(i, s))
                        dve.scalar_tensor_tensor(out=x2[s][:, :], in0=PS[:, Y[s], 0:D], scalar=f_inv[s][:, 0:1],
                                                 in1=x1[s][:, :], op0=ALU.mult, op1=ALU.add).then_inc(x2_ok, 1)
                    for s in range(NS):
                        dve.wait_ge(x2_ok, count(i, s))
                        dve.tensor_tensor(x3[s][:, :], x2[s][:, :],
                                          x_tok[:, bass.ds(i * NS + s, 1), :].rearrange("p o d -> p (o d)"), ALU.add).then_inc(x3_ok, 1)
        signals.clear()


def scan_inputs_phase(nc, a, K):
    import concourse.bass as bass
    from concourse import mybir
    from contextlib import ExitStack
    f32 = mybir.dt.float32
    ALU, ACT = mybir.AluOpType, mybir.ActivationFunctionType
    NS = 2
    PAIRS = NG // NS
    PAD = N_TAPS - 1
    with ExitStack() as ctx:
        def sb(name, shape, dt=f32):
            return ctx.enter_context(nc.sbuf_tensor(name, shape, dt))

        def per(name, shape):
            return [sb(f"{name}{s}", shape) for s in range(NS)]

        signals = Signals(nc, ctx, "pre")
        PS, ident, x3T, gateT, xnT = (K[n] for n in ("PS", "ident", "x3T", "gateT", "xnT"))
        w_inT = sb("w_inT", [D, 2 * DI])
        tembT, taps, chan = sb("tembT", [128, NH, B]), sb("taps", [128, NH, N_TAPS]), sb("chan", [128, NH])
        ln_g, ln_b = sb("ln_g", [S, DI]), sb("ln_b", [S, DI])
        w_B, w_Cdt = sb("w_B", [128, NH, N_STATE]), sb("w_Cdt", [128, NH, 48])
        w_dtT = sb("w_dtT", [48, 48])
        state_cols = sb("state_cols", [N_STATE, 2])
        a_tanh, a_step = sb("a_tanh", [N_STATE, 1]), sb("a_step", [N_STATE, 1])
        ones_col, minus_half, plus_half = sb("ones_col", [128, 1]), sb("minus_half3", [S, GB]), sb("plus_half3", [S, GB])
        xr = per("xr", [128, NH, GB, PAD + S])
        conv = per("conv", [128, NH, GB, S])
        stats, mv, veps, rstd = per("st3", [S, GB, 6]), per("mv3", [S, GB, 2]), per("veps3", [S, GB]), per("rstd3", [S, GB])
        xn = per("xn", [S, GB, DI])
        xng, sq = per("xng", [128, NH, GT]), per("sq", [128, NH, GT])
        norm2, norm = per("norm2", [S, GB]), per("norm", [S, GB])
        bd = per("bd", [S, GB, N_STATE])
        cdt = per("cdt", [48, GT])
        ad = per("ad", [N_STATE, GT])

        loads = [(w_inT[:, :], a["w_inT"]), (tembT[:, :, :], a["condT"].rearrange("(h p) b -> p h b", p=128)),
                 (taps[:, :, :], a["taps"].rearrange("(h p) k -> p h k", p=128)),
                 (chan[:, :], a["b_conv"].rearrange("(h p) -> p h", p=128)),
                 (ln_g[:, :], a["ln_g"].rearrange("(o c) -> o c", o=1).partition_broadcast(S)),
                 (ln_b[:, :], a["ln_b"].rearrange("(o c) -> o c", o=1).partition_broadcast(S)),
                 (w_B[:, :, :], a["w_xpT"][:, 0:16].rearrange("(h p) s -> p h s", p=128)),
                 (w_Cdt[:, :, 0:16], a["w_xpT"][:, 16:32].rearrange("(h p) s -> p h s", p=128)),
                 (w_Cdt[:, :, 32:48], a["w_xpT"][:, 32:48].rearrange("(h p) s -> p h s", p=128)),
                 (w_dtT[32:48, 0:N_STATE], a["w_dtT"]), (state_cols[:, :], a["state_cols"])]
        cleared, loaded, filled, a_tanh_ok, a_step_ok = signals.take_all("cleared loaded filled a_tanh_ok a_step_ok")
        xn_sent, bd_sent, c_sent, ad_sent = signals.take_all("xn_sent bd_sent c_sent ad_sent", NS)
        with nc.Block() as block:
            @block.sync
            def _(sp):
                for s in range(NS):
                    for sent in (xn_sent, bd_sent, c_sent, ad_sent):
                        sp.sem_inc(sent[s], 16)
                sp.wait_ge(cleared, 2)
                for dst, src in loads:
                    sp.dma_start(dst, src, allow_slow_non_contiguous=True).then_inc(loaded, 16)
                sp.wait_ge(loaded, 16 * len(loads))

            @block.gpsimd
            def _(pool):
                pool.memset(w_Cdt[:, :, :], 0.0).then_inc(cleared, 1)
                pool.memset(w_dtT[:, :], 0.0).then_inc(cleared, 1)
                pool.memset(ones_col[:, :], 1.0).then_inc(filled, 1)
                pool.memset(minus_half[:, :], -0.5).then_inc(filled, 1)
                pool.memset(plus_half[:, :], 0.5).then_inc(filled, 1)
                for s in range(NS):
                    pool.memset(xr[s][:, :, :, :], 0.0).then_inc(filled, 1)
                pool.wait_ge(filled, 3 + NS)

            @block.scalar
            def _(act):
                act.wait_ge(loaded, 16 * len(loads))
                act.activation(a_tanh[:, :], state_cols[:, 1:2], ACT.Tanh).then_inc(a_tanh_ok, 1)

            @block.vector
            def _(dve):
                dve.wait_ge(a_tanh_ok, 1)
                dve.tensor_scalar(a_step[:, :], a_tanh[:, :], -0.01, None, ALU.mult).then_inc(a_step_ok, 1)
                dve.wait_ge(a_step_ok, 1)

        (in_raw, gate_ok, xr_ok, conv_ok, xc_ok, xc_tok_raw, st_ok, st_seen, mv_ok, veps_ok, rstd_ok, xhat_ok,
         scaled_ok, xn_ok, xnT_raw, xng_ok, xnT_ok, sq_ok, b_raw, cdt_raw, norm2_ok, norm_ok, bd_ok, cdt_ok, dt_raw,
         tanh_ok, ad_ok) = signals.take_all(
            "in_raw gate_ok xr_ok conv_ok xc_ok xc_tok_raw st_ok st_seen mv_ok veps_ok rstd_ok xhat_ok "
            "scaled_ok xn_ok xnT_raw xng_ok xnT_ok sq_ok b_raw cdt_raw norm2_ok norm_ok bd_ok cdt_ok dt_raw "
            "tanh_ok ad_ok", NS)

        with nc.Block() as block:
            @block.sync
            def _(sp):
                with sp.Fori(0, PAIRS) as i:
                    n = i + 1
                    for s in range(NS):
                        first = (i * NS + s) * GB
                        sp.wait_ge(xn_ok[s], n)
                        sp.dma_start(K["xn_d"][bass.ds(first, GB), :, :].rearrange("b t c -> t b c"), xn[s][:, :, :]).then_inc(xn_sent[s], 16)
                    for s in range(NS):
                        first = (i * NS + s) * GB
                        sp.wait_ge(bd_ok[s], n)
                        sp.dma_start(K["bd_d"][bass.ds(first, GB), :, :].rearrange("b t s -> t b s"), bd[s][:, :, :]).then_inc(bd_sent[s], 16)
                        sp.wait_ge(cdt_ok[s], n)
                        sp.dma_start(K["c_d"][bass.ds(first, GB), :, :].rearrange("b s t -> s b t"),
                                     cdt[s][0:N_STATE, :].rearrange("s (b t) -> s b t", b=GB)).then_inc(c_sent[s], 16)
                        sp.wait_ge(ad_ok[s], n)
                        sp.dma_start(K["ad_d"][bass.ds(first, GB), :, :].rearrange("b s t -> s b t"),
                                     ad[s][:, :].rearrange("s (b t) -> s b t", b=GB)).then_inc(ad_sent[s], 16)
                for s in range(NS):
                    for sent in (xn_sent, bd_sent, c_sent, ad_sent):
                        sp.wait_ge(sent[s], 16 * (PAIRS + 1))

            @block.gpsimd
            def _(pool):
                with pool.Fori(0, PAIRS) as i:
                    n = i + 1
                    for s in range(NS):
                        pool.wait_ge(veps_ok[s], n)
                        pool.tensor_tensor(rstd[s][:, :], veps[s][:, :], minus_half[:, :], ALU.pow).then_inc(rstd_ok[s], 1)
                    for s in range(NS):
                        pool.wait_ge(xhat_ok[s], n)
                        pool.tensor_tensor(xn[s][:, :, :], xn[s][:, :, :], ln_g[:, :].unsqueeze(1).to_broadcast([S, GB, DI]),
                                           ALU.mult).then_inc(scaled_ok[s], 1)
                        pool.wait_ge(scaled_ok[s], n)
                        pool.tensor_tensor(xn[s][:, :, :], xn[s][:, :, :], ln_b[:, :].unsqueeze(1).to_broadcast([S, GB, DI]),
                                           ALU.add).then_inc(xn_ok[s], 1)
                    for s in range(NS):
                        pool.wait_ge(norm2_ok[s], n)
                        pool.tensor_tensor(norm[s][:, :], norm2[s][:, :], plus_half[:, :], ALU.pow).then_inc(norm_ok[s], 1)

            @block.tensor
            def _(pe):
                with pe.Fori(0, PAIRS) as i:
                    n = i + 1
                    for s in range(NS):
                        for j in range(4):
                            mm = pe.matmul(PS[:, 4 * s + j, :], w_inT[:, j * 128:(j + 1) * 128],
                                           x3T[:, bass.ds((i * NS + s) * GT, GT)], start=True, stop=True)
                        mm.then_inc(in_raw[s], 1)
                    for s in range(NS):
                        pe.wait_ge(xc_ok[s], n)
                        for b in range(GB):
                            for h in range(NH):
                                at = (b % 2) * DI + h * 128
                                mm = pe.transpose(PS[:, 4 * s + b // 2, at:at + 128], conv[s][:, h, b, :], ident[:, :])
                        mm.then_inc(xc_tok_raw[s], 1)
                    for s in range(NS):
                        pe.wait_ge(xn_ok[s], n)
                        pe.wait_ge(gate_ok[s], n)
                        for h in range(NH):
                            for b in range(GB):
                                mm = pe.transpose(PS[:, 4 * s + 2 + h, b * S:(b + 1) * S], xn[s][:, b, h * 128:(h + 1) * 128], ident[:, :])
                        mm.then_inc(xnT_raw[s], 1)
                    for s in range(NS):
                        pe.wait_ge(sq_ok[s], n)
                        for h in range(NH):
                            mm = pe.matmul(PS[0:48, 4 * s + 1, :], w_Cdt[:, h, :], xng[s][:, h, :], start=(h == 0), stop=(h == 1))
                        mm.then_inc(cdt_raw[s], 1)
                        for b in range(GB):
                            for h in range(NH):
                                pe.matmul(PS[:, 4 * s, b * 16:(b + 1) * 16], xng[s][:, h, b * S:(b + 1) * S], w_B[:, h, :],
                                          start=(h == 0), stop=(h == 1))
                            for h in range(NH):
                                mm = pe.matmul(PS[:, 4 * s, 64 + b:65 + b], sq[s][:, h, b * S:(b + 1) * S], ones_col[:, :],
                                               start=(h == 0), stop=(h == 1))
                        mm.then_inc(b_raw[s], 1)
                    for s in range(NS):
                        pe.wait_ge(xnT_ok[s], n)
                        pe.wait_ge(cdt_ok[s], n)
                        pe.matmul(PS[0:48, 4 * s + 2, :], w_dtT[32:48, :], cdt[s][32:48, :], start=True, stop=True).then_inc(dt_raw[s], 1)
                    for s in range(NS):
                        pe.wait_ge(bd_ok[s], n)
                        pe.wait_ge(tanh_ok[s], n)

            @block.scalar
            def _(act):
                with act.Fori(0, PAIRS) as i:
                    n = i + 1
                    for s in range(NS):
                        act.wait_ge(in_raw[s], n)
                        for h in range(NH):
                            ins = act.activation(gateT[:, h, bass.ds((i * NS + s) * GT, GT)], PS[:, 4 * s + 2 + h, :], ACT.Silu)
                        ins.then_inc(gate_ok[s], 1)
                    for s in range(NS):
                        act.wait_ge(conv_ok[s], N_TAPS * NH * n)
                        act.activation(conv[s][:, :, :, :], conv[s][:, :, :, :], ACT.Silu).then_inc(xc_ok[s], 1)
                    for s in range(NS):
                        act.wait_ge(xnT_raw[s], n)
                        act.activation(xng[s][:, :, :], PS[:, 4 * s + 2:4 * s + 4, :], ACT.Copy).then_inc(xng_ok[s], 1)
                        act.activation(xnT[:, :, bass.ds((i * NS + s) * GT, GT)], PS[:, 4 * s + 2:4 * s + 4, :], ACT.Copy).then_inc(xnT_ok[s], 1)
                        act.wait_ge(xng_ok[s], n)
                        act.activation(sq[s][:, :, :], xng[s][:, :, :], ACT.Square).then_inc(sq_ok[s], 1)
                    for s in range(NS):
                        act.wait_ge(c_sent[s], 16 * n)
                        act.wait_ge(cdt_raw[s], n)
                        act.activation(cdt[s][:, :], PS[0:48, 4 * s + 1, :], ACT.Copy).then_inc(cdt_ok[s], 1)
                    for s in range(NS):
                        act.wait_ge(ad_sent[s], 16 * n)
                        act.wait_ge(dt_raw[s], n)
                        act.activation(ad[s][:, :], PS[0:N_STATE, 4 * s + 2, :], ACT.Tanh, bias=state_cols[:, 0:1]).then_inc(tanh_ok[s], 1)

            @block.vector
            def _(dve):
                with dve.Fori(0, PAIRS) as i:
                    n = i + 1
                    for s in range(NS):
                        dve.wait_ge(in_raw[s], n)
                        for h in range(NH):
                            dve.tensor_tensor(xr[s][:, h, :, PAD:PAD + S], PS[:, 4 * s + h, :].rearrange("p (b t) -> p b t", b=GB),
                                              tembT[:, h, bass.ds((i * NS + s) * GB, GB)].unsqueeze(2).to_broadcast([128, GB, S]),
                                              ALU.add).then_inc(xr_ok[s], 1)
                    for k in range(N_TAPS):
                        for s in range(NS):
                            for h in range(NH):
                                if k == 0:
                                    dve.wait_ge(xr_ok[s], NH * n)
                                    ins = dve.tensor_scalar(conv[s][:, h, :, :], xr[s][:, h, :, 0:S], taps[:, h, 0:1], chan[:, h:h + 1],
                                                            ALU.mult, ALU.add)
                                else:
                                    dve.wait_ge(conv_ok[s], i * (N_TAPS * NH) + ((k - 1) * NH + h + 1))
                                    ins = dve.scalar_tensor_tensor(out=conv[s][:, h, :, :], in0=xr[s][:, h, :, k:k + S],
                                                                   scalar=taps[:, h, k:k + 1], in1=conv[s][:, h, :, :],
                                                                   op0=ALU.mult, op1=ALU.add)
                                ins.then_inc(conv_ok[s], 1)
                    for s in range(NS):
                        dve.wait_ge(xc_tok_raw[s], n)
                        for b in range(GB):
                            ins = dve.bn_stats(stats[s][:, b, :], PS[:, 4 * s + b // 2, (b % 2) * DI:(b % 2 + 1) * DI])
                        ins.then_inc(st_ok[s], 1)
                        dve.wait_ge(st_ok[s], n)
                        dve.sem_inc(st_seen[s], 1)
                        for b in range(GB):
                            ins = dve.bn_aggr(mv[s][:, b, :], stats[s][:, b, :])
                        ins.then_inc(mv_ok[s], 1)
                        dve.wait_ge(mv_ok[s], n)
                        dve.tensor_scalar(veps[s][:, :].unsqueeze(2), mv[s][:, :, 1:2], LN_EPS, None, ALU.add).then_inc(veps_ok[s], 1)
                    for s in range(NS):
                        dve.wait_ge(xn_sent[s], 16 * n)
                        dve.wait_ge(rstd_ok[s], n)
                        for b in range(GB):
                            ins = dve.tensor_scalar(xn[s][:, b, :], PS[:, 4 * s + b // 2, (b % 2) * DI:(b % 2 + 1) * DI],
                                                    mv[s][:, b, 0:1], rstd[s][:, b:b + 1], ALU.subtract, ALU.mult)
                        ins.then_inc(xhat_ok[s], 1)
                    for s in range(NS):
                        dve.wait_ge(b_raw[s], n)
                        dve.tensor_scalar(norm2[s][:, :], PS[:, 4 * s, 64:64 + GB], 1.0, None, ALU.min).then_inc(norm2_ok[s], 1)
                    for s in range(NS):
                        dve.wait_ge(bd_sent[s], 16 * n)
                        dve.wait_ge(norm_ok[s], n)
                        dve.tensor_tensor(bd[s][:, :, :], PS[:, 4 * s, 0:GB * N_STATE].rearrange("p (b s) -> p b s", b=GB),
                                          norm[s][:, :].unsqueeze(2).to_broadcast([S, GB, N_STATE]), ALU.mult).then_inc(bd_ok[s], 1)
                    for s in range(NS):
                        dve.wait_ge(tanh_ok[s], n)
                        dve.tensor_scalar(ad[s][:, :], ad[s][:, :], a_step[:, 0:1], 1.0, ALU.mult, ALU.add).then_inc(ad_ok[s], 1)
        signals.clear()


def scan_phase(nc, a, K):
    import concourse.bass as bass
    from concourse import mybir
    from contextlib import ExitStack
    f32 = mybir.dt.float32
    ALU, ACT = mybir.AluOpType, mybir.ActivationFunctionType
    BG = 128 // N_STATE
    G = B // BG
    HALF = 8
    STEPS = 2 * HALF
    CHUNKS = S // STEPS
    RING = 4
    with ExitStack() as ctx:
        def sb(name, shape, dt=f32):
            return ctx.enter_context(nc.sbuf_tensor(name, shape, dt))

        signals = Signals(nc, ctx, "scan")
        PS, ident, xnT = (K[n] for n in ("PS", "ident", "xnT"))
        skip = sb("skip", [128, NH])
        decay, c_all = sb("decay", [128, G, S]), sb("c_all", [128, G, S])
        own = sb("own", [128, BG])
        PARTS = 4
        f32r = mybir.dt.float32r
        same_batch = sb("same_batch", [PARTS * B, B])
        x_in = [sb(f"x_in{k}", [PARTS * B, HALF, DI]) for k in range(2)]
        x_part = [sb(f"x_part{k}", [PARTS * B, HALF, DI], f32r) for k in range(2)]
        bd_in = [sb(f"bd_in{k}", [PARTS * B, HALF, N_STATE]) for k in range(2)]
        bd_high = [sb(f"bd_high{k}", [PARTS * B, HALF, N_STATE], f32r) for k in range(2)]
        bd_part = [sb(f"bd_part{k}", [PARTS * B, HALF, N_STATE]) for k in range(2)]
        bd_diag = [sb(f"bd_diag{k}", [PARTS * B, HALF, B, N_STATE], f32r) for k in range(2)]
        decay_now = [sb(f"decay_now{k}", [128, G, HALF]) for k in range(2)]
        WIDE = HALF * BG
        c_diag = [sb(f"c_diag{k}", [128, G * HALF * WIDE + WIDE]) for k in range(2)]
        y_tok = sb("y_tok", [WIDE, G, DI])
        y_new = sb("y_new", [128, NH, HALF * B])
        grown = sb("grown", [128, G, DI])
        state = [K["x3T"][:, k * G * DI:(k + 1) * G * DI].rearrange("p (g c) -> p g c", g=G) for k in range(RING)]

        resident_in, ones_ok, cut_ok, zero_ok, same_ok = signals.take_all("resident_in ones_ok cut_ok zero_ok same_ok")
        x_loaded, bd_loaded, diag_ok, c_ok, decay_ok = signals.take_all("x_loaded bd_loaded diag_ok c_ok decay_ok", 2)
        spread_go, load_go, add_go = signals.take_all("spread_go load_go add_go")
        x_high, x_parts, bd_high_ok, bd_part_ok, bd_low_ok = signals.take_all("x_high x_parts bd_high_ok bd_part_ok bd_low_ok", 2)
        bx_raw, grown_ok, state_ok, y_raw, y_stored = signals.take_all("bx_raw grown_ok state_ok y_raw y_stored")
        y_copied, yT_raw, y_added, wide_zero, skipped, turn_go = signals.take_all("y_copied yT_raw y_added wide_zero skipped turn_go")

        with nc.Block() as block:
            @block.sync
            def _(sp):
                sp.dma_start(decay[:, :, :], K["ad_d"].rearrange("(g b) s t -> (b s) g t", g=G)).then_inc(resident_in, 16)
                sp.dma_start(c_all[:, :, :], K["c_d"].rearrange("(g b) s t -> (b s) g t", g=G)).then_inc(resident_in, 16)
                sp.dma_start(skip[:, :], a["D"].rearrange("(h p) -> p h", p=128), allow_slow_non_contiguous=True).then_inc(resident_in, 16)
                sp.wait_ge(resident_in, 48)
                sp.sem_inc(state_ok, 1)
                sp.sem_inc(grown_ok, 2)
                sp.sem_inc(y_raw, RING)
                sp.sem_inc(y_stored, 2)
                sp.sem_inc(y_added, 1)
                sp.sem_inc(yT_raw, 1)

            @block.gpsimd
            def _(pool):
                pool.memset(own[:, :], 1.0).then_inc(ones_ok, 1)
                pool.memset(state[RING - 1][:, :, :], 0.0).then_inc(zero_ok, 1)
                for k in range(2):
                    pool.memset(c_diag[k][:, :], 0.0).then_inc(wide_zero, 1)
                pool.wait_ge(ones_ok, 1)
                pool.affine_select(out=own[:, :], in_=own[:, :], compare_op=ALU.is_ge, fill=0.0, base=0,
                                   pattern=[[-N_STATE, BG]], channel_multiplier=1).then_inc(cut_ok, 1)
                pool.wait_ge(cut_ok, 1)
                pool.affine_select(out=own[:, :], in_=own[:, :], compare_op=ALU.is_ge, fill=0.0, base=N_STATE - 1,
                                   pattern=[[N_STATE, BG]], channel_multiplier=-1).then_inc(cut_ok, 1)
                pool.wait_ge(cut_ok, 2)
                pool.wait_ge(zero_ok, 1)
                pool.wait_ge(wide_zero, 2)

            @block.vector
            def _(dve):
                dve.wait_ge(resident_in, 48)
                for h in range(NH):
                    dve.tensor_scalar(xnT[:, h, :], xnT[:, h, :], skip[:, h:h + 1], None, ALU.mult).then_inc(skipped, 1)
                dve.wait_ge(skipped, NH)
                dve.tensor_reduce(same_batch[:, :], ident[:, :].rearrange("p (q b) -> p b q", q=PARTS), mybir.AxisListType.X,
                                  ALU.add).then_inc(same_ok, 1)
                dve.wait_ge(same_ok, 1)

        with nc.Block() as block:
            @block.sync
            def _(sp):
                def load(k, at):
                    for q in range(PARTS):
                        sp.dma_start(x_in[k][q * B:(q + 1) * B, :, :], K["xn_d"][:, bass.ds(at, HALF), :]).then_inc(x_loaded[k], 16)
                        sp.dma_start(bd_in[k][q * B:(q + 1) * B, :, :], K["bd_d"][:, bass.ds(at, HALF), :]).then_inc(bd_loaded[k], 16)

                for k in range(2):
                    load(k, k * HALF)
                with sp.Fori(1, CHUNKS) as c:
                    for k in range(2):
                        sp.wait_ge(bd_low_ok[k], 2 * c)
                        sp.wait_ge(x_parts[k], c)
                        sp.sem_inc(load_go, 1)
                        load(k, c * STEPS + k * HALF)

            @block.gpsimd
            def _(pool):
                def spread_bd(k, n):
                    pool.tensor_tensor(bd_diag[k][:, :, :, :],
                                       bd_part[k][:, :, :].unsqueeze(2).to_broadcast([PARTS * B, HALF, B, N_STATE]),
                                       same_batch[:, :].unsqueeze(1).unsqueeze(3).to_broadcast([PARTS * B, HALF, B, N_STATE]),
                                       ALU.mult).then_inc(diag_ok[k], 1)

                def spread_c(k, at, n):
                    for g in range(G):
                        own_columns = c_diag[k][:, g * HALF * WIDE:(g + 1) * HALF * WIDE + WIDE].rearrange(
                            "p (t w) -> p t w", w=WIDE + BG)[:, :, 0:BG]
                        pool.tensor_tensor(own_columns, c_all[:, g, bass.ds(at, HALF)].unsqueeze(2).to_broadcast([128, HALF, BG]),
                                           own[:, :].unsqueeze(1).to_broadcast([128, HALF, BG]), ALU.mult).then_inc(c_ok[k], 1)
                    pool.tensor_copy(decay_now[k][:, :, :], decay[:, :, bass.ds(at, HALF)]).then_inc(decay_ok[k], 1)
                    pool.wait_ge(diag_ok[k], n)
                    pool.wait_ge(c_ok[k], G * n)
                    pool.wait_ge(decay_ok[k], n)

                def x_low(k):
                    low = x_part[k][2 * B:4 * B, :, :]
                    pool.tensor_tensor(low, x_in[k][2 * B:4 * B, :, :], low.bitcast(f32), ALU.subtract).then_inc(x_parts[k], 1)

                def bd_low(k, n):
                    pool.wait_ge(bd_high_ok[k], n)
                    pool.wait_ge(x_parts[k], n)
                    for q in (1, 3):
                        part = (slice(q * B, (q + 1) * B),) + (slice(None),) * 2
                        ins = pool.tensor_tensor(bd_part[k][part], bd_in[k][part], bd_high[k][part].bitcast(f32), ALU.subtract)
                        ins.then_inc(bd_low_ok[k], 1)
                        pool.wait_ge(bd_low_ok[k], 2 * n - (q == 1))
                    pool.wait_ge(bd_part_ok[k], n)

                def add(k, at, n):
                    for h in range(NH):
                        into = xnT[:, h, :].rearrange("p (b t) -> p b t", b=B)[:, :, bass.ds(at, HALF)]
                        ins = pool.tensor_tensor(into, into, y_new[:, h, :].rearrange("p (g t b) -> p g b t", g=G, t=HALF), ALU.add)
                    ins.then_inc(y_added, 1)
                    pool.wait_ge(y_added, n + 1)

                for k in range(2):
                    pool.wait_ge(x_high[k], 1)
                    x_low(k)
                    bd_low(k, 1)
                    spread_bd(k, 1)
                    spread_c(k, k * HALF, 1)
                with pool.Fori(1, CHUNKS) as c:
                    for k in range(2):
                        pool.wait_ge(x_high[k], c + 1)
                        x_low(k)
                        bd_low(k, c + 1)
                        spread_bd(k, c + 1)
                        pool.wait_ge(y_stored, c * 2 + (k + 1))
                        pool.sem_inc(add_go, 1)
                        add(k, (c - 1) * STEPS + k * HALF, c * 2 + (k - 1))
                        spread_c(k, c * STEPS + k * HALF, c + 1)
                for k in range(2):
                    pool.wait_ge(y_stored, CHUNKS * 2 + (k + 1))
                    add(k, (CHUNKS - 1) * STEPS + k * HALF, CHUNKS * 2 + (k - 1))

            @block.tensor
            def _(pe):
                def inputs(c, j):
                    k, tt = j // HALF, j % HALF
                    if tt == 0:
                        pe.wait_ge(x_parts[k], c + 1)
                        pe.wait_ge(diag_ok[k], c + 1)
                    pe.wait_ge(grown_ok, c * STEPS + (j + 1))
                    for g in range(G):
                        mm = pe.matmul(PS[:, 2 * (j % 2) + g // 2, (g % 2) * DI:(g % 2 + 1) * DI],
                                       bd_diag[k][:, tt, g * BG:(g + 1) * BG, :].rearrange("p b s -> p (b s)"), x_part[k][:, tt, :],
                                       start=True, stop=True)
                    mm.then_inc(bx_raw, 1)

                def outputs(c, j):
                    k, tt = j // HALF, j % HALF
                    if tt == 0:
                        pe.wait_ge(c_ok[k], G * (c + 1))
                        pe.wait_ge(y_stored, c * 2 + (k + 1))
                    pe.wait_ge(state_ok, c * STEPS + (j + 2))
                    for g in range(G):
                        at = (g * HALF + tt) * WIDE
                        mm = pe.matmul(PS[0:WIDE, 4 + 2 * k + g // 2, (g % 2) * DI:(g % 2 + 1) * DI], c_diag[k][:, at:at + WIDE],
                                       state[j % RING][:, g, :], start=(tt == 0 and g % 2 == 0),
                                       stop=(tt == HALF - 1 and g % 2 == 1))
                    mm.then_inc(y_raw, 1)
                    if tt == HALF - 1:
                        pe.wait_ge(y_copied, c * 2 + (k + 1))
                        pe.sem_inc(turn_go, 1)
                        for h in range(NH):
                            for g in range(G):
                                at = (h * G + g) * WIDE
                                mm = pe.transpose(PS[:, 4 + 2 * k, at:at + WIDE], y_tok[:, g, h * 128:(h + 1) * 128],
                                                  ident[0:WIDE, 0:WIDE])
                        mm.then_inc(yT_raw, 1)

                inputs(0, 0)
                inputs(0, 1)
                with pe.Fori(0, CHUNKS - 1) as c:
                    for j in range(STEPS):
                        inputs(c + (j + 2) // STEPS, (j + 2) % STEPS)
                        outputs(c, j)
                for j in range(STEPS):
                    if j + 2 < STEPS:
                        inputs(CHUNKS - 1, j + 2)
                    outputs(CHUNKS - 1, j)

            @block.scalar
            def _(act):
                def split_x(k, n):
                    act.wait_ge(x_loaded[k], 16 * PARTS * n)
                    act.activation(x_part[k][:, :, :], x_in[k][:, :, :], ACT.Copy).then_inc(x_high[k], 1)

                def split_bd(k, n):
                    act.wait_ge(bd_loaded[k], 16 * PARTS * n)
                    act.activation(bd_high[k][:, :, :], bd_in[k][:, :, :], ACT.Copy).then_inc(bd_high_ok[k], 1)
                    act.wait_ge(bd_high_ok[k], n)
                    for q in (0, 2):
                        ins = act.activation(bd_part[k][q * B:(q + 1) * B, :, :], bd_high[k][q * B:(q + 1) * B, :, :].bitcast(f32), ACT.Copy)
                    ins.then_inc(bd_part_ok[k], 1)

                def copy_y(c, k):
                    act.wait_ge(yT_raw, c * 2 + (k + 1))
                    act.wait_ge(y_raw, c * STEPS + (RING + (k + 1) * HALF))
                    act.activation(y_tok[:, :, :], PS[0:WIDE, 4 + 2 * k:4 + 2 * k + 2, :], ACT.Copy).then_inc(y_copied, 1)

                def store_y(c, k):
                    act.wait_ge(y_added, c * 2 + (k + 1))
                    act.wait_ge(yT_raw, c * 2 + (k + 2))
                    act.activation(y_new[:, :, :], PS[:, 4 + 2 * k, :], ACT.Copy).then_inc(y_stored, 1)

                for k in range(2):
                    split_x(k, 1)
                    split_bd(k, 1)
                with act.Fori(0, CHUNKS - 1) as c:
                    for k in range(2):
                        act.wait_ge(bx_raw, c * STEPS + (k + 1) * HALF)
                        split_x(k, c + 2)
                        split_bd(k, c + 2)
                        copy_y(c, k)
                        store_y(c, k)
                for k in range(2):
                    copy_y(CHUNKS - 1, k)
                    store_y(CHUNKS - 1, k)

            @block.vector
            def _(dve):
                with dve.Fori(0, CHUNKS) as c:
                    for j in range(STEPS):
                        k, tt = j // HALF, j % HALF
                        if tt == 0:
                            dve.wait_ge(decay_ok[k], c + 1)
                        dve.wait_ge(bx_raw, c * STEPS + (j + 1))
                        dve.wait_ge(state_ok, c * STEPS + (j + 1))
                        for g in range(G):
                            ins = dve.scalar_tensor_tensor(out=grown[:, g, :], in0=state[(j - 1) % RING][:, g, :],
                                                           scalar=decay_now[k][:, g, tt:tt + 1],
                                                           in1=PS[:, 2 * (j % 2) + g // 2, (g % 2) * DI:(g % 2 + 1) * DI],
                                                           op0=ALU.mult, op1=ALU.add)
                        ins.then_inc(grown_ok, 1)
                        dve.wait_ge(grown_ok, c * STEPS + (j + 3))
                        dve.wait_ge(y_raw, c * STEPS + (j + 1))
                        dve.tensor_scalar(state[j % RING][:, :, :], grown[:, :, :], CLIP, -CLIP, ALU.min, ALU.max).then_inc(state_ok, 1)
        signals.clear()


def expert_inputs_phase(nc, a, K):
    import concourse.bass as bass
    from concourse import mybir
    from contextlib import ExitStack
    f32 = mybir.dt.float32
    ALU, ACT, AX = mybir.AluOpType, mybir.ActivationFunctionType, mybir.AxisListType
    NS = 2
    PAIRS = NG // NS
    with ExitStack() as ctx:
        def sb(name, shape, dt=f32):
            return ctx.enter_context(nc.sbuf_tensor(name, shape, dt))

        def per(name, shape):
            return [sb(f"{name}{s}", shape) for s in range(NS)]

        signals = Signals(nc, ctx, "gates")
        PS, ident, yT, gateT, hT, gate = (K[n] for n in ("PS", "ident", "xnT", "gateT", "hT", "gate"))
        w_outT, router = sb("w_outT", [128, NH, D]), sb("router", [D, E_ROUTED])
        minus_half, rank = sb("minus_half5", [S, GB]), sb("rank", [S, E_ROUTED])
        z = per("z", [128, NH, GT])
        x4, x4n, x4T, junk = per("x4", [S, GB, D]), per("x4n", [S, GB, D]), per("x4T", [D, GT]), per("junk", [S, D])
        ms, meps, rrms = per("ms", [S, GB]), per("meps", [S, GB]), per("rrms", [S, GB])
        small = {n: per(n, [S, GB]) for n in ("lmax", "gsum", "ginv", "top", "pick", "msum", "msum_eps", "minv")}
        wide = {n: per(n, [S, GB, E_ROUTED]) for n in ("shifted", "gexp", "g", "same", "ranked", "first", "rest", "second", "both", "kept")}
        loads = [(w_outT[:, :, :], a["w_outT"].rearrange("(h p) d -> p h d", p=128)), (router[:, :], a["router"])]
        loaded, filled = signals.take_all("loaded filled")
        with nc.Block() as block:
            @block.sync
            def _(sp):
                for dst, src in loads:
                    sp.dma_start(dst, src, allow_slow_non_contiguous=True).then_inc(loaded, 16)
                sp.wait_ge(loaded, 16 * len(loads))

            @block.gpsimd
            def _(pool):
                pool.memset(minus_half[:, :], -0.5).then_inc(filled, 1)
                for e in range(E_ROUTED):
                    pool.memset(rank[:, e:e + 1], float(E_ROUTED - e)).then_inc(filled, 1)
                pool.wait_ge(filled, 1 + E_ROUTED)

        (z_ok, x4_raw, ms_ok, x4_ok, meps_ok, rrms_ok, x4n_ok, hT_raw, x4T_raw, hT_ok, x4T_ok, router_raw, link,
         shifted_ok, gexp_ok, inv_ok, gate_ok) = signals.take_all(
            "z_ok x4_raw ms_ok x4_ok meps_ok rrms_ok x4n_ok hT_raw x4T_raw hT_ok x4T_ok router_raw link "
            "shifted_ok gexp_ok inv_ok gate_ok", NS)
        with nc.Block() as block:
            @block.gpsimd
            def _(pool):
                with pool.Fori(0, PAIRS) as i:
                    for s in range(NS):
                        pool.wait_ge(meps_ok[s], i + 1)
                        pool.tensor_tensor(rrms[s][:, :], meps[s][:, :], minus_half[:, :], ALU.pow).then_inc(rrms_ok[s], 1)

            @block.tensor
            def _(pe):
                with pe.Fori(0, PAIRS) as i:
                    n = i + 1
                    for s in range(NS):
                        pe.wait_ge(z_ok[s], NH * n)
                        for b in range(GB):
                            for h in range(NH):
                                mm = pe.matmul(PS[:, 4 * s, b * D:(b + 1) * D], z[s][:, h, b * S:(b + 1) * S], w_outT[:, h, :],
                                               start=(h == 0), stop=(h == 1))
                        mm.then_inc(x4_raw[s], 1)
                    for s in range(NS):
                        pe.wait_ge(x4_ok[s], n)
                        for b in range(GB):
                            mm = pe.transpose(PS[:, 4 * s + 2, b * S:(b + 1) * S], x4[s][:, b, :], ident[:, :])
                        mm.then_inc(x4T_raw[s], 1)
                    for s in range(NS):
                        pe.wait_ge(x4n_ok[s], n)
                        for b in range(GB):
                            mm = pe.transpose(PS[:, 4 * s + 1, b * S:(b + 1) * S], x4n[s][:, b, :], ident[:, :])
                        mm.then_inc(hT_raw[s], 1)
                    for s in range(NS):
                        pe.wait_ge(x4T_ok[s], n)
                        for b in range(GB):
                            mm = pe.matmul(PS[:, 4 * s + 3, b * 16:b * 16 + E_ROUTED], x4T[s][:, b * S:(b + 1) * S], router[:, :],
                                           start=True, stop=True)
                        mm.then_inc(router_raw[s], 1)

            @block.scalar
            def _(act):
                with act.Fori(0, PAIRS) as i:
                    n = i + 1
                    for s in range(NS):
                        act.wait_ge(x4_raw[s], n)
                        for b in range(GB):
                            ins = act.activation(junk[s][:, :], PS[:, 4 * s, b * D:(b + 1) * D], ACT.Square, accum_out=ms[s][:, b:b + 1])
                            ins.then_inc(ms_ok[s], 1)
                            act.wait_ge(ms_ok[s], i * GB + (b + 1))
                        act.activation(x4[s][:, :, :], PS[:, 4 * s, :], ACT.Copy).then_inc(x4_ok[s], 1)
                    for s in range(NS):
                        act.wait_ge(x4T_raw[s], n)
                        act.activation(x4T[s][:, :], PS[:, 4 * s + 2, :], ACT.Copy).then_inc(x4T_ok[s], 1)
                    for s in range(NS):
                        act.wait_ge(hT_raw[s], n)
                        act.activation(hT[:, bass.ds((i * NS + s) * GT, GT)], PS[:, 4 * s + 1, :], ACT.Copy).then_inc(hT_ok[s], 1)
                    for s in range(NS):
                        act.wait_ge(shifted_ok[s], n)
                        act.activation(wide["gexp"][s][:, :, :], wide["shifted"][s][:, :, :], ACT.Exp).then_inc(gexp_ok[s], 1)
                for s in range(NS):
                    act.wait_ge(hT_ok[s], PAIRS)

            @block.vector
            def _(dve):
                LINKS = 4 + 11 + 4

                def spread(v):
                    return v[:, :].unsqueeze(2).to_broadcast([S, GB, E_ROUTED])

                with dve.Fori(0, PAIRS) as i:
                    n = i + 1
                    for s in range(NS):
                        at = (i * NS + s) * GT
                        for h in range(NH):
                            dve.tensor_tensor(z[s][:, h, :], yT[:, h, bass.ds(at, GT)], gateT[:, h, bass.ds(at, GT)], ALU.mult).then_inc(z_ok[s], 1)
                    for s in range(NS):
                        dve.wait_ge(ms_ok[s], GB * n)
                        dve.tensor_scalar(meps[s][:, :], ms[s][:, :], 1.0 / D, RMS_EPS, ALU.mult, ALU.add).then_inc(meps_ok[s], 1)
                    for s in range(NS):
                        dve.wait_ge(x4_ok[s], n)
                        dve.wait_ge(rrms_ok[s], n)
                        dve.tensor_tensor(x4n[s][:, :, :], x4[s][:, :, :], rrms[s][:, :].unsqueeze(2).to_broadcast([S, GB, D]),
                                          ALU.mult).then_inc(x4n_ok[s], 1)
                    for s in range(NS):
                        count = [0]

                        def step(ins):
                            count[0] += 1
                            ins.then_inc(link[s], 1)
                            dve.wait_ge(link[s], i * LINKS + count[0])

                        w = {k: v[s] for k, v in wide.items()}
                        m = {k: v[s] for k, v in small.items()}
                        dve.wait_ge(router_raw[s], n)
                        logits = PS[:, 4 * s + 3, 0:GB * 16].rearrange("p (b e) -> p b e", e=16)[:, :, 0:E_ROUTED]
                        step(dve.tensor_reduce(m["lmax"][:, :], logits, AX.X, ALU.max))
                        dve.tensor_tensor(w["shifted"][:, :, :], logits, spread(m["lmax"]), ALU.subtract).then_inc(shifted_ok[s], 1)
                        dve.wait_ge(gexp_ok[s], n)
                        step(dve.tensor_reduce(m["gsum"][:, :], w["gexp"][:, :, :], AX.X, ALU.add))
                        step(dve.reciprocal(m["ginv"][:, :], m["gsum"][:, :]))
                        step(dve.tensor_tensor(w["g"][:, :, :], w["gexp"][:, :, :], spread(m["ginv"]), ALU.mult))
                        rank_all = rank[:, :].unsqueeze(1).to_broadcast([S, GB, E_ROUTED])
                        for source, found in (("g", "first"), ("rest", "second")):
                            step(dve.tensor_reduce(m["top"][:, :], w[source][:, :, :], AX.X, ALU.max))
                            step(dve.tensor_tensor(w["same"][:, :, :], w[source][:, :, :], spread(m["top"]), ALU.is_equal))
                            step(dve.tensor_tensor(w["ranked"][:, :, :], w["same"][:, :, :], rank_all, ALU.mult))
                            step(dve.tensor_reduce(m["pick"][:, :], w["ranked"][:, :, :], AX.X, ALU.max))
                            step(dve.tensor_tensor(w[found][:, :, :], w["ranked"][:, :, :], spread(m["pick"]), ALU.is_equal))
                            if found == "first":
                                step(dve.scalar_tensor_tensor(out=w["rest"][:, :, :], in0=w["first"][:, :, :], scalar=-2.0,
                                                              in1=w["g"][:, :, :], op0=ALU.mult, op1=ALU.add))
                        step(dve.tensor_tensor(w["both"][:, :, :], w["first"][:, :, :], w["second"][:, :, :], ALU.add))
                        step(dve.tensor_tensor(w["kept"][:, :, :], w["both"][:, :, :], w["g"][:, :, :], ALU.mult))
                        step(dve.tensor_reduce(m["msum"][:, :], w["kept"][:, :, :], AX.X, ALU.add))
                        dve.tensor_scalar(m["msum_eps"][:, :], m["msum"][:, :], GATE_EPS, None, ALU.add).then_inc(link[s], 1)
                        count[0] += 1
                        dve.wait_ge(link[s], i * LINKS + count[0])
                        dve.reciprocal(m["minv"][:, :], m["msum_eps"][:, :]).then_inc(inv_ok[s], 1)
                        dve.wait_ge(inv_ok[s], n)
                        dve.tensor_tensor(gate[:, bass.ds((i * NS + s) * GB, GB), :], w["kept"][:, :, :], spread(m["minv"]),
                                          ALU.mult).then_inc(gate_ok[s], 1)
                        assert count[0] == LINKS, count[0]
                for s in range(NS):
                    dve.wait_ge(gate_ok[s], PAIRS)
        signals.clear()


def experts_phase(nc, a, K, out):
    import concourse.bass as bass
    from concourse import mybir
    from contextlib import ExitStack
    f32 = mybir.dt.float32
    ALU, ACT = mybir.AluOpType, mybir.ActivationFunctionType
    NHID = HIDDEN // 128
    with ExitStack() as ctx:
        def sb(name, shape, dt=f32):
            return ctx.enter_context(nc.sbuf_tensor(name, shape, dt))

        signals = Signals(nc, ctx, "moe")
        PS, hT, gate, x3_tok = (K[n] for n in ("PS", "hT", "gate", "x3_tok"))
        w1, w2 = sb("w1", [D, NE, HIDDEN]), sb("w2", [128, NE, NHID, D])
        rms_wT = sb("rms_wT", [D, NE])
        act_out = [sb(f"act_out{k}", [128, NHID, GT]) for k in range(2)]
        gate_now = sb("gate_now", [S, GB, E_ROUTED])
        total = [sb(f"total{k}", [S, GB, D]) for k in range(2)]
        loads = [(w1[:, :, :], a["w1"].rearrange("e d f -> d e f")), (rms_wT[:, :], a["rms_wT"]),
                 (w2[:, :, :, :], a["w2"].rearrange("e (h p) d -> p e h d", p=128))]
        loaded, scaled = signals.take_all("loaded scaled")
        up_raw, silu_ok, down_raw, sum_ok, stored = signals.take_all("up_raw silu_ok down_raw sum_ok stored")
        gates_here = signals.take("gates_here")
        with nc.Block() as block:
            @block.sync
            def _(sp):
                for dst, src in loads:
                    sp.dma_start(dst, src).then_inc(loaded, 16)
                sp.wait_ge(loaded, 16 * len(loads))
                for s in (silu_ok, down_raw, sum_ok):
                    sp.sem_inc(s, 2)

            @block.vector
            def _(dve):
                dve.wait_ge(loaded, 16 * len(loads))
                for e in range(NE):
                    dve.tensor_scalar(w1[:, e, :], w1[:, e, :], rms_wT[:, e:e + 1], None, ALU.mult).then_inc(scaled, 1)
                dve.wait_ge(scaled, NE)

        with nc.Block() as block:
            @block.tensor
            def _(pe):
                def up(g, e):
                    pe.wait_ge(silu_ok, g * NE + (e + 1))
                    for h in range(NHID):
                        mm = pe.matmul(PS[:, 2 * (e % 2) + h, :], w1[:, e, h * 128:(h + 1) * 128], hT[:, bass.ds(g * GT, GT)],
                                       start=True, stop=True)
                    mm.then_inc(up_raw, 1)

                def down(g, e):
                    pe.wait_ge(silu_ok, g * NE + (e + 3))
                    pe.wait_ge(sum_ok, g * NE + (e + 1))
                    for b in range(GB):
                        for h in range(NHID):
                            mm = pe.matmul(PS[:, 4 + e % 2, b * D:(b + 1) * D], act_out[e % 2][:, h, b * S:(b + 1) * S], w2[:, e, h, :],
                                           start=(h == 0), stop=(h == NHID - 1))
                    mm.then_inc(down_raw, 1)

                with pe.Fori(0, NG) as g:
                    up(g, 0)
                    for e in range(1, NE):
                        up(g, e)
                        down(g, e - 1)
                    down(g, NE - 1)

            @block.scalar
            def _(act):
                with act.Fori(0, NG) as g:
                    for e in range(NE):
                        act.wait_ge(up_raw, g * NE + (e + 1))
                        act.wait_ge(down_raw, g * NE + (e + 1))
                        act.activation(act_out[e % 2][:, :, :], PS[:, 2 * (e % 2):2 * (e % 2) + 2, :], ACT.Silu).then_inc(silu_ok, 1)

            @block.vector
            def _(dve):
                with dve.Fori(0, NG) as g:
                    dve.wait_ge(sum_ok, g * NE + 2)
                    dve.tensor_scalar(gate_now[:, :, :], gate[:, bass.ds(g * GB, GB), :], 1.0, None, ALU.mult).then_inc(gates_here, 1)
                    dve.wait_ge(gates_here, g + 1)
                    for e in range(NE):
                        dve.wait_ge(sum_ok, g * NE + (e + 2))
                        dve.wait_ge(down_raw, g * NE + (e + 3))
                        if e < E_ROUTED:
                            for b in range(GB):
                                prior = x3_tok[:, bass.ds(g * GB + b, 1), :].rearrange("p o d -> p (o d)") if e == 0 else total[(e - 1) % 2][:, b, :]
                                ins = dve.scalar_tensor_tensor(out=total[e % 2][:, b, :], in0=PS[:, 4 + e % 2, b * D:(b + 1) * D],
                                                               scalar=gate_now[:, b, e:e + 1], in1=prior, op0=ALU.mult, op1=ALU.add)
                        else:
                            into = x3_tok[:, bass.ds(g * GB, GB), :] if e == NE - 1 else total[e % 2][:, :, :]
                            ins = dve.tensor_tensor(into, PS[:, 4 + e % 2, :].rearrange("p (b d) -> p b d", b=GB),
                                                    total[(e - 1) % 2][:, :, :], ALU.add)
                        ins.then_inc(sum_ok, 1)

            @block.sync
            def _(sp):
                with sp.Fori(0, NG) as g:
                    sp.wait_ge(sum_ok, g * NE + (NE + 2))
                    sp.dma_start(out[bass.ds(g * GB, GB), :, :].rearrange("b s d -> s b d"), x3_tok[:, bass.ds(g * GB, GB), :]).then_inc(stored, 16)
                sp.wait_ge(stored, 16 * NG)
        signals.clear()


def constants_phase(nc, K):
    from concourse import mybir
    from contextlib import ExitStack
    ALU = mybir.AluOpType
    with ExitStack() as ctx:
        signals = Signals(nc, ctx, "constants")
        zeroed, made = signals.take_all("zeroed made")
        with nc.Block() as block:
          @block.gpsimd
          def _(pool):
            pool.memset(K["ident"][:, :], 0.0).then_inc(zeroed, 1)
            pool.memset(K["ones_row"][:, :], 1.0).then_inc(made, 1)
            pool.wait_ge(zeroed, 1)
            pool.affine_select(out=K["ident"][:, :], in_=K["ident"][:, :], compare_op=ALU.not_equal, fill=1.0, base=0,
                               pattern=[[-1, 128]], channel_multiplier=1).then_inc(made, 1)
            pool.wait_ge(made, 2)
        signals.clear()


def build(nc, a, out, stop="all"):
    from concourse import mybir
    from contextlib import ExitStack
    f32 = mybir.dt.float32
    with ExitStack() as ctx:
        def sb(name, shape, dt=f32):
            return ctx.enter_context(nc.sbuf_tensor(name, shape, dt))
        K = {n: a[n] for n in ("xn_d", "bd_d", "c_d", "ad_d")}
        K |= {"PS": ctx.enter_context(nc.psum_tensor("PS", [128, 8, 512], f32)),
             "ident": sb("ident", [128, 128]), "ones_row": sb("ones_row", [1, 128]),
             "cond_tok": sb("cond_tok", [S, B, D])}
        constants_phase(nc, K)
        edge_phase(nc, a, K)
        if stop != "edge":
            K["x3_tok"], K["x3T"] = K["cond_tok"], sb("x3T", [D, B * S])
            attention_phase(nc, a, K)
            if stop != "attention":
                K["gateT"], K["xnT"] = sb("gateT", [128, NH, B * S]), sb("xnT", [128, NH, B * S])
                scan_inputs_phase(nc, a, K)
                scan_phase(nc, a, K)
                K["hT"], K["gate"] = K["x3T"], sb("gate", [S, B, E_ROUTED])
                expert_inputs_phase(nc, a, K)
                experts_phase(nc, a, K, out)
        if stop in ("edge", "attention"):
            with nc.semaphore("dumped") as dumped, nc.Block() as block:
                @block.sync
                def _(sp):
                    sp.dma_start(out.rearrange("b s d -> s b d"), K["cond_tok" if stop == "edge" else "x3_tok"][:, :, :]).then_inc(dumped, 16)
                    sp.wait_ge(dumped, 16)


def kernel(**inputs):
    import numpy as np
    import concourse.bacc as bacc
    from concourse import mybir
    from concourse.bass_utils import run_bass_kernel_spmd

    L = {k.replace("L0_", ""): np.asarray(v) for k, v in inputs.items()}
    x = L["x"].reshape(B * S, D)
    arrays = {
        "xT": x.T, "adj": L["itok_BxSxS_0_4"], "mask": L["mask_BxS_ff1"], "qeT": L["fside_BxS_0"].T,
        "b_qtT": L["mask_BxS_ff0"][:T_ITER].T, "w_qtT": L["fside_BxSxS_0"][:T_ITER].transpose(0, 2, 1),
        "condT": L["cond_2048"].T,
        "w_qinT": L["cond_w_qin"].T, "w_plT": L["cond_w_pl"].T, "w_pcT": L["cond_w_pc"].T, "w_pkT": L["cond_w_pk"].T,
        "w_pvT": L["cond_w_pv"].T, "w_q": L["cond_w_q"], "w_k": L["cond_w_k"], "w_vT": L["cond_w_v"].T,
        "w_muT": L["cond_w_mu"].T, "w_cbT": L["cond_w_cb"].T,
        "bias": np.stack([L["cond_" + n] for n in ("b_qin", "b_pl", "b_pc", "b_q", "b_k", "b_pk", "b_pv", "b_mu")]
                         + [L["cond_init_mem"][0], L["cond_b_v"]], axis=1),
        "x": L["x"],
        "w_inT": L["cond2_W_in"].T, "taps": L["cond2_W_conv"][:, 0, :], "b_conv": L["cond2_b_conv"],
        "ln_g": L["cond2_ln_g"], "ln_b": L["cond2_ln_b"], "w_xpT": L["cond2_W_xproj"].T, "w_dtT": L["cond2_W_dt"].T,
        "state_cols": np.stack([L["cond2_b_dt"], L["cond2_A_log"]], axis=1), "D": L["cond2_D"],
        "w_outT": L["cond2_W_out"].T, "router": L["ffn_router_w"],
        "w1": np.concatenate([L["ffn_w1"], L["ffn_w1_s"]]), "w2": np.concatenate([L["ffn_w2"], L["ffn_w2_s"]]),
        "rms_wT": np.concatenate([L["ffn_rms_w"], L["ffn_rms_w_s"]]).T,
        "qkv_KT": np.concatenate([L[f"attn_{n}K"].T for n in "qkv"], axis=1),
        "qkv_V": np.stack([L[f"attn_{n}V"] for n in "qkv"]),
        "p_KT": L["attn_pK"].T, "p_V": L["attn_pV"], "f_KT": L["attn_fK"].T, "f_V": L["attn_fV"],
        "b_cb": L["cond_b_cb"],
    }
    nc = bacc.Bacc("TRN2", target_bir_lowering=False, num_devices=1)
    given, aps = {}, {}
    for name, v in arrays.items():
        v = np.ascontiguousarray(v)
        given[f"in_{name}"] = v
        aps[name] = nc.dram_tensor(f"in_{name}", v.shape, mybir.dt.from_np(v.dtype), kind="ExternalInput").ap()
    out = nc.dram_tensor("out_0", (B, S, D), mybir.dt.float32, kind="ExternalOutput").ap()
    for name, shape in (("xn_d", (B, S, DI)), ("bd_d", (B, S, N_STATE)), ("c_d", (B, N_STATE, S)), ("ad_d", (B, N_STATE, S))):
        aps[name] = nc.dram_tensor(name, shape, mybir.dt.float32, kind="Internal").ap()
    build(nc, aps, out, STOP)
    r = run_bass_kernel_spmd(nc, [given], core_ids=[0])
    return r.results[0]["out_0"]


STOP = "all"
```

```python
import math

B, S, D = 32, 128, 128
T_ITER, TYPES = 4, 4
ALPHA = 0.2
NO_EDGE = -9000000000000000.0
SERIES = 10
LN2_HIGH = 0.693359375
LN2_LOW = math.log(2.0) - LN2_HIGH
EXP_LOW = -60.0
LN_EPS = 1e-5
HEADS = 16
HD = D // HEADS
NF = 512
P_SCALE = float(D) ** -0.5
CAUSAL = -1e30
DI = 256
NH = DI // 128
N_STATE = 16
N_TAPS = 4
CLIP = 10.0
E_ROUTED, E_SHARED, HIDDEN = 14, 2, 256
NE = E_ROUTED + E_SHARED
RMS_EPS = 1.1920929e-07
GATE_EPS = 1e-9
GB = 4
GT = GB * S
NG = B // GB


class Signals:

    def __init__(self, nc, ctx, phase):
        self.nc, self.ctx, self.phase, self.taken = nc, ctx, phase, []

    def take(self, name, n=None):
        got = [self.ctx.enter_context(self.nc.semaphore(f"{self.phase}_{name}{i}")) for i in range(n or 1)]
        self.taken += got
        return got if n else got[0]

    def take_all(self, names, n=None):
        return [self.take(name, n) for name in names.split()]

    def clear(self):
        nums, runs = sorted(s.num for s in self.taken), []
        for k in nums:
            if runs and runs[-1][1] == k:
                runs[-1][1] = k + 1
            else:
                runs.append([k, k + 1])
        with self.nc.Block() as block:
            @block.sync
            def _(sp):
                for low, high in runs:
                    sp.sem_clear(range(low, high))


def edge_phase(nc, a, K):
    import concourse.bass as bass
    from concourse import mybir
    from contextlib import ExitStack
    f32, i32 = mybir.dt.float32, mybir.dt.int32
    ALU, ACT, AX = mybir.AluOpType, mybir.ActivationFunctionType, mybir.AxisListType
    ctx = ExitStack()
    NS = 4
    EB = 2
    ET = EB * S
    TURNS = B // (NS * EB)
    X = [2 * s for s in range(NS)]
    Y = [2 * s + 1 for s in range(NS)]
    with ctx:
        def sb(name, shape, dt=f32):
            return ctx.enter_context(nc.sbuf_tensor(name, shape, dt))

        signals = Signals(nc, ctx, "edge")
        sem = signals.take

        PS = K["PS"]
        ident, ones_row = K["ident"], K["ones_row"]
        xT, adj, mask = sb("xT", [D, B * S]), sb("adj", [S, B, S], i32), sb("mask", [D, B * S])
        w_plT, w_pcT, w_qinT = sb("w_plT", [D, D]), sb("w_pcT", [D, D]), sb("w_qinT", [D, D])
        w_pkT, w_pvT = sb("w_pkT", [D, D]), sb("w_pvT", [D, D])
        w_q, w_k, w_vT = sb("w_q", [D, 3 * D]), sb("w_k", [D, 3 * D]), sb("w_vT", [D, 3, D])
        w_muT, w_cbT = sb("w_muT", [D, 2, D]), sb("w_cbT", [D, 2, D])
        w_qtT, qeT = sb("w_qtT", [D, T_ITER, D]), sb("qeT", [D, B])
        b_qtT, wesT = sb("b_qtT", [D, T_ITER]), sb("wesT", [D, 2, B])
        bias = sb("bias", [D, 10])
        rows = sb("rows", [1, D])
        b_qin, b_pl, b_pc, b_q, b_k, b_pk, b_pv, b_mu, init, b_v = (bias[:, n:n + 1] for n in range(10))
        b_cb = rows[0:1, :]
        q_lin, q_neg, q_exp, q_pos, q_base, q_round, q_rest = (
            sb(n, [D, B]) for n in ("q_lin", "q_neg", "q_exp", "q_pos", "q_base", "q_round", "q_rest"))
        q_int = sb("q_int", [D, B], i32)
        cmd, pk, pv = (sb(n, [D, T_ITER, B]) for n in ("cmd", "pk", "pv"))
        w2pk = sb("w2pk", [D, T_ITER * B, TYPES])
        edge_w = sb("edge_w", [D, 3, T_ITER * B, 2 * TYPES])
        edge_b = sb("edge_b", [S, T_ITER * B, 2 * TYPES])
        def per(name, shape):
            return [sb(f"{name}{s}", shape) for s in range(NS)]

        xg, plT, mT, xcT, xctxT, msgT = (per(n, [D, ET]) for n in ("xg", "plT", "mT", "xcT", "xctxT", "msgT"))
        is_type, scored = per("is_type", [S, EB, TYPES, S]), per("scored", [S, EB, TYPES, S])
        lifted, half = per("lifted", [S, EB, 2, S]), per("half", [S, EB, 2, S])
        no_edge, edge, logit, prob, probT = (per(n, [S, EB, S]) for n in ("no_edge", "edge", "logit", "prob", "probT"))
        v_tok, ac = per("v_tok", [S, EB, D]), per("ac", [S, EB, 2 * TYPES])
        VAC = D + 2 * TYPES
        w_vac = per("w_vac", [D, EB, 3, VAC])
        neg_max, row_sum, inv_sum = (per(n, [S, EB]) for n in ("neg_max", "row_sum", "inv_sum"))
        cond_tok = K["cond_tok"]

        loads = [(w_qinT[:, :], a["w_qinT"]), (qeT[:, :], a["qeT"]), (bias[:, :], a["bias"]),
                 (w_qtT[:, :, :], a["w_qtT"].rearrange("t i o -> i t o")), (b_qtT[:, :], a["b_qtT"]),
                 (w_pkT[:, :], a["w_pkT"]), (w_pvT[:, :], a["w_pvT"]),
                 (wesT[:, :, :], a["condT"].rearrange("(h p) b -> p h b", p=D)),
                 (w_q[:, :], a["w_q"]), (w_k[:, :], a["w_k"]),
                 (rows[0:1, :], a["b_cb"].rearrange("(o d) -> o d", o=1))]
        loads2 = [(xT[:, :], a["xT"]), (adj[:, :, :], a["adj"].rearrange("b i j -> i b j")),
                  (mask[:, :], a["mask"].rearrange("(o b) s -> o (b s)", o=1).partition_broadcast(D)),
                  (w_plT[:, :], a["w_plT"]), (w_pcT[:, :], a["w_pcT"]),
                  (w_vT[:, :, :], a["w_vT"].rearrange("(c p) o -> p c o", p=D)),
                  (w_muT[:, :, :], a["w_muT"].rearrange("(c p) o -> p c o", p=D)),
                  (w_cbT[:, :, :], a["w_cbT"].rearrange("(c p) o -> p c o", p=D))]

        small_in, big_in = sem("small_in"), sem("big_in")
        q_lin_raw, q_lin_ok, q_step, q_ok = (sem(n) for n in ("q_lin_raw", "q_lin_ok", "q_step", "q_ok"))
        cmd_raw, cmd_ok, pkv_raw, pkv_ok, w2pk_ok, tab_raw, tab_ok = (
            sem(n) for n in ("cmd_raw", "cmd_ok", "pkv_raw", "pkv_ok", "w2pk_ok", "tab_raw", "tab_ok"))

        w_vac_ok = sem("w_vac_ok")
        xc_ok = sem("xc_ok")

        with nc.Block() as block:
            @block.sync
            def _(sp):
                for dst, src in loads:
                    sp.dma_start(dst, src).then_inc(small_in, 16)
                for dst, src in loads2:
                    sp.dma_start(dst, src).then_inc(big_in, 16)
                sp.wait_ge(small_in, 16 * len(loads))
                sp.wait_ge(big_in, 16 * len(loads2))

            @block.tensor
            def _(pe):
                pe.wait_ge(small_in, 16 * len(loads))
                pe.matmul(PS[:, 0, 0:B], w_qinT[:, :], qeT[:, :], start=True, stop=True).then_inc(q_lin_raw, 1)
                pe.wait_ge(q_ok, 1)
                for t in range(T_ITER):
                    mm = pe.matmul(PS[:, 1, t * B:(t + 1) * B], w_qtT[:, t, :], q_base[:, :], start=True, stop=True)
                mm.then_inc(cmd_raw, 1)
                pe.wait_ge(cmd_ok, 1)
                pe.matmul(PS[:, 2, 0:T_ITER * B], w_pkT[:, :], cmd[:, :, :], start=True, stop=True)
                pe.matmul(PS[:, 3, 0:T_ITER * B], w_pvT[:, :], cmd[:, :, :], start=True, stop=True).then_inc(pkv_raw, 1)
                pe.wait_ge(w2pk_ok, 1)
                for c in range(3):
                    pe.matmul(PS[:, 4 + c, :], w_k[:, c * D:(c + 1) * D], w2pk[:, :, :], start=True, stop=True)
                    pe.matmul(PS[:, 0, c * TYPES:(c + 1) * TYPES], w_q[:, c * D:(c + 1) * D], wesT[:, 0, 0:TYPES],
                              start=True, stop=True)
                pe.matmul(PS[:, 7, :], b_k.to_broadcast([D, S]), w2pk[:, :, :], start=True, stop=True)
                pe.matmul(PS[:, 1, 0:TYPES], b_q.to_broadcast([D, S]), wesT[:, 0, 0:TYPES], start=True, stop=True).then_inc(tab_raw, 1)

            @block.scalar
            def _(act):
                act.wait_ge(big_in, 16 * len(loads2))
                for s in range(NS):
                    for b in range(EB):
                        act.activation(w_vac[s][:, b, :, 0:D], w_vT[:, :, :], ACT.Copy).then_inc(w_vac_ok, 1)
                act.wait_ge(w_vac_ok, NS * EB)

            @block.vector
            def _(dve):
                dve.wait_ge(small_in, 16 * len(loads))
                dve.wait_ge(q_lin_raw, 1)
                dve.tensor_scalar(q_lin[:, :], PS[:, 0, 0:B], b_qin, None, ALU.add).then_inc(q_lin_ok, 1)
                dve.wait_ge(q_lin_ok, 1)
                done = 0

                def step(ins):
                    nonlocal done
                    done += 1
                    ins.then_inc(q_step, 1)
                    dve.wait_ge(q_step, done)

                step(dve.tensor_scalar(q_pos[:, :], q_lin[:, :], 0.0, None, ALU.max))
                step(dve.tensor_scalar(q_neg[:, :], q_lin[:, :], 0.0, EXP_LOW, ALU.min, ALU.max))
                step(dve.tensor_scalar(q_int[:, :], q_neg[:, :], 1.0 / math.log(2.0), None, ALU.mult))
                step(dve.tensor_copy(q_round[:, :], q_int[:, :]))
                step(dve.scalar_tensor_tensor(out=q_rest[:, :], in0=q_round[:, :], scalar=-LN2_HIGH, in1=q_neg[:, :],
                                              op0=ALU.mult, op1=ALU.add))
                step(dve.scalar_tensor_tensor(out=q_rest[:, :], in0=q_round[:, :], scalar=-LN2_LOW, in1=q_rest[:, :],
                                              op0=ALU.mult, op1=ALU.add))
                step(dve.tensor_scalar(q_exp[:, :], q_rest[:, :], 1.0 / math.factorial(SERIES), None, ALU.mult))
                for k in range(SERIES - 1, 0, -1):
                    step(dve.scalar_tensor_tensor(out=q_exp[:, :], in0=q_exp[:, :], scalar=1.0 / math.factorial(k),
                                                  in1=q_rest[:, :], op0=ALU.add, op1=ALU.mult))
                step(dve.tensor_scalar(q_int[:, :], q_round[:, :], 127.0, float(2 ** 23), ALU.add, ALU.mult))
                two_k = q_int[:, :].bitcast(f32)
                step(dve.tensor_tensor(q_exp[:, :], q_exp[:, :], two_k, ALU.mult))
                step(dve.scalar_tensor_tensor(out=q_pos[:, :], in0=two_k, scalar=-1.0, in1=q_pos[:, :], op0=ALU.add, op1=ALU.add))
                dve.tensor_tensor(q_base[:, :], q_exp[:, :], q_pos[:, :], ALU.add).then_inc(q_ok, 1)
                dve.wait_ge(cmd_raw, 1)
                dve.tensor_tensor(cmd[:, :, :], PS[:, 1, 0:T_ITER * B].rearrange("p (t b) -> p t b", t=T_ITER),
                                  b_qtT[:, :].unsqueeze(2).to_broadcast([D, T_ITER, B]), ALU.add).then_inc(cmd_ok, 1)
                dve.wait_ge(pkv_raw, 1)
                dve.tensor_scalar(pk[:, :, :], PS[:, 2, 0:T_ITER * B], b_pk, None, ALU.add).then_inc(pkv_ok, 1)
                dve.tensor_scalar(pv[:, :, :], PS[:, 3, 0:T_ITER * B], b_pv, None, ALU.add).then_inc(pkv_ok, 1)
                dve.wait_ge(pkv_ok, 2)
                dve.tensor_tensor(w2pk[:, :, :], pk[:, :, :].rearrange("p t b -> p (t b)").unsqueeze(2)
                                  .to_broadcast([D, T_ITER * B, TYPES]),
                                  wesT[:, 1:2, 0:TYPES].to_broadcast([D, T_ITER * B, TYPES]), ALU.mult).then_inc(w2pk_ok, 1)
                dve.wait_ge(tab_raw, 1)
                for c in range(3):
                    dve.tensor_copy(edge_w[:, c, :, TYPES:2 * TYPES],
                                    PS[:, 4 + c, :].rearrange("p (n m) -> p n m", m=TYPES)).then_inc(tab_ok, 1)
                    dve.tensor_copy(edge_w[:, c, :, 0:TYPES],
                                    PS[:, 0:1, c * TYPES:(c + 1) * TYPES].to_broadcast([D, T_ITER * B, TYPES])).then_inc(tab_ok, 1)
                dve.tensor_copy(edge_b[:, :, TYPES:2 * TYPES],
                                PS[:, 7, :].rearrange("p (n m) -> p n m", m=TYPES)).then_inc(tab_ok, 1)
                dve.tensor_copy(edge_b[:, :, 0:TYPES],
                                PS[:, 1:2, 0:TYPES].to_broadcast([S, T_ITER * B, TYPES])).then_inc(tab_ok, 1)
                dve.wait_ge(tab_ok, 8)
                dve.sem_inc(xc_ok, NS)

        (x_ok, pl_raw, pl_ok, types_ok, combined_raw, group_done, pc_raw, m_ok, v_raw, v_ok, ac_ok, c_raw, lifted_ok,
         late_ok, early_ok, half_ok, edge_ok, open_ok, relu_ok, max_ok, exp_ok, inv_ok, prob_ok, probT_raw, probT_ok,
         msg_raw, msg_ok, mu_raw, xctx_ok, columns_ok) = signals.take_all(
            "x_ok pl_raw pl_ok types_ok combined_raw group_done pc_raw m_ok v_raw v_ok ac_ok c_raw lifted_ok "
            "late_ok early_ok half_ok edge_ok open_ok relu_ok max_ok exp_ok inv_ok prob_ok probT_raw probT_ok "
            "msg_raw msg_ok mu_raw xctx_ok columns_ok")

        def turn(i, s):
            return i * NS + (s + 1)

        def xc_count(i, s, t):
            return i * ((T_ITER + 1) * NS) + t * NS + (NS + s + 1)

        def types(i, s):
            return i * (NS * (TYPES + 1)) + (s + 1) * (TYPES + 1)

        def round_(i, t, s):
            return i * (T_ITER * NS) + t * NS + (s + 1)

        EARLY, LATE = (0, 1), (2, 3)

        with nc.Block() as block:
            @block.tensor
            def _(pe):
                def head(i, t, pair):
                    for s in pair:
                        pe.wait_ge(xc_ok, xc_count(i, s, t))
                        pe.matmul(PS[:, Y[s], ET:2 * ET], w_pcT[:, :], xcT[s][:, :], start=True, stop=True).then_inc(pc_raw, 1)
                    for s in pair:
                        pe.wait_ge(columns_ok, round_(i, t, s))
                        pe.wait_ge(m_ok, round_(i, t, s))
                        joint = [xg[s], xcT[s], mT[s]]
                        for b in range(EB):
                            for c in range(3):
                                mm = pe.matmul(PS[:, X[s], b * VAC:(b + 1) * VAC], joint[c][:, b * S:(b + 1) * S], w_vac[s][:, b, c, :],
                                               start=(c == 0), stop=(c == 2))
                        mm.then_inc(v_raw, 1)
                    for s in pair:
                        pe.wait_ge(ac_ok, round_(i, t, s))
                        pe.wait_ge(v_ok, round_(i, t, s))
                        for b in range(EB):
                            for m in range(TYPES):
                                mm = pe.transpose(PS[:, (X, Y)[m // 2][s], (b * 2 + m % 2) * S:(b * 2 + m % 2 + 1) * S],
                                                  ac[s][:, b, TYPES + m:TYPES + m + 1].to_broadcast([S, S]), ident[:, :])
                        mm.then_inc(c_raw, 1)

                def tail(i, t, pair):
                    for s in pair:
                        pe.wait_ge(prob_ok, round_(i, t, s))
                        for b in range(EB):
                            mm = pe.transpose(PS[:, X[s], b * S:(b + 1) * S], prob[s][:, b, :], ident[:, :])
                        mm.then_inc(probT_raw, 1)
                    for s in pair:
                        pe.wait_ge(probT_ok, round_(i, t, s))
                        for b in range(EB):
                            mm = pe.matmul(PS[:, Y[s], b * S:(b + 1) * S], v_tok[s][:, b, :], probT[s][:, b, :],
                                           start=True, stop=True)
                        mm.then_inc(msg_raw, 1)
                        pe.matmul(PS[:, X[s], ET:2 * ET], w_muT[:, 0, :], xcT[s][:, :], start=True, stop=False)
                    for s in pair:
                        pe.wait_ge(msg_ok, round_(i, t, s))
                        pe.matmul(PS[:, X[s], ET:2 * ET], w_muT[:, 1, :], msgT[s][:, :], start=False, stop=True).then_inc(mu_raw, 1)

                with pe.Fori(0, TURNS) as i:
                    for s in range(NS):
                        pe.wait_ge(x_ok, turn(i, s))
                        pe.matmul(PS[:, X[s], 0:ET], w_plT[:, :], xg[s][:, :], start=True, stop=True).then_inc(pl_raw, 1)
                    head(i, 0, EARLY)
                    head(i, 0, LATE)
                    with pe.Fori(1, T_ITER) as t:
                        for pair in (EARLY, LATE):
                            tail(i, t - 1, pair)
                            head(i, t, pair)
                    for pair in (EARLY, LATE):
                        tail(i, T_ITER - 1, pair)
                    for s in range(NS):
                        pe.wait_ge(xctx_ok, turn(i, s))
                        for b in range(EB):
                            out = PS[:, Y[s], b * D:(b + 1) * D]
                            pe.matmul(out, ones_row[0:1, :], b_cb, start=True, stop=False)
                            pe.matmul(out, xg[s][:, b * S:(b + 1) * S], w_cbT[:, 0, :], start=False, stop=False)
                            mm = pe.matmul(out, xctxT[s][:, b * S:(b + 1) * S], w_cbT[:, 1, :], start=False, stop=True)
                        mm.then_inc(combined_raw, 1)

            @block.scalar
            def _(act):
                def set_columns(i, t, s):
                    act.activation(w_vac[s][:, :, :, D:VAC], edge_w[:, :, bass.ds(t * B + i * (NS * EB) + s * EB, EB), :]
                                   .rearrange("p c b m -> p b c m"), ACT.Copy).then_inc(columns_ok, 1)

                def keep_v(i, t, s):
                    act.wait_ge(ac_ok, round_(i, t, s))
                    act.activation(v_tok[s][:, :, :], PS[:, X[s], 0:EB * VAC].rearrange("p (b w) -> p b w", b=EB)[:, :, 0:D],
                                   ACT.Copy).then_inc(v_ok, 1)

                def lift(i, t, s):
                    act.wait_ge(c_raw, round_(i, t, s))
                    for b in range(EB):
                        for m in range(2):
                            ins = act.activation(lifted[s][:, b, m, :], PS[:, X[s], (b * 2 + m) * S:(b * 2 + m + 1) * S],
                                                 ACT.Identity, bias=ac[s][:, b, m:m + 1])
                    ins.then_inc(lifted_ok, 1)

                def exp(i, t, s):
                    act.wait_ge(max_ok, round_(i, t, s))
                    for b in range(EB):
                        ins = act.activation(prob[s][:, b, :], logit[s][:, b, :], ACT.Exp,
                                             bias=neg_max[s][:, b:b + 1], accum_out=row_sum[s][:, b:b + 1])
                    ins.then_inc(exp_ok, 1)

                def keep_probT(i, t, s):
                    act.wait_ge(probT_raw, round_(i, t, s))
                    act.activation(probT[s][:, :, :], PS[:, X[s], 0:ET], ACT.Copy).then_inc(probT_ok, 1)

                def beside(i, t_scores, scores, t, other):
                    for s in scores[:1]:
                        lift(i, t_scores, s)
                    for s in other:
                        keep_probT(i, t - 1, s)
                    for s in scores[1:]:
                        lift(i, t_scores, s)
                    for s in other:
                        set_columns(i, t, s)
                    for s, o in zip(scores, other):
                        exp(i, t_scores, s)
                        keep_v(i, t, o)

                with act.Fori(0, TURNS) as i:
                    for s in range(NS):
                        act.activation(xg[s][:, :], xT[:, bass.ds((i * NS + s) * ET, ET)], ACT.Copy).then_inc(x_ok, 1)
                    for s in range(NS):
                        set_columns(i, 0, s)
                    for s in EARLY:
                        keep_v(i, 0, s)
                    for s in EARLY:
                        lift(i, 0, s)
                    for s, o in zip(EARLY, LATE):
                        exp(i, 0, s)
                        keep_v(i, 0, o)
                    with act.Fori(1, T_ITER) as t:
                        beside(i, t - 1, LATE, t, EARLY)
                        beside(i, t, EARLY, t, LATE)
                    for s in LATE:
                        lift(i, T_ITER - 1, s)
                    for s in EARLY:
                        keep_probT(i, T_ITER - 1, s)
                    for s in LATE:
                        exp(i, T_ITER - 1, s)
                    for s in LATE:
                        keep_probT(i, T_ITER - 1, s)
                    for s in range(NS):
                        act.wait_ge(xc_ok, xc_count(i, s, T_ITER))
                        act.activation(xctxT[s][:, :], PS[:, X[s], ET:2 * ET], ACT.Identity, bias=b_mu).then_inc(xctx_ok, 1)
                    for s in range(NS):
                        act.wait_ge(combined_raw, turn(i, s))
                        act.activation(cond_tok[:, bass.ds((i * NS + s) * EB, EB), :],
                                       PS[:, Y[s], 0:ET].rearrange("p (b d) -> p b d", b=EB), ACT.Copy).then_inc(group_done, 1)
                act.wait_ge(group_done, TURNS * NS)

            @block.gpsimd
            def _(pool):
                def add_up(i, t, pair):
                    for s in pair:
                        pool.wait_ge(types_ok, types(i, s))
                        pool.wait_ge(lifted_ok, round_(i, t, s))
                        pool.tensor_tensor(scored[s][:, :, 0:2, :], lifted[s][:, :, :, :], is_type[s][:, :, 0:2, :], ALU.mult)\
                            .then_inc(early_ok, 1)
                        pool.wait_ge(early_ok, round_(i, t, s))
                        pool.wait_ge(late_ok, round_(i, t, s))
                        pool.tensor_tensor(half[s][:, :, :, :], scored[s][:, :, 0:2, :], scored[s][:, :, 2:4, :], ALU.add).then_inc(half_ok, 1)

                with pool.Fori(0, TURNS) as i:
                    add_up(i, 0, EARLY)
                    with pool.Fori(1, T_ITER) as t:
                        add_up(i, t - 1, LATE)
                        add_up(i, t, EARLY)
                    add_up(i, T_ITER - 1, LATE)

            @block.vector
            def _(dve):
                def mark_types(i, s):
                    groups = bass.ds((i * NS + s) * EB, EB)
                    for m in range(TYPES):
                        dve.tensor_scalar(is_type[s][:, :, m, :], adj[:, groups, :], float(m + 1), None, ALU.is_equal).then_inc(types_ok, 1)
                    dve.tensor_scalar(no_edge[s][:, :, :], adj[:, groups, :], 0.0, NO_EDGE, ALU.is_le, ALU.mult).then_inc(types_ok, 1)

                def multiply(i, t, s):
                    dve.wait_ge(pl_ok, turn(i, s))
                    dve.wait_ge(pc_raw, round_(i, t, s))
                    dve.scalar_tensor_tensor(out=mT[s][:, :], in0=PS[:, Y[s], ET:2 * ET], scalar=b_pc, in1=plT[s][:, :],
                                             op0=ALU.add, op1=ALU.mult).then_inc(m_ok, 1)

                def keep_ac(i, t, s):
                    dve.wait_ge(v_raw, round_(i, t, s))
                    dve.tensor_tensor(ac[s][:, :, :], PS[:, X[s], 0:EB * VAC].rearrange("p (b w) -> p b w", b=EB)[:, :, D:VAC],
                                      edge_b[:, bass.ds(t * B + i * (NS * EB) + s * EB, EB), :], ALU.add).then_inc(ac_ok, 1)

                def late_types(i, t, s):
                    dve.wait_ge(types_ok, types(i, s))
                    dve.wait_ge(ac_ok, round_(i, t, s))
                    dve.wait_ge(c_raw, round_(i, t, s))
                    for b in range(EB):
                        for m in (2, 3):
                            ins = dve.scalar_tensor_tensor(
                                out=scored[s][:, b, m, :], in0=PS[:, Y[s], (b * 2 + m - 2) * S:(b * 2 + m - 1) * S],
                                scalar=ac[s][:, b, m:m + 1], in1=is_type[s][:, b, m, :], op0=ALU.add, op1=ALU.mult)
                    ins.then_inc(late_ok, 1)

                def to_max(i, t, s):
                    dve.wait_ge(half_ok, round_(i, t, s))
                    dve.tensor_tensor(edge[s][:, :, :], half[s][:, :, 0, :], half[s][:, :, 1, :], ALU.add).then_inc(edge_ok, 1)
                    dve.wait_ge(edge_ok, round_(i, t, s))
                    dve.scalar_tensor_tensor(out=logit[s][:, :, :], in0=edge[s][:, :, :], scalar=ALPHA, in1=edge[s][:, :, :],
                                             op0=ALU.mult, op1=ALU.max).then_inc(relu_ok, 1)
                    dve.wait_ge(relu_ok, round_(i, t, s))
                    dve.tensor_tensor(logit[s][:, :, :], logit[s][:, :, :], no_edge[s][:, :, :], ALU.add).then_inc(open_ok, 1)
                    dve.wait_ge(open_ok, round_(i, t, s))
                    dve.tensor_reduce(neg_max[s][:, :], logit[s][:, :, :], AX.X, ALU.max, negate=True).then_inc(max_ok, 1)

                def to_prob(i, t, s):
                    dve.wait_ge(exp_ok, round_(i, t, s))
                    dve.reciprocal(inv_sum[s][:, :], row_sum[s][:, :]).then_inc(inv_ok, 1)
                    dve.wait_ge(inv_ok, round_(i, t, s))
                    dve.tensor_tensor(prob[s][:, :, :], prob[s][:, :, :],
                                      inv_sum[s][:, :].unsqueeze(2).to_broadcast([S, EB, S]), ALU.mult).then_inc(prob_ok, 1)

                def update(i, t, pair):
                    for s in pair:
                        dve.wait_ge(msg_raw, round_(i, t, s))
                        dve.scalar_tensor_tensor(out=msgT[s][:, :].rearrange("p (b j) -> p b j", b=EB),
                                                 in0=PS[:, Y[s], 0:ET].rearrange("p (b j) -> p b j", b=EB), scalar=b_v,
                                                 in1=pv[:, bass.ds(t, 1), bass.ds(i * (NS * EB) + s * EB, EB)]
                                                 .rearrange("p o b -> p (o b)").unsqueeze(2).to_broadcast([D, EB, S]),
                                                 op0=ALU.add, op1=ALU.mult).then_inc(msg_ok, 1)
                    for s in pair:
                        dve.wait_ge(mu_raw, round_(i, t, s))
                        dve.scalar_tensor_tensor(out=xcT[s][:, :], in0=PS[:, X[s], ET:2 * ET], scalar=b_mu,
                                                 in1=mask[:, bass.ds((i * NS + s) * ET, ET)], op0=ALU.add, op1=ALU.mult).then_inc(xc_ok, 1)

                def beside(i, t_scores, scores, t, other, first=False):
                    for s in scores:
                        late_types(i, t_scores, s)
                    if not first:
                        update(i, t - 1, other)
                    for s in other:
                        multiply(i, t, s)
                        if first:
                            mark_types(i, s)
                    for s in scores:
                        to_max(i, t_scores, s)
                    for s, o in zip(scores, other):
                        keep_ac(i, t, o)
                        to_prob(i, t_scores, s)

                with dve.Fori(0, TURNS) as i:
                    for s in range(NS):
                        g = i * NS + s
                        dve.wait_ge(xc_ok, xc_count(i, s, 0) - NS)
                        dve.tensor_scalar(xcT[s][:, :], mask[:, bass.ds(g * ET, ET)], init, None, ALU.mult).then_inc(xc_ok, 1)
                    for s in range(NS):
                        dve.wait_ge(pl_raw, turn(i, s))
                        dve.tensor_scalar(plT[s][:, :], PS[:, X[s], 0:ET], b_pl, None, ALU.add).then_inc(pl_ok, 1)
                    for s in EARLY:
                        multiply(i, 0, s)
                    for s in EARLY:
                        mark_types(i, s)
                    for s in EARLY:
                        keep_ac(i, 0, s)
                    beside(i, 0, EARLY, 0, LATE, first=True)
                    with dve.Fori(1, T_ITER) as t:
                        beside(i, t - 1, LATE, t, EARLY)
                        beside(i, t, EARLY, t, LATE)
                    for s in LATE:
                        late_types(i, T_ITER - 1, s)
                    update(i, T_ITER - 1, EARLY)
                    for s in LATE:
                        to_max(i, T_ITER - 1, s)
                    for s in LATE:
                        to_prob(i, T_ITER - 1, s)
                    update(i, T_ITER - 1, LATE)
        signals.clear()



def attention_phase(nc, a, K):
    import concourse.bass as bass
    from concourse import mybir
    from contextlib import ExitStack
    f32, bf16 = mybir.dt.float32, mybir.dt.bfloat16
    ALU, ACT, AX = mybir.AluOpType, mybir.ActivationFunctionType, mybir.AxisListType
    NS = 4
    TURNS = B // NS
    QUADS = HEADS // 4
    WIDE = HEADS * HD
    X = [2 * s for s in range(NS)]
    Y = [2 * s + 1 for s in range(NS)]
    with ExitStack() as ctx:
        def sb(name, shape, dt=f32):
            return ctx.enter_context(nc.sbuf_tensor(name, shape, dt))

        def per(name, shape):
            return [sb(f"{name}{s}", shape) for s in range(NS)]

        signals = Signals(nc, ctx, "attn")

        PS, ident, cond_tok, x3_tok, x3T = (K[n] for n in ("PS", "ident", "cond_tok", "x3_tok", "x3T"))
        x_tok = sb("x_tok", [S, B, D])
        qkv_KT, qkv_V = sb("qkv_KT", [D, 3 * D]), sb("qkv_V", [D, 3, D])
        p_KT, p_V = sb("p_KT", [D, D]), sb("p_V", [D, D])
        f_KT, f_V = sb("f_KT", [D, NF]), sb("f_V", [D, NF // 128, D])
        causal = sb("causal", [S, S])
        causal_bf, ident_bf = sb("causal_bf", [S, S], bf16), sb("ident_bf", [S, S], bf16)
        head16, head4, quad_rows = sb("head16", [D, HEADS]), sb("head4", [D, 4]), sb("quad_rows", [D, QUADS])
        minus_half, ones_wide = sb("minus_half", [S, 1]), sb("ones_wide", [S, HEADS, HD])
        stats, mv = sb("stats", [S, NS, 6]), sb("mv", [S, NS, 2])
        veps, rstd = sb("veps", [S, NS]), sb("rstd", [S, NS])
        stats2, mv2, veps2, rstd2 = per("stats2", [S, 6]), per("mv2", [S, 2]), per("veps2", [S, 1]), per("rstd2", [S, 1])
        h, hT, h2, h2T = per("h", [S, D]), per("hT", [D, S]), per("h2", [S, D]), per("h2T", [D, S])
        qkv_nmax, qkv_sum, qkv_inv = (per(n, [S, 3]) for n in ("qkv_nmax", "qkv_sum", "qkv_inv"))
        q_rows, k_heads = per("q_rows", [D, QUADS, S]), per("k_heads", [D, 4, S])
        v_wide = per("v_wide", [S, HEADS * WIDE + WIDE])
        weight, head_nmax, weightT = per("weight", [S, HEADS, S]), per("head_nmax", [S, HEADS]), per("weightT", [S, HEADS, S])
        head_sum, head_inv, inv_wide, inv_rows, oT = per("head_sum", [S, HEADS]), per("head_inv", [S, HEADS]), per("inv_wide", [S, HEADS, HD]), per("inv_rows", [D, S]), per("oT", [D, S])
        p_nmax, p_sum, p_inv = (per(n, [S, 1]) for n in ("p_nmax", "p_sum", "p_inv"))
        p_a, p_aT, x1 = per("p_a", [S, D]), per("p_aT", [D, S]), per("x1", [S, D])
        f_nmax, f_sum, f_inv = (per(n, [S, 1]) for n in ("f_nmax", "f_sum", "f_inv"))
        x2, x3 = per("x2", [S, D]), per("x3", [S, D])
        qkv_a, qkv_aT = [w[:, 0:3, :] for w in weight], [w[:, 0:3, :] for w in weightT]
        f_a, f_aT = [w[:, 4:8, :].rearrange("p j n -> p (j n)") for w in weight], [w[:, 4:8, :] for w in weightT]

        loads = [(qkv_KT[:, :], a["qkv_KT"]),
                 (qkv_V[:, :, :], a["qkv_V"].rearrange("j n c -> n j c")), (p_KT[:, :], a["p_KT"]),
                 (p_V[:, :], a["p_V"]), (f_KT[:, :], a["f_KT"]),
                 (f_V[:, :, :], a["f_V"].rearrange("(j n) c -> n j c", n=D))]
        loaded, filled, cut, made, x_loaded = signals.take_all("loaded filled cut made x_loaded")

        with nc.Block() as block:
            @block.sync
            def _(sp):
                for dst, src in loads:
                    sp.dma_start(dst, src).then_inc(loaded, 16)
                sp.dma_start(x_tok[:, :, :], a["x"].rearrange("b s d -> s b d")).then_inc(x_loaded, 16)
                sp.wait_ge(loaded, 16 * len(loads))

            @block.gpsimd
            def _(pool):
                pool.memset(causal[:, :], 0.0).then_inc(filled, 1)
                pool.memset(head16[:, :], float(HD) ** -0.5).then_inc(filled, 1)
                pool.memset(quad_rows[:, :], 1.0).then_inc(filled, 1)
                pool.memset(minus_half[:, :], -0.5).then_inc(filled, 1)
                pool.memset(ones_wide[:, :, :], 1.0).then_inc(filled, 1)
                for s in range(NS // 2):
                    pool.memset(v_wide[s][:, :], 0.0).then_inc(filled, 1)
                pool.wait_ge(filled, 5 + NS)
                pool.affine_select(out=causal[:, :], in_=causal[:, :], compare_op=ALU.is_ge, fill=CAUSAL, base=0,
                                   pattern=[[-1, S]], channel_multiplier=1).then_inc(cut, 1)
                for t, width, n in ((head16, HD, HEADS), (quad_rows, 4 * HD, QUADS)):
                    pool.affine_select(out=t[:, :], in_=t[:, :], compare_op=ALU.is_ge, fill=0.0, base=0,
                                       pattern=[[-width, n]], channel_multiplier=1).then_inc(cut, 1)
                pool.wait_ge(cut, 3)
                for t, width, n in ((head16, HD, HEADS), (quad_rows, 4 * HD, QUADS)):
                    pool.affine_select(out=t[:, :], in_=t[:, :], compare_op=ALU.is_ge, fill=0.0, base=width - 1,
                                       pattern=[[width, n]], channel_multiplier=-1).then_inc(cut, 1)

            @block.vector
            def _(dve):
                for s in range(NS // 2, NS):
                    dve.memset(v_wide[s][:, :], 0.0).then_inc(filled, 1)
                dve.wait_ge(cut, 5)
                dve.tensor_reduce(head4[:, :], head16[:, :].rearrange("p (r j) -> p j r", j=4), AX.X, ALU.add).then_inc(made, 1)
                dve.tensor_copy(causal_bf[:, :], causal[:, :]).then_inc(made, 1)
                dve.tensor_copy(ident_bf[:, :], ident[:, :]).then_inc(made, 1)
                dve.wait_ge(loaded, 16 * len(loads))
                for t in (qkv_KT, p_KT, f_KT):
                    dve.tensor_scalar(t[:, :], t[:, :], P_SCALE, None, ALU.mult).then_inc(made, 1)
                dve.wait_ge(made, 6)

        (st_ok, st_seen, mv_ok, veps_ok, rstd_ok, h_ok, hT_raw, hT_ok, qkv_raw, qkv_nmax_ok, qkv_exp, qkv_inv_ok,
         qkv_a_ok, qkv_aT_raw, qkv_aT_ok, proj_raw, v_ok, qk_ok, score_raw, hmax_ok, hexp_ok, hinv_ok, hwide_ok,
         wT_raw, wT_even, wT_odd, inv_raw, inv_ok, o_raw, oT_ok) = signals.take_all(
            "a_st_ok a_st_seen a_mv_ok a_veps_ok a_rstd_ok a_h_ok hT_raw hT_ok qkv_raw qkv_nmax_ok qkv_exp qkv_inv_ok "
            "qkv_a_ok qkv_aT_raw qkv_aT_ok proj_raw v_ok qk_ok score_raw hmax_ok hexp_ok hinv_ok hwide_ok "
            "wT_raw wT_even wT_odd inv_raw inv_ok o_raw oT_ok")
        (p_raw, p_nmax_ok, p_exp, p_aT_raw, p_aT_ok, p_out_raw, p_inv_ok, x1_ok,
         f_st_ok, f_st_seen, f_mv_ok, f_veps_ok, f_rstd_ok, h2_ok, h2T_raw, h2T_ok, f_raw, f_nmax_ok, f_exp, f_aT_raw,
         f_aT_ok, f_out_raw, f_inv_ok, x2_ok, x3_ok, x3T_raw, stored) = signals.take_all(
            "p_raw p_nmax_ok p_exp p_aT_raw p_aT_ok p_out_raw p_inv_ok x1_ok "
            "f_st_ok f_st_seen f_mv_ok f_veps_ok f_rstd_ok h2_ok h2T_raw h2T_ok f_raw f_nmax_ok f_exp f_aT_raw "
            "f_aT_ok f_out_raw f_inv_ok x2_ok x3_ok x3T_raw x3_stored")

        EARLY, LATE, NONE = (0, 1), (2, 3), ()

        def count(i, s, part=0, parts=1):
            return i * (parts * NS) + (s // 2 * 2 * parts + part * 2 + s % 2 + 1)

        with nc.Block() as block:
            @block.gpsimd
            def _(pool):
                def side_by_side(i, pair, j, other):
                    for s in pair:
                        pool.wait_ge(veps_ok, count(i, s))
                        pool.tensor_tensor(rstd[:, s:s + 1], veps[:, s:s + 1], minus_half[:, 0:1], ALU.pow).then_inc(rstd_ok, 1)
                    for s in other:
                        pool.wait_ge(f_veps_ok, count(j, s))
                        pool.tensor_tensor(rstd2[s][:, :], veps2[s][:, :], minus_half[:, 0:1], ALU.pow).then_inc(f_rstd_ok, 1)
                    for s in pair:
                        pool.wait_ge(hinv_ok, count(i, s))
                        pool.tensor_tensor(inv_wide[s][:, :, :], head_inv[s][:, :].unsqueeze(2).to_broadcast([S, HEADS, HD]),
                                           ones_wide[:, :, :], ALU.mult).then_inc(hwide_ok, 1)

                side_by_side(0, EARLY, 0, NONE)
                with pool.Fori(1, TURNS) as i:
                    side_by_side(i - 1, LATE, i - 1, EARLY)
                    side_by_side(i, EARLY, i - 1, LATE)
                side_by_side(TURNS - 1, LATE, TURNS - 1, EARLY)
                side_by_side(TURNS - 1, NONE, TURNS - 1, LATE)

            @block.tensor
            def _(pe):
                def turn_h(i, pair):
                    for s in pair:
                        pe.wait_ge(h_ok, count(i, s))
                        pe.transpose(PS[:, X[s], 0:S], h[s][:, :], ident[:, :]).then_inc(hT_raw, 1)

                def scores_qkv(i, pair):
                    for s in pair:
                        pe.wait_ge(hT_ok, count(i, s))
                        pe.matmul(PS[:, Y[s], 0:3 * D], hT[s][:, :], qkv_KT[:, :], start=True, stop=True).then_inc(qkv_raw, 1)

                def turn_qkv(i, pair):
                    for s in pair:
                        pe.wait_ge(qkv_a_ok, count(i, s))
                        for j in range(3):
                            mm = pe.transpose(PS[:, X[s], j * S:(j + 1) * S], qkv_a[s][:, j, :], ident[:, :])
                        mm.then_inc(qkv_aT_raw, 1)

                def project(i, pair):
                    for s in pair:
                        pe.wait_ge(qkv_aT_ok, count(i, s))
                        pe.matmul(PS[:, Y[s], 0:S], qkv_V[:, 0, :], qkv_aT[s][:, 0, :], start=True, stop=True)
                        pe.matmul(PS[:, Y[s], S:2 * S], qkv_V[:, 1, :], qkv_aT[s][:, 1, :], start=True, stop=True)
                        pe.matmul(PS[:, X[s], 0:S], qkv_aT[s][:, 2, :], qkv_V[:, 2, :], start=True, stop=True).then_inc(proj_raw, 1)

                def scores(i, pair, r):
                    for s in pair:
                        if r == 0:
                            pe.wait_ge(qk_ok, i * (2 * NS) + 2 * (s + 1))
                            pe.wait_ge(v_ok, count(i, s))
                        if r >= 2:
                            pe.wait_ge(hexp_ok, count(i, s, r - 2, QUADS))
                        bank = PS[:, (X, Y)[r % 2][s], :]
                        pe.matmul(bank, q_rows[s][:, r, :], k_heads[s][:, :, :], start=True, stop=False)
                        pe.matmul(bank, ident_bf[:, :], causal_bf[:, :].unsqueeze(1).to_broadcast([S, 4, S]), start=False,
                                  stop=True).then_inc(score_raw, 1)

                def turn_weights(i, pair, r):
                    for s in pair:
                        if r < 2:
                            pe.wait_ge(hexp_ok, count(i, s, r + 2, QUADS))
                        else:
                            pe.wait_ge((wT_even, wT_odd)[r % 2], count(i, s, 0, 2))
                        for j in range(4):
                            mm = pe.transpose(PS[:, (X, Y)[r % 2][s], j * S:(j + 1) * S], weight[s][:, 4 * r + j, :], ident[:, :])
                        mm.then_inc(wT_raw, 1)

                def heads(i, pair):
                    for s in pair:
                        pe.wait_ge(wT_odd, count(i, s, 1, 2))
                        pe.wait_ge(hwide_ok, count(i, s))
                        pe.transpose(PS[:, Y[s], 0:S], inv_wide[s][:, :, :].rearrange("p h d -> p (h d)"), ident[:, :])\
                          .then_inc(inv_raw, 1)
                        pe.wait_ge(wT_even, count(i, s, 1, 2))
                        for j in range(HEADS):
                            mm = pe.matmul(PS[:, X[s], 0:S], v_wide[s][:, j * WIDE:(j + 1) * WIDE], weightT[s][:, j, :],
                                           start=(j == 0), stop=(j == HEADS - 1))
                        mm.then_inc(o_raw, 1)

                def scores_p(i, pair):
                    for s in pair:
                        pe.wait_ge(oT_ok, count(i, s))
                        pe.matmul(PS[:, Y[s], 128:256], oT[s][:, :], p_KT[:, :], start=True, stop=True).then_inc(p_raw, 1)

                def turn_p(i, pair):
                    for s in pair:
                        pe.wait_ge(p_exp, count(i, s))
                        pe.transpose(PS[:, X[s], 128:256], p_a[s][:, :], ident[:, :]).then_inc(p_aT_raw, 1)

                def output_p(i, pair):
                    for s in pair:
                        pe.wait_ge(p_aT_ok, count(i, s))
                        pe.matmul(PS[:, Y[s], 256:384], p_aT[s][:, :], p_V[:, :], start=True, stop=True).then_inc(p_out_raw, 1)

                def turn_h2(i, pair):
                    for s in pair:
                        pe.wait_ge(h2_ok, count(i, s))
                        pe.transpose(PS[:, X[s], 256:384], h2[s][:, :], ident[:, :]).then_inc(h2T_raw, 1)

                def scores_f(i, pair):
                    for s in pair:
                        pe.wait_ge(h2T_ok, count(i, s))
                        pe.matmul(PS[:, Y[s], :], h2T[s][:, :], f_KT[:, :], start=True, stop=True).then_inc(f_raw, 1)

                def turn_f(i, pair):
                    for s in pair:
                        pe.wait_ge(f_exp, count(i, s))
                        for j in range(NF // 128):
                            mm = pe.transpose(PS[:, X[s], j * S:(j + 1) * S], f_a[s][:, j * S:(j + 1) * S], ident[:, :])
                        mm.then_inc(f_aT_raw, 1)

                def output_f(i, pair):
                    for s in pair:
                        pe.wait_ge(f_aT_ok, count(i, s))
                        for j in range(NF // 128):
                            mm = pe.matmul(PS[:, Y[s], 0:D], f_aT[s][:, j, :], f_V[:, j, :], start=(j == 0), stop=(j == 3))
                        mm.then_inc(f_out_raw, 1)

                def turn_x3(i, pair):
                    for s in pair:
                        pe.wait_ge(x3_ok, count(i, s))
                        pe.transpose(PS[:, Y[s], 256:384], x3[s][:, :], ident[:, :]).then_inc(x3T_raw, 1)

                def side_by_side(i, pair, j, other):
                    turn_h(i, pair)
                    heads(j, other[0:1])
                    scores_qkv(i, pair)
                    heads(j, other[1:2])
                    turn_qkv(i, pair)
                    project(i, pair)
                    scores_p(j, other)
                    scores(i, pair, 0)
                    turn_p(j, other)
                    scores(i, pair, 1)
                    output_p(j, other)
                    scores(i, pair, 2)
                    turn_h2(j, other)
                    scores(i, pair, 3)
                    scores_f(j, other)
                    turn_weights(i, pair, 0)
                    turn_weights(i, pair, 1)
                    turn_f(j, other)
                    turn_weights(i, pair, 2)
                    output_f(j, other)
                    turn_weights(i, pair, 3)
                    turn_x3(j, other)

                side_by_side(0, EARLY, 0, NONE)
                with pe.Fori(1, TURNS) as i:
                    side_by_side(i - 1, LATE, i - 1, EARLY)
                    side_by_side(i, EARLY, i - 1, LATE)
                side_by_side(TURNS - 1, LATE, TURNS - 1, EARLY)
                side_by_side(TURNS - 1, NONE, TURNS - 1, LATE)

            @block.scalar
            def _(act):
                def keep_hT(i, pair):
                    for s in pair:
                        act.wait_ge(hT_raw, count(i, s))
                        act.activation(hT[s][:, :], PS[:, X[s], 0:S], ACT.Copy).then_inc(hT_ok, 1)

                def exp_qkv(i, pair):
                    for s in pair:
                        act.wait_ge(qkv_nmax_ok, count(i, s))
                        for j in range(3):
                            ins = act.activation(qkv_a[s][:, j, :], PS[:, Y[s], j * D:(j + 1) * D], ACT.Exp,
                                                 bias=qkv_nmax[s][:, j:j + 1], accum_out=qkv_sum[s][:, j:j + 1])
                        ins.then_inc(qkv_exp, 1)

                def keep_qkvT(i, pair):
                    for s in pair:
                        act.wait_ge(qkv_aT_raw, count(i, s))
                        act.activation(qkv_aT[s][:, :, :], PS[:, X[s], 0:3 * S], ACT.Copy).then_inc(qkv_aT_ok, 1)

                def keep_v(i, pair):
                    for s in pair:
                        act.wait_ge(proj_raw, count(i, s))
                        columns = v_wide[s][:, :].rearrange("p (h w) -> p h w", w=WIDE + HD)[:, :, 0:HD]
                        act.activation(columns, PS[:, X[s], 0:S].rearrange("p (h d) -> p h d", d=HD), ACT.Copy).then_inc(v_ok, 1)

                def exp(i, pair, r):
                    for s in pair:
                        act.wait_ge(hmax_ok, count(i, s, r, QUADS))
                        for j in range(4):
                            k = 4 * r + j
                            ins = act.activation(weight[s][:, k, :], PS[:, (X, Y)[r % 2][s], j * S:(j + 1) * S], ACT.Exp,
                                                 bias=head_nmax[s][:, k:k + 1], accum_out=head_sum[s][:, k:k + 1])
                        ins.then_inc(hexp_ok, 1)

                def keep_weights(i, pair, r):
                    for s in pair:
                        act.wait_ge(wT_raw, count(i, s, r, QUADS))
                        act.activation(weightT[s][:, 4 * r:4 * r + 4, :], PS[:, X[s], :], ACT.Copy).then_inc(wT_even, 1)

                def keep_inv(i, pair):
                    for s in pair:
                        act.wait_ge(inv_raw, count(i, s))
                        act.activation(inv_rows[s][:, :], PS[:, Y[s], 0:S], ACT.Copy).then_inc(inv_ok, 1)

                def exp_p(i, pair):
                    for s in pair:
                        act.wait_ge(p_nmax_ok, count(i, s))
                        act.activation(p_a[s][:, :], PS[:, Y[s], 128:256], ACT.Exp, bias=p_nmax[s][:, 0:1],
                                       accum_out=p_sum[s][:, 0:1]).then_inc(p_exp, 1)

                def keep_pT(i, pair):
                    for s in pair:
                        act.wait_ge(p_aT_raw, count(i, s))
                        act.activation(p_aT[s][:, :], PS[:, X[s], 128:256], ACT.Copy).then_inc(p_aT_ok, 1)

                def keep_h2T(i, pair):
                    for s in pair:
                        act.wait_ge(h2T_raw, count(i, s))
                        act.activation(h2T[s][:, :], PS[:, X[s], 256:384], ACT.Copy).then_inc(h2T_ok, 1)

                def exp_f(i, pair):
                    for s in pair:
                        act.wait_ge(f_nmax_ok, count(i, s))
                        act.activation(f_a[s][:, :], PS[:, Y[s], :], ACT.Exp, bias=f_nmax[s][:, 0:1],
                                       accum_out=f_sum[s][:, 0:1]).then_inc(f_exp, 1)

                def keep_fT(i, pair):
                    for s in pair:
                        act.wait_ge(f_aT_raw, count(i, s))
                        act.activation(f_aT[s][:, :, :], PS[:, X[s], :], ACT.Copy).then_inc(f_aT_ok, 1)

                def store(i, pair):
                    for s in pair:
                        act.wait_ge(x3T_raw, count(i, s))
                        act.activation(x3T[:, bass.ds((i * NS + s) * S, S)], PS[:, Y[s], 256:384], ACT.Copy).then_inc(stored, 1)
                        act.activation(x3_tok[:, bass.ds(i * NS + s, 1), :], x3[s][:, :], ACT.Copy).then_inc(stored, 1)

                def side_by_side(i, pair, j, other):
                    keep_hT(i, pair)
                    keep_inv(j, other)
                    exp_qkv(i, pair)
                    keep_qkvT(i, pair)
                    keep_v(i, pair)
                    exp_p(j, other)
                    exp(i, pair, 0)
                    keep_pT(j, other)
                    exp(i, pair, 1)
                    exp(i, pair, 2)
                    keep_h2T(j, other)
                    exp(i, pair, 3)
                    exp_f(j, other)
                    keep_weights(i, pair, 0)
                    keep_fT(j, other)
                    keep_weights(i, pair, 2)
                    store(j, other)

                side_by_side(0, EARLY, 0, NONE)
                with act.Fori(1, TURNS) as i:
                    side_by_side(i - 1, LATE, i - 1, EARLY)
                    side_by_side(i, EARLY, i - 1, LATE)
                side_by_side(TURNS - 1, LATE, TURNS - 1, EARLY)
                side_by_side(TURNS - 1, NONE, TURNS - 1, LATE)
                act.wait_ge(stored, 2 * B)

            @block.vector
            def _(dve):
                def first_norm(i, pair):
                    for s in pair:
                        dve.bn_stats(stats[:, s, :], cond_tok[:, bass.ds(i * NS + s, 1), :]).then_inc(st_ok, 1)
                    for s in pair:
                        dve.wait_ge(st_ok, count(i, s))
                        dve.sem_inc(st_seen, 1)
                        dve.bn_aggr(mv[:, s, :], stats[:, s, :]).then_inc(mv_ok, 1)
                    for s in pair:
                        dve.wait_ge(mv_ok, count(i, s))
                        dve.tensor_scalar(veps[:, s:s + 1], mv[:, s, 1:2], LN_EPS, None, ALU.add).then_inc(veps_ok, 1)

                def apply_norm(i, pair):
                    for s in pair:
                        dve.wait_ge(rstd_ok, count(i, s))
                        dve.tensor_scalar(h[s][:, :], cond_tok[:, bass.ds(i * NS + s, 1), :].rearrange("p o d -> p (o d)"),
                                          mv[:, s, 0:1], rstd[:, s:s + 1], ALU.subtract, ALU.mult).then_inc(h_ok, 1)

                def max_qkv(i, pair):
                    for s in pair:
                        dve.wait_ge(qkv_raw, count(i, s))
                        dve.tensor_reduce(qkv_nmax[s][:, :], PS[:, Y[s], 0:3 * D].rearrange("p (j n) -> p j n", j=3),
                                          AX.X, ALU.max, negate=True).then_inc(qkv_nmax_ok, 1)

                def normalize_qkv(i, pair):
                    for s in pair:
                        dve.wait_ge(qkv_exp, count(i, s))
                        dve.reciprocal(qkv_inv[s][:, :], qkv_sum[s][:, :]).then_inc(qkv_inv_ok, 1)
                        dve.wait_ge(qkv_inv_ok, count(i, s))
                        dve.tensor_tensor(qkv_a[s][:, :, :], qkv_a[s][:, :, :],
                                          qkv_inv[s][:, :].unsqueeze(2).to_broadcast([S, 3, D]), ALU.mult).then_inc(qkv_a_ok, 1)

                def split_qk(i, pair):
                    for s in pair:
                        dve.wait_ge(proj_raw, count(i, s))
                        dve.tensor_tensor(q_rows[s][:, :, :], PS[:, Y[s]:Y[s] + 1, 0:S].to_broadcast([D, QUADS, S]),
                                          quad_rows[:, :].unsqueeze(2).to_broadcast([D, QUADS, S]), ALU.mult).then_inc(qk_ok, 1)
                        dve.tensor_tensor(k_heads[s][:, :, :], PS[:, Y[s]:Y[s] + 1, S:2 * S].to_broadcast([D, 4, S]),
                                          head4[:, :].unsqueeze(2).to_broadcast([D, 4, S]), ALU.mult).then_inc(qk_ok, 1)

                def max_heads(i, pair, r):
                    for s in pair:
                        dve.wait_ge(score_raw, count(i, s, r, QUADS))
                        dve.tensor_reduce(head_nmax[s][:, 4 * r:4 * r + 4],
                                          PS[:, (X, Y)[r % 2][s], :].rearrange("p (j k) -> p j k", j=4),
                                          AX.X, ALU.max, negate=True).then_inc(hmax_ok, 1)

                def invert_sums(i, pair):
                    for s in pair:
                        dve.wait_ge(hexp_ok, count(i, s, QUADS - 1, QUADS))
                        dve.reciprocal(head_inv[s][:, :], head_sum[s][:, :]).then_inc(hinv_ok, 1)

                def keep_weights(i, pair, r):
                    for s in pair:
                        dve.wait_ge(wT_raw, count(i, s, r, QUADS))
                        dve.tensor_copy(weightT[s][:, 4 * r:4 * r + 4, :], PS[:, Y[s], :].rearrange("p (j k) -> p j k", j=4)).then_inc(wT_odd, 1)

                def normalize_heads(i, pair):
                    for s in pair:
                        dve.wait_ge(o_raw, count(i, s))
                        dve.wait_ge(inv_ok, count(i, s))
                        dve.tensor_tensor(oT[s][:, :], PS[:, X[s], 0:S], inv_rows[s][:, :], ALU.mult).then_inc(oT_ok, 1)

                def max_p(i, pair):
                    for s in pair:
                        dve.wait_ge(p_raw, count(i, s))
                        dve.tensor_reduce(p_nmax[s][:, :], PS[:, Y[s], 128:256], AX.X, ALU.max, negate=True).then_inc(p_nmax_ok, 1)

                def invert_p(i, pair):
                    for s in pair:
                        dve.wait_ge(p_exp, count(i, s))
                        dve.reciprocal(p_inv[s][:, :], p_sum[s][:, :]).then_inc(p_inv_ok, 1)

                def first_sum(i, pair):
                    for s in pair:
                        dve.wait_ge(p_inv_ok, count(i, s))
                        dve.wait_ge(p_out_raw, count(i, s))
                        dve.scalar_tensor_tensor(out=x1[s][:, :], in0=PS[:, Y[s], 256:384], scalar=p_inv[s][:, 0:1],
                                                 in1=cond_tok[:, bass.ds(i * NS + s, 1), :].rearrange("p o d -> p (o d)"),
                                                 op0=ALU.mult, op1=ALU.add).then_inc(x1_ok, 1)

                def second_norm(i, pair):
                    for s in pair:
                        dve.wait_ge(x1_ok, count(i, s))
                        dve.bn_stats(stats2[s][:, :], x1[s][:, :]).then_inc(f_st_ok, 1)
                    for s in pair:
                        dve.wait_ge(f_st_ok, count(i, s))
                        dve.sem_inc(f_st_seen, 1)
                        dve.bn_aggr(mv2[s][:, :], stats2[s][:, :]).then_inc(f_mv_ok, 1)
                    for s in pair:
                        dve.wait_ge(f_mv_ok, count(i, s))
                        dve.tensor_scalar(veps2[s][:, :], mv2[s][:, 1:2], LN_EPS, None, ALU.add).then_inc(f_veps_ok, 1)

                def apply_norm2(i, pair):
                    for s in pair:
                        dve.wait_ge(f_rstd_ok, count(i, s))
                        dve.tensor_scalar(h2[s][:, :], x1[s][:, :], mv2[s][:, 0:1], rstd2[s][:, 0:1],
                                          ALU.subtract, ALU.mult).then_inc(h2_ok, 1)

                def max_f(i, pair):
                    for s in pair:
                        dve.wait_ge(f_raw, count(i, s))
                        dve.tensor_reduce(f_nmax[s][:, :], PS[:, Y[s], :], AX.X, ALU.max, negate=True).then_inc(f_nmax_ok, 1)

                def invert_f(i, pair):
                    for s in pair:
                        dve.wait_ge(f_exp, count(i, s))
                        dve.reciprocal(f_inv[s][:, :], f_sum[s][:, :]).then_inc(f_inv_ok, 1)

                def second_sum(i, pair):
                    for s in pair:
                        dve.wait_ge(f_inv_ok, count(i, s))
                        dve.wait_ge(f_out_raw, count(i, s))
                        dve.scalar_tensor_tensor(out=x2[s][:, :], in0=PS[:, Y[s], 0:D], scalar=f_inv[s][:, 0:1],
                                                 in1=x1[s][:, :], op0=ALU.mult, op1=ALU.add).then_inc(x2_ok, 1)

                def third_sum(i, pair):
                    for s in pair:
                        dve.wait_ge(x2_ok, count(i, s))
                        dve.wait_ge(x_loaded, 16)
                        dve.tensor_tensor(x3[s][:, :], x2[s][:, :],
                                          x_tok[:, bass.ds(i * NS + s, 1), :].rearrange("p o d -> p (o d)"), ALU.add).then_inc(x3_ok, 1)

                def side_by_side(i, pair, j, other):
                    first_norm(i, pair)
                    apply_norm(i, pair)
                    max_qkv(i, pair)
                    normalize_qkv(i, pair)
                    normalize_heads(j, other)
                    split_qk(i, pair)
                    max_p(j, other)
                    max_heads(i, pair, 0)
                    invert_p(j, other)
                    max_heads(i, pair, 1)
                    first_sum(j, other)
                    second_norm(j, other)
                    max_heads(i, pair, 2)
                    apply_norm2(j, other)
                    max_heads(i, pair, 3)
                    max_f(j, other)
                    invert_sums(i, pair)
                    invert_f(j, other)
                    keep_weights(i, pair, 1)
                    second_sum(j, other)
                    third_sum(j, other)
                    keep_weights(i, pair, 3)

                side_by_side(0, EARLY, 0, NONE)
                with dve.Fori(1, TURNS) as i:
                    side_by_side(i - 1, LATE, i - 1, EARLY)
                    side_by_side(i, EARLY, i - 1, LATE)
                side_by_side(TURNS - 1, LATE, TURNS - 1, EARLY)
                side_by_side(TURNS - 1, NONE, TURNS - 1, LATE)
        signals.clear()


def scan_inputs_phase(nc, a, K):
    import concourse.bass as bass
    from concourse import mybir
    from contextlib import ExitStack
    f32 = mybir.dt.float32
    ALU, ACT = mybir.AluOpType, mybir.ActivationFunctionType
    NS = 4
    EB = 2
    ET = EB * S
    TURNS = B // (NS * EB)
    X = [2 * s for s in range(NS)]
    Y = [2 * s + 1 for s in range(NS)]
    PAD = N_TAPS - 1
    with ExitStack() as ctx:
        def sb(name, shape, dt=f32):
            return ctx.enter_context(nc.sbuf_tensor(name, shape, dt))

        def per(name, shape):
            return [sb(f"{name}{s}", shape) for s in range(NS)]

        signals = Signals(nc, ctx, "pre")
        PS, ident, x3T, gateT, xnT = (K[n] for n in ("PS", "ident", "x3T", "gateT", "xnT"))
        w_inT = sb("w_inT", [D, 2 * DI])
        tembT, taps, chan = sb("tembT", [128, NH, B]), sb("taps", [128, NH, N_TAPS]), sb("chan", [128, NH])
        ln_g, ln_b = sb("ln_g", [S, DI]), sb("ln_b", [S, DI])
        w_B, w_Cdt = sb("w_B", [128, NH, N_STATE]), sb("w_Cdt", [128, NH, 48])
        w_dtT = sb("w_dtT", [48, 48])
        state_cols = sb("state_cols", [N_STATE, 2])
        a_tanh, a_step = sb("a_tanh", [N_STATE, 1]), sb("a_step", [N_STATE, 1])
        ones_col, minus_half, plus_half = sb("ones_col", [128, 1]), sb("minus_half3", [S, EB]), sb("plus_half3", [S, EB])
        xr = per("xr", [128, NH, EB, PAD + S])
        conv = per("conv", [128, NH, EB, S])
        stats, mv, veps, rstd = per("st3", [S, EB, 6]), per("mv3", [S, EB, 2]), per("veps3", [S, EB]), per("rstd3", [S, EB])
        xn = per("xn", [S, EB, DI])
        xng, sq = per("xng", [128, NH, ET]), per("sq", [128, NH, ET])
        norm2, norm = per("norm2", [S, EB]), per("norm", [S, EB])
        bd = per("bd", [S, EB, N_STATE])
        cdt = per("cdt", [48, ET])
        ad = per("ad", [N_STATE, ET])

        loads = [(w_inT[:, :], a["w_inT"]), (tembT[:, :, :], a["condT"].rearrange("(h p) b -> p h b", p=128)),
                 (taps[:, :, :], a["taps"].rearrange("(h p) k -> p h k", p=128)),
                 (chan[:, :], a["b_conv"].rearrange("(h p) -> p h", p=128)),
                 (ln_g[:, :], a["ln_g"].rearrange("(o c) -> o c", o=1).partition_broadcast(S)),
                 (ln_b[:, :], a["ln_b"].rearrange("(o c) -> o c", o=1).partition_broadcast(S)),
                 (w_B[:, :, :], a["w_xpT"][:, 0:16].rearrange("(h p) s -> p h s", p=128)),
                 (w_Cdt[:, :, 0:16], a["w_xpT"][:, 16:32].rearrange("(h p) s -> p h s", p=128)),
                 (w_Cdt[:, :, 32:48], a["w_xpT"][:, 32:48].rearrange("(h p) s -> p h s", p=128)),
                 (w_dtT[32:48, 0:N_STATE], a["w_dtT"]), (state_cols[:, :], a["state_cols"])]
        cleared, loaded, filled, a_tanh_ok, a_step_ok = signals.take_all("cleared loaded filled a_tanh_ok a_step_ok")
        xn_sent, bd_sent, c_sent, ad_sent = signals.take_all("xn_sent bd_sent c_sent ad_sent", NS)
        with nc.Block() as block:
            @block.sync
            def _(sp):
                for s in range(NS):
                    for sent in (xn_sent, bd_sent, c_sent, ad_sent):
                        sp.sem_inc(sent[s], 16)
                sp.wait_ge(cleared, 2)
                for dst, src in loads:
                    sp.dma_start(dst, src, allow_slow_non_contiguous=True).then_inc(loaded, 16)
                sp.wait_ge(loaded, 16 * len(loads))

            @block.gpsimd
            def _(pool):
                pool.memset(w_Cdt[:, :, :], 0.0).then_inc(cleared, 1)
                pool.memset(w_dtT[:, :], 0.0).then_inc(cleared, 1)
                pool.memset(ones_col[:, :], 1.0).then_inc(filled, 1)
                pool.memset(minus_half[:, :], -0.5).then_inc(filled, 1)
                pool.memset(plus_half[:, :], 0.5).then_inc(filled, 1)
                for s in range(NS):
                    pool.memset(xr[s][:, :, :, :], 0.0).then_inc(filled, 1)
                pool.wait_ge(filled, 3 + NS)

            @block.scalar
            def _(act):
                act.wait_ge(loaded, 16 * len(loads))
                act.activation(a_tanh[:, :], state_cols[:, 1:2], ACT.Tanh).then_inc(a_tanh_ok, 1)

            @block.vector
            def _(dve):
                dve.wait_ge(a_tanh_ok, 1)
                dve.tensor_scalar(a_step[:, :], a_tanh[:, :], -0.01, None, ALU.mult).then_inc(a_step_ok, 1)
                dve.wait_ge(a_step_ok, 1)

        (in_raw, gate_ok, xr_ok, conv_ok, xc_ok, xc_tok_raw, st_ok, st_seen, mv_ok, veps_ok, rstd_ok, xhat_ok,
         scaled_ok, xn_ok, xnT_raw, xng_ok, xnT_ok, sq_ok, b_raw, cdt_raw, norm2_ok, norm_ok, bd_ok, cdt_ok, dt_raw,
         tanh_ok, ad_ok) = signals.take_all(
            "in_raw gate_ok xr_ok conv_ok xc_ok xc_tok_raw st_ok st_seen mv_ok veps_ok rstd_ok xhat_ok "
            "scaled_ok xn_ok xnT_raw xng_ok xnT_ok sq_ok b_raw cdt_raw norm2_ok norm_ok bd_ok cdt_ok dt_raw "
            "tanh_ok ad_ok", NS)

        EARLY, LATE = (0, 1), (2, 3)

        with nc.Block() as block:
            @block.sync
            def _(sp):
                def send(i, pair):
                    n = i + 1
                    for s in pair:
                        first = (i * NS + s) * EB
                        sp.wait_ge(xn_ok[s], n)
                        sp.dma_start(K["xn_d"][bass.ds(first, EB), :, :].rearrange("b t c -> t b c"), xn[s][:, :, :]).then_inc(xn_sent[s], 16)
                    for s in pair:
                        first = (i * NS + s) * EB
                        sp.wait_ge(bd_ok[s], n)
                        sp.dma_start(K["bd_d"][bass.ds(first, EB), :, :].rearrange("b t s -> t b s"), bd[s][:, :, :]).then_inc(bd_sent[s], 16)
                        sp.wait_ge(cdt_ok[s], n)
                        sp.dma_start(K["c_d"][bass.ds(first, EB), :, :].rearrange("b s t -> s b t"),
                                     cdt[s][0:N_STATE, :].rearrange("s (b t) -> s b t", b=EB)).then_inc(c_sent[s], 16)
                        sp.wait_ge(ad_ok[s], n)
                        sp.dma_start(K["ad_d"][bass.ds(first, EB), :, :].rearrange("b s t -> s b t"),
                                     ad[s][:, :].rearrange("s (b t) -> s b t", b=EB)).then_inc(ad_sent[s], 16)
                with sp.Fori(0, TURNS) as i:
                    send(i, EARLY)
                    send(i, LATE)
                for s in range(NS):
                    for sent in (xn_sent, bd_sent, c_sent, ad_sent):
                        sp.wait_ge(sent[s], 16 * (TURNS + 1))

            @block.gpsimd
            def _(pool):
                def second(n, pair):
                    for s in pair:
                        pool.wait_ge(veps_ok[s], n)
                        pool.tensor_tensor(rstd[s][:, :], veps[s][:, :], minus_half[:, :], ALU.pow).then_inc(rstd_ok[s], 1)
                    for s in pair:
                        pool.wait_ge(xhat_ok[s], n)
                        pool.tensor_tensor(xn[s][:, :, :], xn[s][:, :, :], ln_g[:, :].unsqueeze(1).to_broadcast([S, EB, DI]),
                                           ALU.mult).then_inc(scaled_ok[s], 1)
                        pool.wait_ge(scaled_ok[s], n)
                        pool.tensor_tensor(xn[s][:, :, :], xn[s][:, :, :], ln_b[:, :].unsqueeze(1).to_broadcast([S, EB, DI]),
                                           ALU.add).then_inc(xn_ok[s], 1)
                    for s in pair:
                        pool.wait_ge(norm2_ok[s], n)
                        pool.tensor_tensor(norm[s][:, :], norm2[s][:, :], plus_half[:, :], ALU.pow).then_inc(norm_ok[s], 1)

                with pool.Fori(0, TURNS) as i:
                    second(i + 1, EARLY)
                    second(i + 1, LATE)

            @block.tensor
            def _(pe):
                def first(i, pair):
                    for s in pair:
                        if needs_free(i):
                            pe.wait_ge(bd_ok[s], i)
                            pe.wait_ge(tanh_ok[s], i)
                        for j in range(4):
                            mm = pe.matmul(PS[:, (X, Y)[j // 2][s], (j % 2) * ET:(j % 2 + 1) * ET], w_inT[:, j * 128:(j + 1) * 128],
                                           x3T[:, bass.ds((i * NS + s) * ET, ET)], start=True, stop=True)
                        mm.then_inc(in_raw[s], 1)

                def turn_conv(n, pair):
                    for s in pair:
                        pe.wait_ge(xc_ok[s], n)
                        for b in range(EB):
                            for h in range(NH):
                                at = b * DI + h * 128
                                mm = pe.transpose(PS[:, X[s], at:at + 128], conv[s][:, h, b, :], ident[:, :])
                        mm.then_inc(xc_tok_raw[s], 1)

                def project(n, pair):
                    for s in pair:
                        pe.wait_ge(xn_ok[s], n)
                        pe.wait_ge(gate_ok[s], n)
                        for h in range(NH):
                            for b in range(EB):
                                mm = pe.transpose(PS[:, Y[s], (h * EB + b) * S:(h * EB + b + 1) * S], xn[s][:, b, h * 128:(h + 1) * 128], ident[:, :])
                        mm.then_inc(xnT_raw[s], 1)
                    for s in pair:
                        pe.wait_ge(sq_ok[s], n)
                        for h in range(NH):
                            mm = pe.matmul(PS[0:48, X[s], 0:ET], w_Cdt[:, h, :], xng[s][:, h, :], start=(h == 0), stop=(h == 1))
                        mm.then_inc(cdt_raw[s], 1)
                        for b in range(EB):
                            for h in range(NH):
                                pe.matmul(PS[:, Y[s], b * 16:(b + 1) * 16], xng[s][:, h, b * S:(b + 1) * S], w_B[:, h, :],
                                          start=(h == 0), stop=(h == 1))
                            for h in range(NH):
                                mm = pe.matmul(PS[:, Y[s], 64 + b:65 + b], sq[s][:, h, b * S:(b + 1) * S], ones_col[:, :],
                                               start=(h == 0), stop=(h == 1))
                        mm.then_inc(b_raw[s], 1)
                    for s in pair:
                        pe.wait_ge(xnT_ok[s], n)
                        pe.wait_ge(cdt_ok[s], n)
                        pe.matmul(PS[0:48, X[s], ET:2 * ET], w_dtT[32:48, :], cdt[s][32:48, :], start=True, stop=True).then_inc(dt_raw[s], 1)

                def needs_free(i):
                    return not isinstance(i, int)

                first(0, EARLY)
                first(0, LATE)
                turn_conv(1, EARLY)
                project(1, EARLY)
                with pe.Fori(1, TURNS) as i:
                    turn_conv(i, LATE)
                    first(i, EARLY)
                    project(i, LATE)
                    turn_conv(i + 1, EARLY)
                    first(i, LATE)
                    project(i + 1, EARLY)
                turn_conv(TURNS, LATE)
                project(TURNS, LATE)

            @block.scalar
            def _(act):
                def gates(i, pair):
                    for s in pair:
                        act.wait_ge(in_raw[s], i + 1)
                        for h in range(NH):
                            ins = act.activation(gateT[:, h, bass.ds((i * NS + s) * ET, ET)], PS[:, Y[s], h * ET:(h + 1) * ET], ACT.Silu)
                        ins.then_inc(gate_ok[s], 1)

                def silu(n, pair):
                    for s in pair:
                        act.wait_ge(conv_ok[s], N_TAPS * NH * n)
                        act.activation(conv[s][:, :, :, :], conv[s][:, :, :, :], ACT.Silu).then_inc(xc_ok[s], 1)

                def keep_xn(i, pair):
                    n = i + 1
                    for s in pair:
                        act.wait_ge(xnT_raw[s], n)
                        act.activation(xng[s][:, :, :], PS[:, Y[s], :].rearrange("p (h t) -> p h t", h=NH), ACT.Copy).then_inc(xng_ok[s], 1)
                        act.activation(xnT[:, :, bass.ds((i * NS + s) * ET, ET)], PS[:, Y[s], :].rearrange("p (h t) -> p h t", h=NH),
                                       ACT.Copy).then_inc(xnT_ok[s], 1)
                        act.wait_ge(xng_ok[s], n)
                        act.activation(sq[s][:, :, :], xng[s][:, :, :], ACT.Square).then_inc(sq_ok[s], 1)

                def steps(n, pair):
                    for s in pair:
                        act.wait_ge(c_sent[s], 16 * n)
                        act.wait_ge(cdt_raw[s], n)
                        act.activation(cdt[s][:, :], PS[0:48, X[s], 0:ET], ACT.Copy).then_inc(cdt_ok[s], 1)
                    for s in pair:
                        act.wait_ge(ad_sent[s], 16 * n)
                        act.wait_ge(dt_raw[s], n)
                        act.activation(ad[s][:, :], PS[0:N_STATE, X[s], ET:2 * ET], ACT.Tanh, bias=state_cols[:, 0:1]).then_inc(tanh_ok[s], 1)

                gates(0, EARLY)
                gates(0, LATE)
                silu(1, EARLY)
                keep_xn(0, EARLY)
                silu(1, LATE)
                steps(1, EARLY)
                with act.Fori(1, TURNS) as i:
                    gates(i, EARLY)
                    keep_xn(i - 1, LATE)
                    silu(i + 1, EARLY)
                    steps(i, LATE)
                    gates(i, LATE)
                    keep_xn(i, EARLY)
                    silu(i + 1, LATE)
                    steps(i + 1, EARLY)
                keep_xn(TURNS - 1, LATE)
                steps(TURNS, LATE)

            @block.vector
            def _(dve):
                def convolve(i, pair):
                    n = i + 1
                    for s in pair:
                        dve.wait_ge(in_raw[s], n)
                        for h in range(NH):
                            dve.tensor_tensor(xr[s][:, h, :, PAD:PAD + S], PS[:, X[s], h * ET:(h + 1) * ET].rearrange("p (b t) -> p b t", b=EB),
                                              tembT[:, h, bass.ds((i * NS + s) * EB, EB)].unsqueeze(2).to_broadcast([128, EB, S]),
                                              ALU.add).then_inc(xr_ok[s], 1)
                    for k in range(N_TAPS):
                        for s in pair:
                            for h in range(NH):
                                if k == 0:
                                    dve.wait_ge(xr_ok[s], NH * n)
                                    ins = dve.tensor_scalar(conv[s][:, h, :, :], xr[s][:, h, :, 0:S], taps[:, h, 0:1], chan[:, h:h + 1],
                                                            ALU.mult, ALU.add)
                                else:
                                    dve.wait_ge(conv_ok[s], i * (N_TAPS * NH) + ((k - 1) * NH + h + 1))
                                    ins = dve.scalar_tensor_tensor(out=conv[s][:, h, :, :], in0=xr[s][:, h, :, k:k + S],
                                                                   scalar=taps[:, h, k:k + 1], in1=conv[s][:, h, :, :],
                                                                   op0=ALU.mult, op1=ALU.add)
                                ins.then_inc(conv_ok[s], 1)

                def normalize(n, pair):
                    for s in pair:
                        dve.wait_ge(xc_tok_raw[s], n)
                        for b in range(EB):
                            ins = dve.bn_stats(stats[s][:, b, :], PS[:, X[s], b * DI:(b + 1) * DI])
                        ins.then_inc(st_ok[s], 1)
                        dve.wait_ge(st_ok[s], n)
                        dve.sem_inc(st_seen[s], 1)
                        for b in range(EB):
                            ins = dve.bn_aggr(mv[s][:, b, :], stats[s][:, b, :])
                        ins.then_inc(mv_ok[s], 1)
                        dve.wait_ge(mv_ok[s], n)
                        dve.tensor_scalar(veps[s][:, :].unsqueeze(2), mv[s][:, :, 1:2], LN_EPS, None, ALU.add).then_inc(veps_ok[s], 1)
                    for s in pair:
                        dve.wait_ge(xn_sent[s], 16 * n)
                        dve.wait_ge(rstd_ok[s], n)
                        for b in range(EB):
                            ins = dve.tensor_scalar(xn[s][:, b, :], PS[:, X[s], b * DI:(b + 1) * DI],
                                                    mv[s][:, b, 0:1], rstd[s][:, b:b + 1], ALU.subtract, ALU.mult)
                        ins.then_inc(xhat_ok[s], 1)

                def finish(n, pair):
                    for s in pair:
                        dve.wait_ge(b_raw[s], n)
                        dve.tensor_scalar(norm2[s][:, :], PS[:, Y[s], 64:64 + EB], 1.0, None, ALU.min).then_inc(norm2_ok[s], 1)
                    for s in pair:
                        dve.wait_ge(bd_sent[s], 16 * n)
                        dve.wait_ge(norm_ok[s], n)
                        dve.tensor_tensor(bd[s][:, :, :], PS[:, Y[s], 0:EB * N_STATE].rearrange("p (b s) -> p b s", b=EB),
                                          norm[s][:, :].unsqueeze(2).to_broadcast([S, EB, N_STATE]), ALU.mult).then_inc(bd_ok[s], 1)
                    for s in pair:
                        dve.wait_ge(tanh_ok[s], n)
                        dve.tensor_scalar(ad[s][:, :], ad[s][:, :], a_step[:, 0:1], 1.0, ALU.mult, ALU.add).then_inc(ad_ok[s], 1)

                convolve(0, EARLY)
                normalize(1, EARLY)
                convolve(0, LATE)
                finish(1, EARLY)
                with dve.Fori(1, TURNS) as i:
                    normalize(i, LATE)
                    convolve(i, EARLY)
                    finish(i, LATE)
                    normalize(i + 1, EARLY)
                    convolve(i, LATE)
                    finish(i + 1, EARLY)
                normalize(TURNS, LATE)
                finish(TURNS, LATE)
        signals.clear()


def scan_phase(nc, a, K):
    import concourse.bass as bass
    from concourse import mybir
    from contextlib import ExitStack
    f32 = mybir.dt.float32
    ALU, ACT = mybir.AluOpType, mybir.ActivationFunctionType
    BG = 128 // N_STATE
    G = B // BG
    HALF = 8
    STEPS = 2 * HALF
    CHUNKS = S // STEPS
    RING = 4
    with ExitStack() as ctx:
        def sb(name, shape, dt=f32):
            return ctx.enter_context(nc.sbuf_tensor(name, shape, dt))

        signals = Signals(nc, ctx, "scan")
        PS, ident, xnT = (K[n] for n in ("PS", "ident", "xnT"))
        skip = sb("skip", [128, NH])
        decay, c_all = sb("decay", [128, G, S]), sb("c_all", [128, G, S])
        own = sb("own", [128, BG])
        PARTS = 4
        f32r = mybir.dt.float32r
        same_batch = sb("same_batch", [PARTS * B, B])
        x_in = [sb(f"x_in{k}", [PARTS * B, HALF, DI]) for k in range(2)]
        x_part = [sb(f"x_part{k}", [PARTS * B, HALF, DI], f32r) for k in range(2)]
        bd_in = [sb(f"bd_in{k}", [PARTS * B, HALF, N_STATE]) for k in range(2)]
        bd_high = [sb(f"bd_high{k}", [PARTS * B, HALF, N_STATE], f32r) for k in range(2)]
        bd_part = [sb(f"bd_part{k}", [PARTS * B, HALF, N_STATE]) for k in range(2)]
        bd_diag = [sb(f"bd_diag{k}", [PARTS * B, HALF, B, N_STATE], f32r) for k in range(2)]
        decay_now = [sb(f"decay_now{k}", [128, G, HALF]) for k in range(2)]
        WIDE = HALF * BG
        c_diag = [sb(f"c_diag{k}", [128, G * HALF * WIDE + WIDE]) for k in range(2)]
        y_tok = sb("y_tok", [WIDE, G, DI])
        y_new = sb("y_new", [128, NH, HALF * B])
        grown = sb("grown", [128, G, DI])
        state = [K["x3T"][:, k * G * DI:(k + 1) * G * DI].rearrange("p (g c) -> p g c", g=G) for k in range(RING)]

        resident_in, ones_ok, cut_ok, zero_ok, same_ok = signals.take_all("resident_in ones_ok cut_ok zero_ok same_ok")
        x_loaded, bd_loaded, diag_ok, c_ok, decay_ok = signals.take_all("x_loaded bd_loaded diag_ok c_ok decay_ok", 2)
        load_go, add_go, skip_in = signals.take_all("load_go add_go skip_in")
        x_high, x_parts, bd_high_ok, bd_part_ok, bd_low_ok = signals.take_all("x_high x_parts bd_high_ok bd_part_ok bd_low_ok", 2)
        bx_raw, grown_ok, state_ok, y_raw, y_stored = signals.take_all("bx_raw grown_ok state_ok y_raw y_stored")
        y_copied, yT_raw, y_added, wide_zero, skipped, turn_go = signals.take_all("y_copied yT_raw y_added wide_zero skipped turn_go")

        def load(sp, k, at):
            for q in range(PARTS):
                sp.dma_start(x_in[k][q * B:(q + 1) * B, :, :], K["xn_d"][:, bass.ds(at, HALF), :]).then_inc(x_loaded[k], 16)
                sp.dma_start(bd_in[k][q * B:(q + 1) * B, :, :], K["bd_d"][:, bass.ds(at, HALF), :]).then_inc(bd_loaded[k], 16)

        with nc.Block() as block:
            @block.sync
            def _(sp):
                sp.dma_start(skip[:, :], a["D"].rearrange("(h p) -> p h", p=128), allow_slow_non_contiguous=True).then_inc(skip_in, 16)
                for k in range(2):
                    load(sp, k, k * HALF)
                sp.dma_start(decay[:, :, :], K["ad_d"].rearrange("(g b) s t -> (b s) g t", g=G)).then_inc(resident_in, 16)
                sp.dma_start(c_all[:, :, :], K["c_d"].rearrange("(g b) s t -> (b s) g t", g=G)).then_inc(resident_in, 16)
                sp.wait_ge(resident_in, 32)
                sp.sem_inc(state_ok, 1)
                sp.sem_inc(grown_ok, 2)
                sp.sem_inc(y_raw, RING)
                sp.sem_inc(y_stored, 2)
                sp.sem_inc(y_added, 1)
                sp.sem_inc(yT_raw, 1)

            @block.gpsimd
            def _(pool):
                pool.memset(own[:, :], 1.0).then_inc(ones_ok, 1)
                pool.memset(state[RING - 1][:, :, :], 0.0).then_inc(zero_ok, 1)
                for k in range(2):
                    pool.memset(c_diag[k][:, :], 0.0).then_inc(wide_zero, 1)
                pool.wait_ge(ones_ok, 1)
                pool.affine_select(out=own[:, :], in_=own[:, :], compare_op=ALU.is_ge, fill=0.0, base=0,
                                   pattern=[[-N_STATE, BG]], channel_multiplier=1).then_inc(cut_ok, 1)
                pool.wait_ge(cut_ok, 1)
                pool.affine_select(out=own[:, :], in_=own[:, :], compare_op=ALU.is_ge, fill=0.0, base=N_STATE - 1,
                                   pattern=[[N_STATE, BG]], channel_multiplier=-1).then_inc(cut_ok, 1)
                pool.wait_ge(cut_ok, 2)
                pool.wait_ge(zero_ok, 1)
                pool.wait_ge(wide_zero, 2)

            @block.vector
            def _(dve):
                dve.wait_ge(skip_in, 16)
                for h in range(NH):
                    dve.tensor_scalar(xnT[:, h, :], xnT[:, h, :], skip[:, h:h + 1], None, ALU.mult).then_inc(skipped, 1)
                dve.wait_ge(skipped, NH)
                dve.tensor_reduce(same_batch[:, :], ident[:, :].rearrange("p (q b) -> p b q", q=PARTS), mybir.AxisListType.X,
                                  ALU.add).then_inc(same_ok, 1)
                dve.wait_ge(same_ok, 1)

        with nc.Block() as block:
            @block.sync
            def _(sp):
                with sp.Fori(1, CHUNKS) as c:
                    for k in range(2):
                        sp.wait_ge(bd_low_ok[k], 2 * c)
                        sp.wait_ge(x_parts[k], c)
                        sp.sem_inc(load_go, 1)
                        load(sp, k, c * STEPS + k * HALF)

            @block.gpsimd
            def _(pool):
                def spread_bd(k, n):
                    pool.tensor_tensor(bd_diag[k][:, :, :, :],
                                       bd_part[k][:, :, :].unsqueeze(2).to_broadcast([PARTS * B, HALF, B, N_STATE]),
                                       same_batch[:, :].unsqueeze(1).unsqueeze(3).to_broadcast([PARTS * B, HALF, B, N_STATE]),
                                       ALU.mult).then_inc(diag_ok[k], 1)

                def spread_c(k, at, n):
                    for g in range(G):
                        own_columns = c_diag[k][:, g * HALF * WIDE:(g + 1) * HALF * WIDE + WIDE].rearrange(
                            "p (t w) -> p t w", w=WIDE + BG)[:, :, 0:BG]
                        pool.tensor_tensor(own_columns, c_all[:, g, bass.ds(at, HALF)].unsqueeze(2).to_broadcast([128, HALF, BG]),
                                           own[:, :].unsqueeze(1).to_broadcast([128, HALF, BG]), ALU.mult).then_inc(c_ok[k], 1)
                    pool.tensor_copy(decay_now[k][:, :, :], decay[:, :, bass.ds(at, HALF)]).then_inc(decay_ok[k], 1)
                    pool.wait_ge(diag_ok[k], n)
                    pool.wait_ge(c_ok[k], G * n)
                    pool.wait_ge(decay_ok[k], n)

                def x_low(k):
                    low = x_part[k][2 * B:4 * B, :, :]
                    pool.tensor_tensor(low, x_in[k][2 * B:4 * B, :, :], low.bitcast(f32), ALU.subtract).then_inc(x_parts[k], 1)

                def bd_low(k, n):
                    pool.wait_ge(bd_high_ok[k], n)
                    pool.wait_ge(x_parts[k], n)
                    for q in (1, 3):
                        part = (slice(q * B, (q + 1) * B),) + (slice(None),) * 2
                        ins = pool.tensor_tensor(bd_part[k][part], bd_in[k][part], bd_high[k][part].bitcast(f32), ALU.subtract)
                        ins.then_inc(bd_low_ok[k], 1)
                        pool.wait_ge(bd_low_ok[k], 2 * n - (q == 1))
                    pool.wait_ge(bd_part_ok[k], n)

                def add(k, at, n):
                    for h in range(NH):
                        into = xnT[:, h, :].rearrange("p (b t) -> p b t", b=B)[:, :, bass.ds(at, HALF)]
                        ins = pool.tensor_tensor(into, into, y_new[:, h, :].rearrange("p (g t b) -> p g b t", g=G, t=HALF), ALU.add)
                    ins.then_inc(y_added, 1)
                    pool.wait_ge(y_added, n + 1)

                for k in range(2):
                    bd_low(k, 1)
                    spread_bd(k, 1)
                    spread_c(k, k * HALF, 1)
                with pool.Fori(1, CHUNKS) as c:
                    for k in range(2):
                        pool.wait_ge(x_high[k], c + 1)
                        x_low(k)
                        bd_low(k, c + 1)
                        spread_bd(k, c + 1)
                        pool.wait_ge(y_stored, c * 2 + (k + 1))
                        pool.sem_inc(add_go, 1)
                        add(k, (c - 1) * STEPS + k * HALF, c * 2 + (k - 1))
                        spread_c(k, c * STEPS + k * HALF, c + 1)
                for k in range(2):
                    pool.wait_ge(y_stored, CHUNKS * 2 + (k + 1))
                    add(k, (CHUNKS - 1) * STEPS + k * HALF, CHUNKS * 2 + (k - 1))

            @block.tensor
            def _(pe):
                def inputs(c, j):
                    k, tt = j // HALF, j % HALF
                    if tt == 0:
                        pe.wait_ge(x_parts[k], c + 1)
                        pe.wait_ge(diag_ok[k], c + 1)
                    pe.wait_ge(grown_ok, c * STEPS + (j + 1))
                    for g in range(G):
                        mm = pe.matmul(PS[:, 2 * (j % 2) + g // 2, (g % 2) * DI:(g % 2 + 1) * DI],
                                       bd_diag[k][:, tt, g * BG:(g + 1) * BG, :].rearrange("p b s -> p (b s)"), x_part[k][:, tt, :],
                                       start=True, stop=True)
                    mm.then_inc(bx_raw, 1)

                def outputs(c, j):
                    k, tt = j // HALF, j % HALF
                    if tt == 0:
                        pe.wait_ge(c_ok[k], G * (c + 1))
                        pe.wait_ge(y_stored, c * 2 + (k + 1))
                    pe.wait_ge(state_ok, c * STEPS + (j + 2))
                    for g in range(G):
                        at = (g * HALF + tt) * WIDE
                        mm = pe.matmul(PS[0:WIDE, 4 + 2 * k + g // 2, (g % 2) * DI:(g % 2 + 1) * DI], c_diag[k][:, at:at + WIDE],
                                       state[j % RING][:, g, :], start=(tt == 0 and g % 2 == 0),
                                       stop=(tt == HALF - 1 and g % 2 == 1))
                    mm.then_inc(y_raw, 1)
                    if tt == HALF - 1:
                        pe.wait_ge(y_copied, c * 2 + (k + 1))
                        pe.sem_inc(turn_go, 1)
                        for h in range(NH):
                            for g in range(G):
                                at = (h * G + g) * WIDE
                                mm = pe.transpose(PS[:, 4 + 2 * k, at:at + WIDE], y_tok[:, g, h * 128:(h + 1) * 128],
                                                  ident[0:WIDE, 0:WIDE])
                        mm.then_inc(yT_raw, 1)

                inputs(0, 0)
                inputs(0, 1)
                with pe.Fori(0, CHUNKS - 1) as c:
                    for j in range(STEPS):
                        inputs(c + (j + 2) // STEPS, (j + 2) % STEPS)
                        outputs(c, j)
                for j in range(STEPS):
                    if j + 2 < STEPS:
                        inputs(CHUNKS - 1, j + 2)
                    outputs(CHUNKS - 1, j)

            @block.scalar
            def _(act):
                def split_x(k, n):
                    act.wait_ge(x_loaded[k], 16 * PARTS * n)
                    act.activation(x_part[k][:, :, :], x_in[k][:, :, :], ACT.Copy).then_inc(x_high[k], 1)

                def split_bd(k, n):
                    act.wait_ge(bd_loaded[k], 16 * PARTS * n)
                    act.activation(bd_high[k][:, :, :], bd_in[k][:, :, :], ACT.Copy).then_inc(bd_high_ok[k], 1)
                    act.wait_ge(bd_high_ok[k], n)
                    for q in (0, 2):
                        ins = act.activation(bd_part[k][q * B:(q + 1) * B, :, :], bd_high[k][q * B:(q + 1) * B, :, :].bitcast(f32), ACT.Copy)
                    ins.then_inc(bd_part_ok[k], 1)

                def copy_y(c, k):
                    act.wait_ge(yT_raw, c * 2 + (k + 1))
                    act.wait_ge(y_raw, c * STEPS + (RING + (k + 1) * HALF))
                    act.activation(y_tok[:, :, :], PS[0:WIDE, 4 + 2 * k:4 + 2 * k + 2, :], ACT.Copy).then_inc(y_copied, 1)

                def store_y(c, k):
                    act.wait_ge(y_added, c * 2 + (k + 1))
                    act.wait_ge(yT_raw, c * 2 + (k + 2))
                    act.activation(y_new[:, :, :], PS[:, 4 + 2 * k, :], ACT.Copy).then_inc(y_stored, 1)

                for k in range(2):
                    split_x(k, 1)
                    split_bd(k, 1)
                with act.Fori(0, CHUNKS - 1) as c:
                    for k in range(2):
                        act.wait_ge(bx_raw, c * STEPS + (k + 1) * HALF)
                        split_x(k, c + 2)
                        split_bd(k, c + 2)
                        copy_y(c, k)
                        store_y(c, k)
                for k in range(2):
                    copy_y(CHUNKS - 1, k)
                    store_y(CHUNKS - 1, k)

            @block.vector
            def _(dve):
                for k in range(2):
                    dve.wait_ge(x_high[k], 1)
                    low = x_part[k][2 * B:4 * B, :, :]
                    dve.tensor_tensor(low, x_in[k][2 * B:4 * B, :, :], low.bitcast(f32), ALU.subtract).then_inc(x_parts[k], 1)
                with dve.Fori(0, CHUNKS) as c:
                    for j in range(STEPS):
                        k, tt = j // HALF, j % HALF
                        if tt == 0:
                            dve.wait_ge(decay_ok[k], c + 1)
                        dve.wait_ge(bx_raw, c * STEPS + (j + 1))
                        dve.wait_ge(state_ok, c * STEPS + (j + 1))
                        for g in range(G):
                            ins = dve.scalar_tensor_tensor(out=grown[:, g, :], in0=state[(j - 1) % RING][:, g, :],
                                                           scalar=decay_now[k][:, g, tt:tt + 1],
                                                           in1=PS[:, 2 * (j % 2) + g // 2, (g % 2) * DI:(g % 2 + 1) * DI],
                                                           op0=ALU.mult, op1=ALU.add)
                        ins.then_inc(grown_ok, 1)
                        dve.wait_ge(grown_ok, c * STEPS + (j + 3))
                        dve.wait_ge(y_raw, c * STEPS + (j + 1))
                        dve.tensor_scalar(state[j % RING][:, :, :], grown[:, :, :], CLIP, -CLIP, ALU.min, ALU.max).then_inc(state_ok, 1)
        signals.clear()


def experts_phase(nc, a, K, out):
    import concourse.bass as bass
    from concourse import mybir
    from contextlib import ExitStack
    f32 = mybir.dt.float32
    ALU, ACT, AX = mybir.AluOpType, mybir.ActivationFunctionType, mybir.AxisListType
    NHID = HIDDEN // 128
    X4, H = 6, 7
    with ExitStack() as ctx:
        def sb(name, shape, dt=f32):
            return ctx.enter_context(nc.sbuf_tensor(name, shape, dt))

        signals = Signals(nc, ctx, "moe")
        f32r = mybir.dt.float32r
        PS, ident, yT, gateT, gate, x3_tok = (K[n] for n in ("PS", "ident", "xnT", "gateT", "gate", "x3_tok"))
        w1_high, w1_low = sb("w1_high", [D, NE, HIDDEN], f32r), sb("w1_low", [D, NE, HIDDEN], f32r)
        h_high, h_low = sb("h_high", [D, GT], f32r), sb("h_low", [D, GT], f32r)
        w1, w2 = sb("w1", [D, NE, HIDDEN]), sb("w2", [128, NE, NHID, D])
        rms_wT = sb("rms_wT", [D, NE])
        act_out = [sb(f"act_out{k}", [128, NHID, GT]) for k in range(2)]
        gate_now = sb("gate_now", [S, GB, E_ROUTED])
        total = [sb(f"total{k}", [S, GB, D]) for k in range(2)]
        w_outT, router = sb("w_outT", [128, NH, D]), sb("router", [D, E_ROUTED])
        minus_half, rank = sb("minus_half5", [S, GB]), sb("rank", [S, E_ROUTED])
        z, x4, x4n, x4T, junk = sb("z", [128, NH, GT]), sb("x4", [S, GB, D]), sb("x4n", [S, GB, D]), sb("x4T", [D, GT]), sb("junk", [S, D])
        ms, meps, rrms = sb("ms", [S, GB]), sb("meps", [S, GB]), sb("rrms", [S, GB])
        lmax, gsum, ginv, top, pick, msum, msum_eps, minv = (
            sb(n, [S, GB]) for n in ("lmax", "gsum", "ginv", "top", "pick", "msum", "msum_eps", "minv"))
        shifted, gexp, g_all, same, ranked, first, rest, second, both, kept = (
            sb(n, [S, GB, E_ROUTED]) for n in ("shifted", "gexp", "g_all", "same", "ranked", "first", "rest", "second", "both", "kept"))
        small_loads = [(w_outT[:, :, :], a["w_outT"].rearrange("(h p) d -> p h d", p=128)), (router[:, :], a["router"])]
        loads = [(rms_wT[:, :], a["rms_wT"]), (w1[:, :, :], a["w1"].rearrange("e d f -> d e f"))]
        QUARTER = NE // 4
        small_loaded, loaded, w2_loaded, scaled, filled = signals.take_all("small_loaded loaded w2_loaded scaled filled")
        w1_high_ok, w1_low_ok, h_high_ok, h_low_ok = signals.take_all("w1_high_ok w1_low_ok h_high_ok h_low_ok")
        up_raw, silu_ok, down_raw, sum_ok, stored = signals.take_all("up_raw silu_ok down_raw sum_ok stored")
        gates_here = signals.take("gates_here")
        (z_ok, x4_raw, ms_ok, x4_ok, meps_ok, rrms_ok, x4n_ok, hT_raw, x4T_raw, x4T_ok, router_raw, link,
         shifted_ok, gexp_ok, inv_ok, gate_ok) = signals.take_all(
            "z_ok x4_raw ms_ok x4_ok meps_ok rrms_ok x4n_ok hT_raw x4T_raw x4T_ok router_raw link "
            "shifted_ok gexp_ok inv_ok gate_ok")
        with nc.Block() as block:
            @block.sync
            def _(sp):
                for dst, src in small_loads:
                    sp.dma_start(dst, src).then_inc(small_loaded, 16)
                for dst, src in loads:
                    sp.dma_start(dst, src).then_inc(loaded, 16)
                sp.dma_start(w2[:, :, :, :], a["w2"].rearrange("e (h p) d -> p e h d", p=128)).then_inc(w2_loaded, 16)
                sp.wait_ge(small_loaded, 16 * len(small_loads))
                for sem in (silu_ok, down_raw, sum_ok):
                    sp.sem_inc(sem, 2)

            @block.gpsimd
            def _(pool):
                pool.memset(minus_half[:, :], -0.5).then_inc(filled, 1)
                for e in range(E_ROUTED):
                    pool.memset(rank[:, e:e + 1], float(E_ROUTED - e)).then_inc(filled, 1)
                pool.wait_ge(filled, 1 + E_ROUTED)

        with nc.Block() as block:
            @block.gpsimd
            def _(pool):
                def inputs(g):
                    pool.wait_ge(meps_ok, g + 1)
                    pool.tensor_tensor(rrms[:, :], meps[:, :], minus_half[:, :], ALU.pow).then_inc(rrms_ok, 1)

                inputs(0)
                with pool.Fori(1, NG) as g:
                    inputs(g)

            @block.tensor
            def _(pe):
                def inputs(g, e):
                    n = g + 1
                    if e == 2:
                        pe.wait_ge(z_ok, NH * n)
                        for b in range(GB):
                            for h in range(NH):
                                mm = pe.matmul(PS[:, X4, b * D:(b + 1) * D], z[:, h, b * S:(b + 1) * S], w_outT[:, h, :],
                                               start=(h == 0), stop=(h == 1))
                        mm.then_inc(x4_raw, 1)
                    if e == 5:
                        pe.wait_ge(x4_ok, n)
                        for b in range(GB):
                            mm = pe.transpose(PS[:, H, b * S:(b + 1) * S], x4[:, b, :], ident[:, :])
                        mm.then_inc(x4T_raw, 1)
                    if e == 8:
                        pe.wait_ge(x4T_ok, n)
                        for b in range(GB):
                            mm = pe.matmul(PS[:, X4, b * 16:b * 16 + E_ROUTED], x4T[:, b * S:(b + 1) * S], router[:, :],
                                           start=True, stop=True)
                        mm.then_inc(router_raw, 1)
                        pe.wait_ge(x4n_ok, n)
                        for b in range(GB):
                            mm = pe.transpose(PS[:, H, b * S:(b + 1) * S], x4n[:, b, :], ident[:, :])
                        mm.then_inc(hT_raw, 1)

                def up(g, e):
                    pe.wait_ge(silu_ok, g * NE + (e + 1))
                    for h in range(NHID):
                        bank, columns = PS[:, 2 * (e % 2) + h, :], slice(h * 128, (h + 1) * 128)
                        pe.matmul(bank, w1_high[:, e, columns], h_high[:, :], start=True, stop=False)
                        pe.matmul(bank, w1_high[:, e, columns], h_low[:, :], start=False, stop=False)
                        mm = pe.matmul(bank, w1_low[:, e, columns], h_high[:, :], start=False, stop=True)
                    mm.then_inc(up_raw, 1)

                def down(g, e):
                    pe.wait_ge(silu_ok, g * NE + (e + 3))
                    pe.wait_ge(sum_ok, g * NE + (e + 1))
                    for b in range(GB):
                        for h in range(NHID):
                            mm = pe.matmul(PS[:, 4 + e % 2, b * D:(b + 1) * D], act_out[e % 2][:, h, b * S:(b + 1) * S], w2[:, e, h, :],
                                           start=(h == 0), stop=(h == NHID - 1))
                    mm.then_inc(down_raw, 1)

                def experts(g, more):
                    pe.wait_ge(h_low_ok, g + 1)
                    up(g, 0)
                    for e in range(1, NE):
                        up(g, e)
                        down(g, e - 1)
                        if more:
                            inputs(g + 1, e)
                    down(g, NE - 1)

                for e in range(NE):
                    inputs(0, e)
                pe.wait_ge(w2_loaded, 16)
                pe.wait_ge(w1_low_ok, 4)
                with pe.Fori(0, NG - 1) as g:
                    experts(g, True)
                experts(NG - 1, False)

            @block.scalar
            def _(act):
                def inputs(g, e):
                    n = g + 1
                    if e == 3:
                        act.wait_ge(x4_raw, n)
                        for b in range(GB):
                            act.activation(junk[:, :], PS[:, X4, b * D:(b + 1) * D], ACT.Square, accum_out=ms[:, b:b + 1]).then_inc(ms_ok, 1)
                            act.wait_ge(ms_ok, g * GB + (b + 1))
                        act.activation(x4[:, :, :], PS[:, X4, :], ACT.Copy).then_inc(x4_ok, 1)
                    if e == 6:
                        act.wait_ge(x4T_raw, n)
                        act.activation(x4T[:, :], PS[:, H, :], ACT.Copy).then_inc(x4T_ok, 1)
                    if e == 10:
                        act.wait_ge(shifted_ok, n)
                        act.activation(gexp[:, :, :], shifted[:, :, :], ACT.Exp).then_inc(gexp_ok, 1)
                    if e == NE - 1:
                        act.wait_ge(hT_raw, n)
                        act.activation(h_high[:, :], PS[:, H, :], ACT.Copy).then_inc(h_high_ok, 1)

                def experts(g, more):
                    for e in range(NE):
                        act.wait_ge(up_raw, g * NE + (e + 1))
                        act.wait_ge(down_raw, g * NE + (e + 1))
                        act.activation(act_out[e % 2][:, :, :], PS[:, 2 * (e % 2):2 * (e % 2) + 2, :], ACT.Silu).then_inc(silu_ok, 1)
                        if more:
                            inputs(g + 1, e)

                for e in range(NE):
                    inputs(0, e)
                for q in range(4):
                    part = slice(q * QUARTER, (q + 1) * QUARTER)
                    act.wait_ge(scaled, (q + 1) * QUARTER)
                    act.activation(w1_high[:, part, :], w1[:, part, :], ACT.Copy).then_inc(w1_high_ok, 1)
                with act.Fori(0, NG - 1) as g:
                    experts(g, True)
                experts(NG - 1, False)

            @block.vector
            def _(dve):
                LINKS = 4 + 11 + 4

                def spread(v):
                    return v[:, :].unsqueeze(2).to_broadcast([S, GB, E_ROUTED])

                def inputs(g, e):
                    n, at = g + 1, g * GT
                    done = {9: 0, 11: 1, 12: 4, 13: 10, 15: 15}.get(e, 0)

                    def step(ins):
                        nonlocal done
                        done += 1
                        ins.then_inc(link, 1)
                        dve.wait_ge(link, g * LINKS + done)

                    def largest(source, found):
                        step(dve.tensor_reduce(top[:, :], source[:, :, :], AX.X, ALU.max))
                        step(dve.tensor_tensor(same[:, :, :], source[:, :, :], spread(top), ALU.is_equal))
                        step(dve.tensor_tensor(ranked[:, :, :], same[:, :, :], rank[:, :].unsqueeze(1).to_broadcast([S, GB, E_ROUTED]), ALU.mult))
                        step(dve.tensor_reduce(pick[:, :], ranked[:, :, :], AX.X, ALU.max))
                        step(dve.tensor_tensor(found[:, :, :], ranked[:, :, :], spread(pick), ALU.is_equal))

                    if e == 1:
                        for h in range(NH):
                            dve.tensor_tensor(z[:, h, :], yT[:, h, bass.ds(at, GT)], gateT[:, h, bass.ds(at, GT)], ALU.mult).then_inc(z_ok, 1)
                    if e == 4:
                        dve.wait_ge(ms_ok, GB * n)
                        dve.tensor_scalar(meps[:, :], ms[:, :], 1.0 / D, RMS_EPS, ALU.mult, ALU.add).then_inc(meps_ok, 1)
                    if e == 6:
                        dve.wait_ge(x4_ok, n)
                        dve.wait_ge(rrms_ok, n)
                        dve.tensor_tensor(x4n[:, :, :], x4[:, :, :], rrms[:, :].unsqueeze(2).to_broadcast([S, GB, D]), ALU.mult).then_inc(x4n_ok, 1)
                    if e == 9:
                        dve.wait_ge(router_raw, n)
                        logits = PS[:, X4, 0:GB * 16].rearrange("p (b e) -> p b e", e=16)[:, :, 0:E_ROUTED]
                        step(dve.tensor_reduce(lmax[:, :], logits, AX.X, ALU.max))
                        dve.tensor_tensor(shifted[:, :, :], logits, spread(lmax), ALU.subtract).then_inc(shifted_ok, 1)
                    if e == 11:
                        dve.wait_ge(gexp_ok, n)
                        step(dve.tensor_reduce(gsum[:, :], gexp[:, :, :], AX.X, ALU.add))
                        step(dve.reciprocal(ginv[:, :], gsum[:, :]))
                        step(dve.tensor_tensor(g_all[:, :, :], gexp[:, :, :], spread(ginv), ALU.mult))
                    if e == 12:
                        largest(g_all, first)
                        step(dve.scalar_tensor_tensor(out=rest[:, :, :], in0=first[:, :, :], scalar=-2.0, in1=g_all[:, :, :],
                                                      op0=ALU.mult, op1=ALU.add))
                    if e == 13:
                        largest(rest, second)
                    if e == NE - 2:
                        dve.wait_ge(h_high_ok, n)
                        dve.tensor_tensor(h_low[:, :], PS[:, H, :], h_high[:, :].bitcast(f32), ALU.subtract).then_inc(h_low_ok, 1)
                    if e == NE - 1:
                        step(dve.tensor_tensor(both[:, :, :], first[:, :, :], second[:, :, :], ALU.add))
                        step(dve.tensor_tensor(kept[:, :, :], both[:, :, :], g_all[:, :, :], ALU.mult))
                        step(dve.tensor_reduce(msum[:, :], kept[:, :, :], AX.X, ALU.add))
                        step(dve.tensor_scalar(msum_eps[:, :], msum[:, :], GATE_EPS, None, ALU.add))
                        dve.reciprocal(minv[:, :], msum_eps[:, :]).then_inc(inv_ok, 1)
                        dve.wait_ge(inv_ok, n)
                        dve.tensor_tensor(gate[:, bass.ds(g * GB, GB), :], kept[:, :, :], spread(minv), ALU.mult).then_inc(gate_ok, 1)
                        assert done == LINKS, done

                def experts(g, more):
                    dve.wait_ge(gate_ok, g + 1)
                    dve.wait_ge(sum_ok, g * NE + 2)
                    dve.tensor_scalar(gate_now[:, :, :], gate[:, bass.ds(g * GB, GB), :], 1.0, None, ALU.mult).then_inc(gates_here, 1)
                    dve.wait_ge(gates_here, g + 1)
                    for e in range(NE):
                        dve.wait_ge(sum_ok, g * NE + (e + 2))
                        dve.wait_ge(down_raw, g * NE + (e + 3))
                        if e < E_ROUTED:
                            for b in range(GB):
                                prior = x3_tok[:, bass.ds(g * GB + b, 1), :].rearrange("p o d -> p (o d)") if e == 0 else total[(e - 1) % 2][:, b, :]
                                ins = dve.scalar_tensor_tensor(out=total[e % 2][:, b, :], in0=PS[:, 4 + e % 2, b * D:(b + 1) * D],
                                                               scalar=gate_now[:, b, e:e + 1], in1=prior, op0=ALU.mult, op1=ALU.add)
                        else:
                            into = x3_tok[:, bass.ds(g * GB, GB), :] if e == NE - 1 else total[e % 2][:, :, :]
                            ins = dve.tensor_tensor(into, PS[:, 4 + e % 2, :].rearrange("p (b d) -> p b d", b=GB),
                                                    total[(e - 1) % 2][:, :, :], ALU.add)
                        ins.then_inc(sum_ok, 1)
                        if more:
                            inputs(g + 1, e)

                for e in range(NE):
                    inputs(0, e)
                    if e == 8:
                        dve.wait_ge(loaded, 16 * len(loads))
                        for w in range(NE):
                            dve.tensor_scalar(w1[:, w, :], w1[:, w, :], rms_wT[:, w:w + 1], None, ALU.mult).then_inc(scaled, 1)
                for q in range(4):
                    part = slice(q * QUARTER, (q + 1) * QUARTER)
                    dve.wait_ge(w1_high_ok, q + 1)
                    dve.tensor_tensor(w1_low[:, part, :], w1[:, part, :], w1_high[:, part, :].bitcast(f32), ALU.subtract).then_inc(w1_low_ok, 1)
                with dve.Fori(0, NG - 1) as g:
                    experts(g, True)
                experts(NG - 1, False)

            @block.sync
            def _(sp):
                with sp.Fori(0, NG) as g:
                    sp.wait_ge(sum_ok, g * NE + (NE + 2))
                    sp.dma_start(out[bass.ds(g * GB, GB), :, :].rearrange("b s d -> s b d"), x3_tok[:, bass.ds(g * GB, GB), :]).then_inc(stored, 16)
                sp.wait_ge(stored, 16 * NG)
        signals.clear()


def constants_phase(nc, K):
    from concourse import mybir
    from contextlib import ExitStack
    ALU = mybir.AluOpType
    with ExitStack() as ctx:
        signals = Signals(nc, ctx, "constants")
        zeroed, made = signals.take_all("zeroed made")
        with nc.Block() as block:
          @block.gpsimd
          def _(pool):
            pool.memset(K["ident"][:, :], 0.0).then_inc(zeroed, 1)
            pool.memset(K["ones_row"][:, :], 1.0).then_inc(made, 1)
            pool.wait_ge(zeroed, 1)
            pool.affine_select(out=K["ident"][:, :], in_=K["ident"][:, :], compare_op=ALU.not_equal, fill=1.0, base=0,
                               pattern=[[-1, 128]], channel_multiplier=1).then_inc(made, 1)
            pool.wait_ge(made, 2)
        signals.clear()


def build(nc, a, out):
    from concourse import mybir
    from contextlib import ExitStack
    f32 = mybir.dt.float32
    with ExitStack() as ctx:
        def sb(name, shape, dt=f32):
            return ctx.enter_context(nc.sbuf_tensor(name, shape, dt))
        K = {n: a[n] for n in ("xn_d", "bd_d", "c_d", "ad_d")}
        K |= {"PS": ctx.enter_context(nc.psum_tensor("PS", [128, 8, 512], f32)),
             "ident": sb("ident", [128, 128]), "ones_row": sb("ones_row", [1, 128]),
             "cond_tok": sb("cond_tok", [S, B, D])}
        constants_phase(nc, K)
        edge_phase(nc, a, K)
        K["x3_tok"], K["x3T"] = K["cond_tok"], sb("x3T", [D, B * S])
        attention_phase(nc, a, K)
        K["gateT"], K["xnT"] = sb("gateT", [128, NH, B * S]), sb("xnT", [128, NH, B * S])
        scan_inputs_phase(nc, a, K)
        scan_phase(nc, a, K)
        K["gate"] = sb("gate", [S, B, E_ROUTED])
        experts_phase(nc, a, K, out)


def kernel(**inputs):
    import numpy as np
    import concourse.bacc as bacc
    from concourse import mybir
    from concourse.bass_utils import run_bass_kernel_spmd

    L = {k.replace("L0_", ""): np.asarray(v) for k, v in inputs.items()}
    x = L["x"].reshape(B * S, D)
    arrays = {
        "xT": x.T, "adj": L["itok_BxSxS_0_4"], "mask": L["mask_BxS_ff1"], "qeT": L["fside_BxS_0"].T,
        "b_qtT": L["mask_BxS_ff0"][:T_ITER].T, "w_qtT": L["fside_BxSxS_0"][:T_ITER].transpose(0, 2, 1),
        "condT": L["cond_2048"].T,
        "w_qinT": L["cond_w_qin"].T, "w_plT": L["cond_w_pl"].T, "w_pcT": L["cond_w_pc"].T, "w_pkT": L["cond_w_pk"].T,
        "w_pvT": L["cond_w_pv"].T, "w_q": L["cond_w_q"], "w_k": L["cond_w_k"], "w_vT": L["cond_w_v"].T,
        "w_muT": L["cond_w_mu"].T, "w_cbT": L["cond_w_cb"].T,
        "bias": np.stack([L["cond_" + n] for n in ("b_qin", "b_pl", "b_pc", "b_q", "b_k", "b_pk", "b_pv", "b_mu")]
                         + [L["cond_init_mem"][0], L["cond_b_v"]], axis=1),
        "x": L["x"],
        "w_inT": L["cond2_W_in"].T, "taps": L["cond2_W_conv"][:, 0, :], "b_conv": L["cond2_b_conv"],
        "ln_g": L["cond2_ln_g"], "ln_b": L["cond2_ln_b"], "w_xpT": L["cond2_W_xproj"].T, "w_dtT": L["cond2_W_dt"].T,
        "state_cols": np.stack([L["cond2_b_dt"], L["cond2_A_log"]], axis=1), "D": L["cond2_D"],
        "w_outT": L["cond2_W_out"].T, "router": L["ffn_router_w"],
        "w1": np.concatenate([L["ffn_w1"], L["ffn_w1_s"]]), "w2": np.concatenate([L["ffn_w2"], L["ffn_w2_s"]]),
        "rms_wT": np.concatenate([L["ffn_rms_w"], L["ffn_rms_w_s"]]).T,
        "qkv_KT": np.concatenate([L[f"attn_{n}K"].T for n in "qkv"], axis=1),
        "qkv_V": np.stack([L[f"attn_{n}V"] for n in "qkv"]),
        "p_KT": L["attn_pK"].T, "p_V": L["attn_pV"], "f_KT": L["attn_fK"].T, "f_V": L["attn_fV"],
        "b_cb": L["cond_b_cb"],
    }
    nc = bacc.Bacc("TRN2", target_bir_lowering=False, num_devices=1)
    given, aps = {}, {}
    for name, v in arrays.items():
        v = np.ascontiguousarray(v)
        given[f"in_{name}"] = v
        aps[name] = nc.dram_tensor(f"in_{name}", v.shape, mybir.dt.from_np(v.dtype), kind="ExternalInput").ap()
    out = nc.dram_tensor("out_0", (B, S, D), mybir.dt.float32, kind="ExternalOutput").ap()
    for name, shape in (("xn_d", (B, S, DI)), ("bd_d", (B, S, N_STATE)), ("c_d", (B, N_STATE, S)), ("ad_d", (B, N_STATE, S))):
        aps[name] = nc.dram_tensor(name, shape, mybir.dt.float32, kind="Internal").ap()
    build(nc, aps, out)
    r = run_bass_kernel_spmd(nc, [given], core_ids=[0])
    return r.results[0]["out_0"]
```
